# Optimizing a Trainium2 kernel written in Bass

```python
import numpy as np
import jax
import jax.numpy as jnp

def _softmax(x, axis=-1):
    return jax.nn.softmax(x, axis=axis)

def _gelu(x):
    return jax.nn.gelu(x, approximate=True)

def _silu(x):
    return jax.nn.silu(x)

def _sigmoid(x):
    return jax.nn.sigmoid(x)

def _layernorm(x, axis=-1, eps=1e-05):
    m = jnp.mean(x, axis=axis, keepdims=True)
    v = jnp.var(x, axis=axis, keepdims=True)
    return (x - m) / jnp.sqrt(v + eps)

def _scatter_add(tgt, idx, src, axis=0):
    return tgt.at[idx].add(src)

def _segment_sum(src, seg, n):
    return jax.ops.segment_sum(src, seg, n)
kernel_name = 'mk_metaformer_d2_conv_nhwc512_r4_d45907'

def setup_inputs(seed: int=0):
    np.random.seed(seed)
    _w = jnp.asarray

    def _rec_inputs():
        import jax
        import jax.numpy as jnp
        _gk = jax.random.key(seed)
        x = -9.26e-05 + 0.9999 * jax.random.normal(jax.random.fold_in(_gk, 1), (8, 24, 24, 128), jnp.float32)
        return x
    x = _rec_inputs()

    def _L0_conv_setup():
        import jax, jax.numpy as jnp
        import numpy as np
        DIM = 128
        HID = 16
        MAX_LEN = 24
        key = jax.random.key(seed)
        ks = jax.random.split(key, 10)
        B, S = (8, 24)
        x = jax.random.normal(ks[0], (B, S, S, DIM), dtype=jnp.float32)
        s_in = 1.0 / np.sqrt(DIM)
        s_hid = 1.0 / np.sqrt(HID)
        return {'x': x, 'wq_w': jax.random.normal(ks[1], (HID, DIM), jnp.float32) * s_in, 'wq_b': jax.random.normal(ks[2], (HID,), jnp.float32) * 0.01, 'wk_w': jax.random.normal(ks[3], (HID, DIM), jnp.float32) * s_in, 'wk_b': jax.random.normal(ks[4], (HID,), jnp.float32) * 0.01, 'wv_w': jax.random.normal(ks[5], (HID, DIM), jnp.float32) * s_in, 'wv_b': jax.random.normal(ks[6], (HID,), jnp.float32) * 0.01, 'out_w': jax.random.normal(ks[7], (DIM, HID), jnp.float32) * s_hid, 'out_b': jax.random.normal(ks[8], (DIM,), jnp.float32) * 0.01, 'w_bias_table': jax.random.normal(ks[9], (MAX_LEN, MAX_LEN), jnp.float32) * 0.1}
    _L0_conv_all = _L0_conv_setup()
    _L0_conv_in = {k: v for k, v in _L0_conv_all.items() if k in ('wq_w', 'wq_b', 'wk_w', 'wk_b', 'wv_w', 'wv_b', 'out_w', 'out_b', 'w_bias_table')}
    del _L0_conv_all

    def _L0_ffn_setup():
        import jax, jax.numpy as jnp
        import numpy as np
        B, T, D = (4, 256, 128)
        E, TOP_K, H = (8, 2, 64)
        key = jax.random.key(seed)
        ks = jax.random.split(key, 8)
        s = 0.02
        return {'x': jax.random.normal(ks[0], (B, T, D), dtype=jnp.float32), 'router': jax.random.normal(ks[1], (D, E), dtype=jnp.float32) * s, 'shared_gate': jax.random.normal(ks[2], (D, H), dtype=jnp.float32) * s, 'shared_up': jax.random.normal(ks[3], (D, H), dtype=jnp.float32) * s, 'shared_down': jax.random.normal(ks[4], (H, D), dtype=jnp.float32) * s, 'W_gate': jax.random.normal(ks[5], (E, D, H), dtype=jnp.float32) * s, 'W_up': jax.random.normal(ks[6], (E, D, H), dtype=jnp.float32) * s, 'W_down': jax.random.normal(ks[7], (E, H, D), dtype=jnp.float32) * s}
    _L0_ffn_all = _L0_ffn_setup()
    _L0_ffn_in = {k: v for k, v in _L0_ffn_all.items() if k in ('router', 'shared_gate', 'shared_up', 'shared_down', 'W_gate', 'W_up', 'W_down')}
    del _L0_ffn_all

    def _L1_conv_setup():
        import jax, jax.numpy as jnp
        import numpy as np
        key = jax.random.key(seed)
        k1, k2, k3, k4, k5 = jax.random.split(key, 5)
        B, H, W, C = (4, 16, 16, 128)
        ratio = 8
        d = C // ratio
        x = jax.random.normal(k1, (B, H, W, C), dtype=jnp.float32)
        Wq = jax.random.normal(k2, (C, d), dtype=jnp.float32) * np.sqrt(2.0 / C)
        Wk = jax.random.normal(k3, (C, d), dtype=jnp.float32) * np.sqrt(2.0 / C)
        Wv = jax.random.normal(k4, (C, C), dtype=jnp.float32) * np.sqrt(2.0 / C)
        gamma = jax.random.normal(k5, (1,), dtype=jnp.float32)
        return {'x': x, 'Wq': Wq, 'Wk': Wk, 'Wv': Wv, 'gamma': gamma}
    _L1_conv_all = _L1_conv_setup()
    _L1_conv_in = {k: v for k, v in _L1_conv_all.items() if k in ('Wq', 'Wk', 'Wv', 'gamma')}
    del _L1_conv_all

    def _L1_ffn_setup():
        import jax, jax.numpy as jnp
        import numpy as np
        CAPACITY_FACTOR = 1.2
        key = jax.random.key(seed)
        k1, k2, k3 = jax.random.split(key, 3)
        B, S, D, E = (8, 1024, 128, 16)
        x = jax.random.normal(k1, (B, S, D), dtype=jnp.float32)
        switch_w = jax.random.normal(k2, (E, D), dtype=jnp.float32) * 0.02
        switch_b = jnp.zeros((E,), dtype=jnp.float32)
        expert_w = jax.random.normal(k3, (E, D, D), dtype=jnp.float32) * 0.02
        expert_b = jnp.zeros((E, D), dtype=jnp.float32)
        return {'x': x, 'switch_w': switch_w, 'switch_b': switch_b, 'expert_w': expert_w, 'expert_b': expert_b}
    _L1_ffn_all = _L1_ffn_setup()
    _L1_ffn_in = {k: v for k, v in _L1_ffn_all.items() if k in ('switch_w', 'switch_b', 'expert_w', 'expert_b')}
    del _L1_ffn_all
    return {'x': x, 'L0_conv_wq_w': _L0_conv_in['wq_w'], 'L0_conv_wq_b': _L0_conv_in['wq_b'], 'L0_conv_wk_w': _L0_conv_in['wk_w'], 'L0_conv_wk_b': _L0_conv_in['wk_b'], 'L0_conv_wv_w': _L0_conv_in['wv_w'], 'L0_conv_wv_b': _L0_conv_in['wv_b'], 'L0_conv_out_w': _L0_conv_in['out_w'], 'L0_conv_out_b': _L0_conv_in['out_b'], 'L0_conv_w_bias_table': _L0_conv_in['w_bias_table'], 'L0_ffn_router': _L0_ffn_in['router'], 'L0_ffn_shared_gate': _L0_ffn_in['shared_gate'], 'L0_ffn_shared_up': _L0_ffn_in['shared_up'], 'L0_ffn_shared_down': _L0_ffn_in['shared_down'], 'L0_ffn_W_gate': _L0_ffn_in['W_gate'], 'L0_ffn_W_up': _L0_ffn_in['W_up'], 'L0_ffn_W_down': _L0_ffn_in['W_down'], 'L1_conv_Wq': _L1_conv_in['Wq'], 'L1_conv_Wk': _L1_conv_in['Wk'], 'L1_conv_Wv': _L1_conv_in['Wv'], 'L1_conv_gamma': _L1_conv_in['gamma'], 'L1_ffn_switch_w': _L1_ffn_in['switch_w'], 'L1_ffn_switch_b': _L1_ffn_in['switch_b'], 'L1_ffn_expert_w': _L1_ffn_in['expert_w'], 'L1_ffn_expert_b': _L1_ffn_in['expert_b']}

def reference(x, L0_conv_wq_w, L0_conv_wq_b, L0_conv_wk_w, L0_conv_wk_b, L0_conv_wv_w, L0_conv_wv_b, L0_conv_out_w, L0_conv_out_b, L0_conv_w_bias_table, L0_ffn_router, L0_ffn_shared_gate, L0_ffn_shared_up, L0_ffn_shared_down, L0_ffn_W_gate, L0_ffn_W_up, L0_ffn_W_down, L1_conv_Wq, L1_conv_Wk, L1_conv_Wv, L1_conv_gamma, L1_ffn_switch_w, L1_ffn_switch_b, L1_ffn_expert_w, L1_ffn_expert_b):
    import jax
    import jax.numpy as jnp

    def _L0_conv_ref(x, wq_w, wq_b, wk_w, wk_b, wv_w, wv_b, out_w, out_b, w_bias_table):
        import jax, jax.numpy as jnp
        import numpy as np
        DIM = 128
        HID = 16
        MAX_LEN = 24
        B, H, W, C = x.shape
        q = jnp.einsum('bhwc,dc->bhwd', x, wq_w) + wq_b
        k = jnp.einsum('bhwc,dc->bhwd', x, wk_w) + wk_b
        v = jnp.einsum('bhwc,dc->bhwd', x, wv_w) + wv_b
        w_bias = w_bias_table[:H, :W]
        max_k = jnp.max(k, axis=0, keepdims=True)
        exp_k = jnp.exp(k - max_k)
        exp_w_bias = jnp.exp(w_bias)
        num = jnp.einsum('iw,bhwd->bhid', exp_w_bias, exp_k * v)
        den = jnp.einsum('iw,bhwd->bhid', exp_w_bias, exp_k)
        y = jax.nn.sigmoid(q) * num / den
        return jnp.einsum('bhwd,cd->bhwc', y, out_w) + out_b

    def _L0_ffn_ref(x, router, shared_gate, shared_up, shared_down, W_gate, W_up, W_down):
        import jax, jax.numpy as jnp
        import numpy as np
        B, T, D = (4, 256, 128)
        E, TOP_K, H = (8, 2, 64)
        b, t, d = x.shape
        n = b * t
        x_flat = x.reshape(n, d)
        shared_out = jax.nn.silu(x_flat @ shared_gate) * (x_flat @ shared_up) @ shared_down
        probs = jax.nn.softmax(x_flat @ router, axis=-1)
        topk_scores, topk_idx = jax.lax.top_k(probs, TOP_K)
        combine = jnp.zeros((n, E), dtype=x.dtype)
        combine = combine.at[jnp.arange(n)[:, None], topk_idx].set(topk_scores)
        gate = jax.nn.silu(jnp.einsum('nd,edh->enh', x_flat, W_gate))
        up = jnp.einsum('nd,edh->enh', x_flat, W_up)
        y = jnp.einsum('enh,ehd->end', gate * up, W_down)
        routed_out = jnp.einsum('ne,end->nd', combine, y)
        return (shared_out + routed_out).reshape(b, t, d)

    def _L1_conv_ref(x, Wq, Wk, Wv, gamma):
        import jax, jax.numpy as jnp
        import numpy as np
        B, H, W, C = x.shape
        N = H * W
        q = jnp.einsum('bhwc,cd->bhwd', x, Wq).reshape(B, N, -1)
        k = jnp.einsum('bhwc,cd->bhwd', x, Wk).reshape(B, N, -1)
        v = jnp.einsum('bhwc,cd->bhwd', x, Wv).reshape(B, N, C)
        energy = jnp.einsum('bid,bjd->bij', k, q)
        attn = jax.nn.softmax(energy, axis=-1)
        out = jnp.einsum('bij,bjc->bic', attn, v)
        out = out.reshape(B, H, W, C)
        return gamma * out

    def _L1_ffn_ref(x, switch_w, switch_b, expert_w, expert_b):
        import jax, jax.numpy as jnp
        import numpy as np
        CAPACITY_FACTOR = 1.2
        B, S, D = x.shape
        E = switch_w.shape[0]
        N = B * S
        xf = x.reshape(N, D)
        logits = xf @ switch_w.T + switch_b
        probs = jax.nn.softmax(logits, axis=-1)
        route_probs = jnp.max(probs, axis=-1)
        routes = jnp.argmax(probs, axis=-1)
        oh = jax.nn.one_hot(routes, E, dtype=jnp.int32)
        pos = jnp.take_along_axis(jnp.cumsum(oh, axis=0), routes[:, None], axis=1)[:, 0] - 1
        capacity = int(CAPACITY_FACTOR * N / E)
        keep = pos < capacity
        buf = jnp.zeros((E, capacity, D), dtype=xf.dtype).at[routes, pos].set(xf)
        y = jnp.einsum('ecd,efd->ecf', buf, expert_w) + expert_b[:, None, :]
        gathered = y[routes, jnp.minimum(pos, capacity - 1)]
        out = jnp.where(keep[:, None], gathered, xf) * route_probs[:, None]
        return out.reshape(B, S, D)

    def _gn(v, G=32, eps=1e-05):
        B_, H_, W_, C_ = v.shape
        g = v.reshape(B_, H_, W_, G, C_ // G)
        m = jnp.mean(g, axis=(1, 2, 4), keepdims=True)
        s = jnp.var(g, axis=(1, 2, 4), keepdims=True)
        return ((g - m) / jnp.sqrt(s + eps)).reshape(v.shape)

    def _ln_c(v, eps=1e-06):
        m = jnp.mean(v, axis=-1, keepdims=True)
        s = jnp.var(v, axis=-1, keepdims=True)
        return (v - m) / jnp.sqrt(s + eps)

    def _ln_t(v, eps=1e-05):
        m = jnp.mean(v, axis=-1, keepdims=True)
        s = jnp.var(v, axis=-1, keepdims=True)
        return (v - m) / jnp.sqrt(s + eps)

    def _to_tokens(v):
        B_, H_, W_, C_ = v.shape
        return v.reshape(B_, H_ * W_, C_)

    def _from_tokens(t, like):
        return t.reshape(like.shape)
    x = x + _L0_conv_ref(_ln_c(x), L0_conv_wq_w, L0_conv_wq_b, L0_conv_wk_w, L0_conv_wk_b, L0_conv_wv_w, L0_conv_wv_b, L0_conv_out_w, L0_conv_out_b, L0_conv_w_bias_table)
    t = _to_tokens(x)
    t = t + _L0_ffn_ref(_ln_t(t), L0_ffn_router, L0_ffn_shared_gate, L0_ffn_shared_up, L0_ffn_shared_down, L0_ffn_W_gate, L0_ffn_W_up, L0_ffn_W_down)
    x = _from_tokens(t, x)
    x = x + _L1_conv_ref(_ln_c(x), L1_conv_Wq, L1_conv_Wk, L1_conv_Wv, L1_conv_gamma)
    t = _to_tokens(x)
    t = t + _L1_ffn_ref(_ln_t(t), L1_ffn_switch_w, L1_ffn_switch_b, L1_ffn_expert_w, L1_ffn_expert_b)
    x = _from_tokens(t, x)
    return x

_drawn_inputs = setup_inputs


def setup_inputs(seed=0):
    import zlib

    import numpy as np

    out = dict(_drawn_inputs(seed))
    spreads = {'L1_ffn_switch_b': (0.0, 0.27), 'L1_ffn_expert_b': (0.0, 2.0)}
    factors = {'L0_conv_wq_b': 8.0,
     'L0_conv_wk_b': 64.0,
     'L0_conv_wv_b': 4.797,
     'L0_ffn_router': 8.0,
     'L0_ffn_shared_gate': 4.161,
     'L0_ffn_shared_up': 4.079,
     'L0_ffn_shared_down': 4.108,
     'L0_ffn_W_gate': 8.0,
     'L0_ffn_W_up': 8.0,
     'L0_ffn_W_down': 8.0,
     'L1_ffn_expert_w': 4.413}
    for name, (base, spread) in spreads.items():
        noise = np.random.default_rng([zlib.crc32(name.encode()), seed]).standard_normal(out[name].shape)
        drawn = base * np.exp(spread * noise) if base else spread * noise
        out[name] = jnp.asarray(drawn.astype(out[name].dtype))
    for name, factor in factors.items():
        out[name] = (out[name] * factor).astype(out[name].dtype)
    return out
```

```python
from contextlib import ExitStack

import concourse.bass as bass
from concourse import mybir

F32 = mybir.dt.float32
F32R = mybir.dt.float32r
BF16 = mybir.dt.bfloat16
I32 = mybir.dt.int32
ALU = mybir.AluOpType
ACT = mybir.ActivationFunctionType
AX = mybir.AxisListType

B, S, C = 8, 24, 128
SS = S * S
N = B * SS
P = 128
NT = N // P
HID = 16
G96 = 4 * S
T96 = SS // G96
E2, H2 = 8, 64
NB2 = E2 // 2 + 1
E1 = 16
CAP = int(1.2 * N / E1)
SLOTS = E1 * CAP
SR = CAP // 3
GT = 9
CH = 3 * P
HALF = SS // 2
NB_SS = -(-SS // P)
EPS_C, EPS_T = 1e-6, 1e-5
BIG = 1.0e4

K_ID, K_TRI, K_ONE, K_DIAG, K_SEL, K_SGN, K_PRI, K_EB = 0, 128, 256, 384, 480, 992, 994, 1026
K_N = K_EB + 16
K_COLS = K_N + NT


class Steps:

    def __init__(self, eng, sem):
        self.eng, self.sem, self.base, self.n = eng, sem, 0, 0

    def did(self, ins):
        ins.then_inc(self.sem, 1)
        self.n += 1

    def wait(self):
        self.eng.wait_ge(self.sem, self.base + self.n)

    def enter(self, i, per):
        self.start, self.per = self.base + self.n, per
        self.base, self.n = self.start + i * per, 0

    def leave(self, trips):
        assert self.n == self.per, (self.n, self.per)
        self.base, self.n = self.start + trips * self.per, 0


def metaformer_kernel(nc, A, out, upto=8, dbg=None):
    ctx = ExitStack()
    with ctx:
        def sb(name, shape, dt=F32):
            return ctx.enter_context(nc.sbuf_tensor(name, shape, dt))

        early, early_sems = ExitStack(), []

        def sem(name):
            if early_sems is not None and not stage5[0]:
                early_sems.append(early.enter_context(nc.semaphore(name)))
                return early_sems[-1]
            return ctx.enter_context(nc.semaphore(name))

        stage5 = [False]

        def sems(name, n=2):
            return [sem(f"{name}{j}") for j in range(n)]

        R = sb("R", [P, NT, C])
        konst = sb("konst", [P, K_COLS])
        ident = konst[:, K_ID:K_ID + P]
        ones_row = konst[0:1, K_ONE:K_ONE + P]
        xn = [sb(f"xn{p}", [P, GT, C]) for p in range(2)]
        st = [sb(f"st{p}", [P, GT, 6]) for p in range(2)]
        sm = [sb(f"sm{p}", [P, 6, GT]) for p in range(2)]
        rstd = [sb(f"rstd{p}", [P, GT]) for p in range(2)]
        xTf = [sb(f"xTf{p}", [P, CH]) for p in range(2)]
        wide0 = sb("wide0", [P, 2 * 5 * SS])
        wide1 = sb("wide1", [P, N], F32R)
        wide2 = sb("wide2", [P, N], F32R)
        neg_half = sb("neg_half", [P, GT])
        psum = [ctx.enter_context(nc.psum_tensor(f"ps{j}", [P, 1024], F32)) for j in range(4)]
        bank = [psum[j // 2][:, (j % 2) * 512:(j % 2) * 512 + 512] for j in range(8)]

        slots = nc.dram_tensor("slots", [2 * SLOTS + N, C], F32, kind="Internal").ap()

        def norm_stats(d, src, n, p, rows, eps, var_ok):
            for t in range(n):
                ins = nc.vector.bn_stats(st[p][:rows, t, :], src[:, t, :])
            d.did(ins)
            d.wait()
            s, m = st[p][:rows, 0:n, :], sm[p]
            d.did(nc.vector.tensor_tensor(m[:rows, 1, :n], s[:, :, 1], s[:, :, 4], ALU.subtract))
            d.did(nc.vector.tensor_tensor(m[:rows, 0, :n], s[:, :, 1], s[:, :, 4], ALU.add))
            d.did(nc.vector.tensor_tensor(m[:rows, 2, :n], s[:, :, 2], s[:, :, 5], ALU.add))
            d.wait()
            d.did(nc.vector.tensor_tensor(m[:rows, 3, :n], m[:rows, 1, :n], m[:rows, 1, :n], ALU.mult))
            d.did(nc.vector.tensor_scalar(m[:rows, 4, :n], m[:rows, 0, :n], 0.5, None, ALU.mult))
            d.wait()
            d.did(nc.vector.scalar_tensor_tensor(m[:rows, 3, :n], m[:rows, 3, :n], C / 4.0, m[:rows, 2, :n],
                                                 ALU.mult, ALU.add))
            d.wait()
            nc.vector.tensor_scalar(m[:rows, 5, :n], m[:rows, 3, :n], 1.0 / C, eps,
                                    ALU.mult, ALU.add).then_inc(var_ok, 1)
        NORM_STEPS = 7

        def norm_rstd(n, p, rows, rstd_ok):
            nc.gpsimd.tensor_tensor(rstd[p][:rows, :n], sm[p][:rows, 5, :n], neg_half[:rows, :n],
                                    ALU.pow).then_inc(rstd_ok, 1)

        def norm_apply(src, n, p, rows, xn_ok):
            for t in range(n):
                ins = nc.vector.tensor_scalar(xn[p][:rows, t, :], src[:, t, :], sm[p][:rows, 4, t:t + 1],
                                              rstd[p][:rows, t:t + 1], ALU.subtract, ALU.mult)
            ins.then_inc(xn_ok, 1)

        wkvq = sb("wkvq", [C, 3 * HID])
        bkvq = sb("bkvq", [1, T96 * 3 * HID])
        woT = sb("woT", [T96 * HID, T96, C])
        ob = sb("ob", [C, 1])
        tabT = sb("tabT", [G96, S])
        Wmix = sb("Wmix", [G96, G96])
        wcol = 2 * NB2 * P - P
        wstage = sb("wstage", [C, wcol + 2 * C])
        gu_w = [sb(f"gu_w{h}", [C, wcol + 2 * C], F32R) for h in range(2)]
        wd = sb("wd", [P, NB2, C])
        sel = sb("sel", [40, E2 // 2 * P], F32R)
        rt2 = sb("rt2", [C, E2])
        rt1 = sb("rt1", [C, E1])
        rb1 = sb("rb1", [P, E1])
        gam = sb("gam", [P, 1])
        ew = sb("ew", [C, E1, C])
        eb = sb("eb", [P, E1, C])
        W_QK, W_V = wcol, wcol + C

        ld = sem("ld")
        ld2 = sem("ld2")
        n_ld = [0, 0]

        local = ExitStack()
        ctx.callback(local.close)

        def lsb(name, shape, dt=F32):
            return local.enter_context(nc.sbuf_tensor(name, shape, dt))

        kvq = lsb("kvq", [G96, B, T96, 3 * HID])
        xa = [wide0[:G96, p * T96 * C:(p + 1) * T96 * C].rearrange("p (t c) -> p t c", c=C) for p in range(2)]
        xaT = [wide0[:, 1536 + p * SS:1536 + (p + 1) * SS] for p in range(2)]
        xv = A["x"].rearrange("b (t r) w c -> b (r w) t c", r=4)
        xa_in, xn_ok, xaT_ps, xaT_ok = sems("xa_in"), sems("xn_ok"), sems("xaT_ps"), sems("xaT_ok")
        var_ok, rstd_ok, kvq_ps, kvq_ok = sems("var_ok"), sems("rstd_ok"), sems("kvq_ps"), sems("kvq_ok")
        dve1, msk = sem("dve1"), sem("msk")
        woT0 = sem("woT0")
        LOADS1 = 3
        with nc.Block() as block:
            @block.sync
            def _(sp):
                sp.dma_start(konst[:], A["konst"]).then_inc(ld, 16)
                sp.dma_start(wkvq[:], A["wkvq"]).then_inc(ld, 16)
                sp.dma_start(bkvq[:], A["bkvq"]).then_inc(ld, 16)
                with sp.Fori(0, B // 2) as i:
                    for p in range(2):
                        image = sp.snap(2 * i + p)
                        sp.wait_ge(xn_ok[p], i)
                        sp.dma_start(xa[p], xv[image]).then_inc(xa_in[p], 16)
                sp.dma_start(R[:], A["x"].rearrange("b h w c -> (b h w) c").rearrange(
                    "(t p) c -> p t c", p=P)).then_inc(ld2, 16)
                for k in range(4):
                    sp.dma_start(tabT[k * S:(k + 1) * S, :], A["tabT"]).then_inc(ld2, 16)
                sp.wait_ge(woT0, 1)
                for t in range(T96):
                    sp.dma_start(woT[t * HID:(t + 1) * HID, t, :], A["woT"]).then_inc(ld2, 16)
                sp.dma_start(ob[:], A["ob"].rearrange("(c o) -> c o", o=1)).then_inc(ld2, 16)
                sp.dma_start(wstage[:], A["wstage"]).then_inc(ld2, 16)
                sp.dma_start(wd[:, 0:NB2 - 1, :], A["wd"].rearrange("(k p) c -> p k c", p=P)).then_inc(ld2, 16)
                sp.dma_start(wd[0:H2, NB2 - 1, :], A["wd_s"]).then_inc(ld2, 16)
                sp.dma_start(rt2[:], A["rt2"]).then_inc(ld2, 16)
                sp.dma_start(rt1[:], A["rt1"]).then_inc(ld2, 16)
                sp.dma_start(rb1[:], A["rb1"].rearrange("(o e) -> o e", o=1).to_broadcast([P, E1])).then_inc(ld2, 16)
                sp.dma_start(gam[:], A["gam"].rearrange("(o e) -> o e", o=1).to_broadcast([P, 1])).then_inc(ld2, 16)
                sp.dma_start(ew[:], A["ew"]).then_inc(ld2, 16)
                sp.dma_start(eb[:], A["eb"].rearrange("(o e) c -> o e c", o=1).to_broadcast([P, E1, C])).then_inc(ld2, 16)
                n_ld[1] = 1 + 4 + T96 + 10
                sp.wait_ge(ld2, 16 * n_ld[1])

            @block.gpsimd
            def _(pool):
                nc.gpsimd.memset(woT[:], 0.0).then_inc(woT0, 1)
                nc.gpsimd.memset(neg_half[:], -0.5).then_inc(msk, 1)
                pool.wait_ge(msk, 1)
                with pool.Fori(0, B // 2) as i:
                    for p in range(2):
                        pool.wait_ge(var_ok[p], i + 1)
                        norm_rstd(T96, p, G96, rstd_ok[p])

            @block.vector
            def _(dve):
                d = Steps(dve, dve1)
                with dve.Fori(0, B // 2) as i:
                    d.enter(i, 2 * NORM_STEPS)
                    for p in range(2):
                        dve.wait_ge(xa_in[p], 16 * i + 16)
                        norm_stats(d, xa[p], T96, p, G96, EPS_C, var_ok[p])
                    for p in range(2):
                        dve.wait_ge(rstd_ok[p], i + 1)
                        dve.wait_ge(xaT_ps[p], i)
                        norm_apply(xa[p], T96, p, G96, xn_ok[p])
                d.leave(B // 2)

            @block.tensor
            def _(pe):
                pe.wait_ge(ld, 16 * LOADS1)
                with pe.Fori(0, B // 2) as i:
                    for p in range(2):
                        pe.wait_ge(xn_ok[p], i + 1)
                        pe.wait_ge(xaT_ok[p], i)
                        for t in range(T96):
                            last = nc.tensor.transpose(
                                psum[p][:, (t // 3) * 512 + (t % 3) * G96:(t // 3) * 512 + (t % 3) * G96 + G96],
                                xn[p][:G96, t, :], ident[:G96, :G96])
                        last.then_inc(xaT_ps[p], 1)
                    for p in range(2):
                        pe.wait_ge(xaT_ok[p], i + 1)
                        pe.wait_ge(kvq_ok[p], i)
                        o = bank[4 + p]
                        nc.tensor.matmul(o[:G96, :T96 * 3 * HID], ones_row[:, :G96], bkvq[:], start=True, stop=False)
                        for t in range(T96):
                            last = nc.tensor.matmul(o[:G96, t * 3 * HID:(t + 1) * 3 * HID],
                                                    xaT[p][:, t * G96:(t + 1) * G96], wkvq[:],
                                                    start=False, stop=t == T96 - 1)
                        last.then_inc(kvq_ps[p], 1)

            @block.scalar
            def _(act):
                with act.Fori(0, B // 2) as i:
                    for p in range(2):
                        act.wait_ge(xaT_ps[p], i + 1)
                        act.wait_ge(kvq_ps[p], i)
                        nc.scalar.activation(xaT[p].rearrange("c (h n) -> c h n", h=2),
                                             psum[p][:].rearrange("c (h n) -> c h n", h=2)[:, :, :HALF],
                                             ACT.Copy).then_inc(xaT_ok[p], 1)
                    for p in range(2):
                        act.wait_ge(kvq_ps[p], i + 1)
                        nc.scalar.activation(
                            kvq[:, 2 * i + p], bank[4 + p][:G96, :T96 * 3 * HID].rearrange("p (t d) -> p t d", t=T96),
                            ACT.Copy).then_inc(kvq_ok[p], 1)
        if upto == 1:
            dbg(nc, ctx, kvq[:].rearrange("p b t d -> p (b t d)"))
            return

        TD = T96 * HID
        kx = lsb("kx", [G96, T96, HID])
        ek = lsb("ek", [G96, B, TD])
        ekv = lsb("ekv", [G96, B, TD])
        eq = lsb("eq", [G96, B, TD])
        mt = lsb("mt", [TD, 4, CH])
        y = [lsb(f"y{p}", [TD, CH]) for p in range(2)]
        oT = wide0[:, :N]
        kmax, ksub, eks, ekvs, eqs, tab, wmix = (sem(n) for n in "kmax ksub eks ekvs eqs tab wmix".split())
        mix_ps, qTs, y_ok, oT_ps, oT_ok, tok_ps, tok_ok = (
            sem(n) for n in "mix_ps qTs y_ok oT_ps oT_ok tok_ps tok_ok".split())
        dve2 = sem("dve2")
        kv4 = kvq[:].rearrange("p b t (x d) -> p b t x d", x=3)
        split_h, split_l = sem("split_h"), sem("split_l")
        with nc.Block() as block:
            @block.vector
            def _(dve):
                d = Steps(dve, dve2)
                d.did(nc.vector.tensor_reduce(kx[:], kv4[:, :, :, 0, :].rearrange("p b t d -> p t d b"), AX.X, ALU.max))
                d.wait()
                for b in range(B):
                    ins = nc.vector.tensor_tensor(ek[:, b].rearrange("p (t d) -> p t d", t=T96), kv4[:, b, :, 0, :],
                                                  kx[:], ALU.subtract)
                ins.then_inc(ksub, 1)
                dve.wait_ge(tab, 1)
                nc.vector.tensor_tensor(Wmix[:].rearrange("p (k i) -> p k i", k=4),
                                        konst[:G96, K_DIAG:K_DIAG + G96].rearrange("p (k i) -> p k i", k=4),
                                        tabT[:].unsqueeze(1).to_broadcast([G96, 4, S]), ALU.mult).then_inc(wmix, 1)
                dve.wait_ge(eks, 1)
                for b in range(B):
                    ins = nc.vector.tensor_tensor(ekv[:, b].rearrange("p (t d) -> p t d", t=T96),
                                                  ek[:, b].rearrange("p (t d) -> p t d", t=T96),
                                                  kv4[:, b, :, 1, :], ALU.mult)
                ins.then_inc(ekvs, 1)
                dve.wait_ge(eqs, 1)
                d.did(nc.vector.tensor_scalar(eq[:], eq[:], 1.0, None, ALU.add))
                for h in range(2):
                    m = mt[:, 2 * h:2 * h + 2]
                    dve.wait_ge(qTs, h + 1)
                    d.did(nc.vector.tensor_tensor(m[:, 1], bank[3 * h][:TD, :CH], m[:, 0], ALU.mult))
                    d.wait()
                    d.did(nc.vector.reciprocal(m[:, 0], m[:, 1]))
                    d.wait()
                    nc.vector.tensor_tensor(y[h][:], bank[3 * h + 1][:TD, :CH], m[:, 0], ALU.mult).then_inc(y_ok, 1)
                dve.wait_ge(split_h, 1)
                nc.vector.tensor_tensor(gu_w[1][:], wstage[:], gu_w[0][:].bitcast(F32), ALU.subtract).then_inc(split_l, 1)
                with dve.Fori(0, NT // 3) as i:
                    dve.wait_ge(tok_ps, i + 1)
                    nc.vector.tensor_tensor(R[:, bass.ds(3 * i, 3), :], R[:, bass.ds(3 * i, 3), :],
                                            bank[6][:, :CH].rearrange("p (t c) -> p t c", c=C),
                                            ALU.add).then_inc(tok_ok, 1)

            @block.scalar
            def _(act):
                nc.scalar.activation(tabT[:], tabT[:], ACT.Exp).then_inc(tab, 1)
                for b in range(B):
                    ins = nc.scalar.activation(eq[:, b].rearrange("p (t d) -> p t d", t=T96), kv4[:, b, :, 2, :],
                                               ACT.Exp, scale=-1.0)
                ins.then_inc(eqs, 1)
                act.wait_ge(ksub, 1)
                nc.scalar.activation(ek[:], ek[:], ACT.Exp).then_inc(eks, 1)
                for h in range(2):
                    act.wait_ge(mix_ps, h + 1)
                    nc.scalar.activation(mt[:, 2 * h], bank[3 * h + 2][:TD, :CH], ACT.Copy).then_inc(qTs, 1)
                nc.scalar.activation(gu_w[0][:], wstage[:], ACT.Copy).then_inc(split_h, 1)
                for h in range(2):
                    for t in range(T96):
                        n = h * T96 + t
                        act.wait_ge(oT_ps, n + 1)
                        nc.scalar.activation(
                            oT.rearrange("c (b t n) -> c b t n", b=B, t=T96)[:, 4 * h:4 * h + 4, t, :],
                            bank[6 + n % 2][:, :CH].rearrange("c (b n) -> c b n", b=4),
                            ACT.Identity, bias=ob[:]).then_inc(oT_ok, 1)

            @block.tensor
            def _(pe):
                pe.wait_ge(ekvs, 1)
                pe.wait_ge(wmix, 1)
                pe.wait_ge(dve2, 2)
                for h in range(2):
                    for b in range(4):
                        at = slice(b * G96, (b + 1) * G96)
                        nc.tensor.matmul(bank[3 * h][:TD, at], ek[:, 4 * h + b], Wmix[:], start=True, stop=True)
                        nc.tensor.matmul(bank[3 * h + 1][:TD, at], ekv[:, 4 * h + b], Wmix[:], start=True, stop=True)
                        last = nc.tensor.transpose(bank[3 * h + 2][:TD, at], eq[:, 4 * h + b], ident[:G96, :G96])
                    last.then_inc(mix_ps, 1)
                for h in range(2):
                    pe.wait_ge(y_ok, h + 1)
                    for t in range(T96):
                        n = h * T96 + t
                        if n >= 2:
                            pe.wait_ge(oT_ok, n - 1)
                        nc.tensor.matmul(bank[6 + n % 2][:, :CH], woT[:, t, :], y[h][:], start=True,
                                         stop=True).then_inc(oT_ps, 1)
                pe.wait_ge(oT_ok, 2 * T96)
                for i in range(NT // 3):
                    if i >= 1:
                        pe.wait_ge(tok_ok, i)
                    for t in range(3):
                        last = nc.tensor.transpose(bank[6][:, t * P:(t + 1) * P],
                                                   oT[:, (3 * i + t) * P:(3 * i + t + 1) * P], ident)
                    last.then_inc(tok_ps, 1)
        if upto == 2:
            dbg(nc, ctx, R[:].rearrange("p t c -> p (t c)"))
            return
        local.close()

        def group(i, p):
            return bass.ds(2 * GT * i + GT * p, GT)

        def chunk_use(i, p, j):
            u = 3 * p + j
            return u % 2, 3 * i + u // 2

        lg2 = sb("lg2", [P, NT, E2])
        local = ExitStack()
        ctx.callback(local.close)
        xTH, xTL = wide1, wide2
        var3, rs3, xn3, tr3, xt3, xl3, lm3, lg3 = (
            sems(n) for n in "var3 rs3 xn3 tr3 xt3 xl3 lm3 lg3".split())
        dve3, dve3b, ex3, spl3, cps3, csb3, cdr3, cT3, cz3, sl3 = (
            sem(n) for n in "dve3 dve3b ex3 spl3 cps3 csb3 cdr3 cT3 cz3 sl3".split())
        cT = lsb("cT", [40, N], F32R)
        with nc.Block() as block:
            @block.gpsimd
            def _(pool):
                nc.gpsimd.memset(cT[:].bitcast(F32), 0.0).then_inc(cz3, 1)
                with pool.Fori(0, 2) as i:
                    for p in range(2):
                        pool.wait_ge(var3[p], i + 1)
                        norm_rstd(GT, p, P, rs3[p])

            @block.vector
            def _(dve):
                d = Steps(dve, dve3)
                with dve.Fori(0, 2) as i:
                    d.enter(i, 2 * NORM_STEPS)
                    for p in range(2):
                        norm_stats(d, R[:, group(i, p), :], GT, p, P, EPS_T, var3[p])
                    for p in range(2):
                        dve.wait_ge(rs3[p], i + 1)
                        dve.wait_ge(tr3[0], 3 * i)
                        dve.wait_ge(tr3[1], 3 * i)
                        norm_apply(R[:, group(i, p), :], GT, p, P, xn3[p])
                        for j in range(3):
                            q, n = chunk_use(i, p, j)
                            dve.wait_ge(xt3[q], n + 1)
                            at = bass.ds(CH * (6 * i + 3 * p + j), CH)
                            nc.vector.tensor_tensor(xTL[:, at], bank[q][:, :CH], xTH[:, at].bitcast(F32),
                                                    ALU.subtract).then_inc(xl3[q], 1)
                        dve.wait_ge(lm3[q], n + 1)
                        nc.vector.tensor_copy(lg2[:, group(i, p), :],
                                              bank[2 + p][:, :GT * E2].rearrange("p (t e) -> p t e", e=E2)
                                              ).then_inc(lg3[p], 1)
                d.leave(2)

            @block.scalar
            def _(act):
                with act.Fori(0, 2) as i:
                    for p in range(2):
                        for j in range(3):
                            q, n = chunk_use(i, p, j)
                            act.wait_ge(tr3[q], n + 1)
                            act.wait_ge(lm3[q], n)
                            nc.scalar.activation(xTf[q][:], bank[q][:, :CH], ACT.Copy)
                            nc.scalar.activation(xTH[:, bass.ds(CH * (6 * i + 3 * p + j), CH)], bank[q][:, :CH],
                                                 ACT.Copy).then_inc(xt3[q], 1)

            @block.tensor
            def _(pe):
                def logits(i, p, j):
                    q, n = chunk_use(i, p, j)
                    pe.wait_ge(xt3[q], n + 1)
                    for t in range(3):
                        k = 3 * j + t
                        last = nc.tensor.matmul(bank[2 + p][:, k * E2:(k + 1) * E2], xTf[q][:, t * P:(t + 1) * P],
                                                rt2[:], start=True, stop=True)
                    last.then_inc(lm3[q], 1)

                with pe.Fori(0, 2) as i:
                    for p in range(2):
                        pe.wait_ge(xn3[p], i + 1)
                        pe.wait_ge(lg3[p], i)
                        for j in range(3):
                            q, n = chunk_use(i, p, j)
                            pe.wait_ge(xl3[q], n)
                            for t in range(3):
                                last = nc.tensor.transpose(bank[q][:, t * P:(t + 1) * P], xn[p][:, 3 * j + t, :], ident)
                            last.then_inc(tr3[q], 1)
                            if j:
                                logits(i, p, j - 1)
                        logits(i, p, 2)

        d8 = lsb("d8", [P, NT, E2])
        ex8 = lsb("ex8", [P, NT, E2])
        w8 = [lsb(f"w8_{k}", [P, NT, E2]) for k in range(3)]
        col = [lsb(f"col{k}", [P, NT]) for k in range(4)]
        cH = lsb("cH", [P, 2, NT * E2])
        cHr = lsb("cHr", [P, NT * E2], F32R)
        cS = lsb("cS", [P, 2, 3, P])
        cdram = nc.dram_tensor("cdram", [2, NT * E2, P], F32, kind="Internal").ap()
        CR = [P, P, NT * E2 - 2 * P]
        with nc.Block() as block:
            @block.vector
            def _(dve):
                d = Steps(dve, dve3b)

                def wide(c):
                    return c[:].unsqueeze(2).to_broadcast([P, NT, E2])

                pri = konst[:, K_PRI:K_PRI + E2].unsqueeze(1).to_broadcast([P, NT, E2])

                def first_max(v, oh, tmp, m):
                    d.did(nc.vector.tensor_reduce(m[:], v[:], AX.X, ALU.max))
                    d.wait()
                    d.did(nc.vector.tensor_tensor(tmp[:], v[:], wide(m), ALU.is_equal))
                    d.wait()
                    d.did(nc.vector.tensor_tensor(tmp[:], tmp[:], pri, ALU.mult))
                    d.wait()
                    d.did(nc.vector.tensor_reduce(m[:], tmp[:], AX.X, ALU.max))
                    d.wait()
                    d.did(nc.vector.tensor_tensor(oh[:], tmp[:], wide(m), ALU.is_equal))
                    d.wait()

                d.did(nc.vector.tensor_reduce(col[0][:], lg2[:], AX.X, ALU.max))
                d.wait()
                nc.vector.tensor_tensor(d8[:], lg2[:], wide(col[0]), ALU.subtract).then_inc(sl3, 1)
                dve.wait_ge(sl3, 1)
                first_max(d8, w8[0], w8[2], col[1])
                d.did(nc.vector.scalar_tensor_tensor(lg2[:], w8[0][:], -1.0e30, d8[:], ALU.mult, ALU.add))
                d.wait()
                first_max(lg2, w8[1], w8[2], col[2])
                d.did(nc.vector.tensor_tensor(w8[0][:], w8[0][:], w8[1][:], ALU.add))
                dve.wait_ge(ex3, 1)
                d.did(nc.vector.tensor_reduce(col[0][:], ex8[:], AX.X, ALU.add))
                d.wait()
                d.did(nc.vector.reciprocal(col[3][:], col[0][:]))
                d.did(nc.vector.tensor_tensor(w8[1][:], w8[0][:], ex8[:], ALU.mult))
                d.wait()
                d.did(nc.vector.tensor_tensor(w8[2][:], w8[1][:], wide(col[3]), ALU.mult))
                d.wait()
                d.did(nc.vector.tensor_copy(cHr[:], w8[2][:].rearrange("p t e -> p (t e)")))
                d.wait()
                d.did(nc.vector.tensor_copy(cH[:, 0], cHr[:].bitcast(F32)))
                d.did(nc.vector.tensor_tensor(cH[:, 1], w8[2][:].rearrange("p t e -> p (t e)"), cHr[:].bitcast(F32),
                                              ALU.subtract))
                d.wait()
                nc.vector.tensor_copy(sel[:], konst[:40, K_SEL:K_SEL + E2 * H2]).then_inc(spl3, 1)

            @block.scalar
            def _(act):
                act.wait_ge(sl3, 1)
                nc.scalar.activation(ex8[:], d8[:], ACT.Exp).then_inc(ex3, 1)
                act.wait_ge(cps3, 1)
                for h in range(2):
                    for k in range(3):
                        ins = nc.scalar.activation(cS[:CR[k], h, k, :], bank[h][:CR[k], k * P:(k + 1) * P], ACT.Copy)
                ins.then_inc(csb3, 1)

            @block.tensor
            def _(pe):
                pe.wait_ge(spl3, 1)
                for h in range(2):
                    for k in range(3):
                        last = nc.tensor.transpose(bank[h][:CR[k], k * P:(k + 1) * P],
                                                   cH[:, h, k * P:k * P + CR[k]], ident)
                last.then_inc(cps3, 1)

            @block.sync
            def _(sp):
                sp.wait_ge(csb3, 1)
                for h in range(2):
                    for k in range(3):
                        sp.dma_start(cdram[h, k * P:k * P + CR[k], :], cS[:CR[k], h, k, :]).then_inc(cdr3, 16)
                sp.wait_ge(cdr3, 16 * 6)
                for h in range(2):
                    sp.dma_start(cT[32 * h:32 * h + E2, :].bitcast(F32).rearrange("e (t n) -> e t n", t=NT),
                                 cdram[h].rearrange("(t e) n -> e t n", e=E2)).then_inc(cT3, 16)
                sp.wait_ge(cT3, 32)
        if upto == 3:
            dbg(nc, ctx, cT[:].bitcast(F32), xTH[:].bitcast(F32), xTL[:].bitcast(F32))
            return

        s4 = [lsb(f"s4_{q}", [P, CH]) for q in range(2)]
        t4 = [lsb(f"t4_{q}", [P, CH]) for q in range(2)]
        h4 = [lsb(f"h4_{q}", [P, CH]) for q in range(2)]
        y4 = [lsb(f"y4_{p}", [P, CH]) for p in range(2)]
        g_ps, u_ps, s_ok, h_ok, dn, yS, zt = (sems(n) for n in "g_ps u_ps s_ok h_ok dn yS zt".split())
        cb_ps, t_ok, R_ok = sem("cb_ps"), sem("t_ok"), sem("R_ok")
        TRIPS = N // CH // 2
        UB = 2 * NB2
        UPS = NB2 - 1

        def use(i, u):
            return u % 2, NB2 * i + u // 2

        def rows(k):
            return P if k < NB2 - 1 else H2

        with nc.Block() as block:
            @block.tensor
            def _(pe):
                def tokens(i, u):
                    return bass.ds(CH * (2 * i + u // NB2), CH)

                def gate_up(i, u):
                    q, n = use(i, u)
                    k = u % NB2
                    for which, done in ((0, g_ps), (1, u_ps)):
                        if k == NB2 - 1 and which == 1:
                            break
                        if which == 0:
                            pe.wait_ge(s_ok[q], n)
                        pe.wait_ge(h_ok[q], n)
                        o = bank[2 * which + q][:, :CH]
                        w = slice((2 * k + which) * P, (2 * k + which + 1) * P)
                        at = tokens(i, u)
                        nc.tensor.matmul(o, gu_w[0][:, w], xTH[:, at], start=True, stop=False)
                        nc.tensor.matmul(o, gu_w[0][:, w], xTL[:, at], start=False, stop=False)
                        nc.tensor.matmul(o, gu_w[1][:, w], xTH[:, at], start=False, stop=True).then_inc(done[q], 1)

                def spread(i, u):
                    k = u % NB2
                    if k < NB2 - 1:
                        nc.tensor.matmul(bank[4][:, :CH], sel[:, k * P:(k + 1) * P], cT[:, tokens(i, u)],
                                         start=True, stop=True).then_inc(cb_ps, 1)

                def down(i, u):
                    q, n = use(i, u)
                    k, p = u % NB2, u // NB2
                    if k == 0:
                        pe.wait_ge(yS[p], i)
                    pe.wait_ge(h_ok[q], n + 1)
                    nc.tensor.matmul(bank[5 + p][:, :CH], wd[:rows(k), k, :], h4[q][:rows(k), :],
                                     start=k == 0, stop=k == NB2 - 1).then_inc(dn[q], 1)

                def back(i, p):
                    pe.wait_ge(yS[p], i + 1)
                    if p == 0:
                        pe.wait_ge(R_ok, 2 * i)
                    else:
                        pe.wait_ge(R_ok, 2 * i + 1)
                    for t in range(3):
                        last = nc.tensor.transpose(bank[7][:, t * P:(t + 1) * P], y4[p][:, t * P:(t + 1) * P], ident)
                    last.then_inc(zt[p], 1)

                def trip(i, final):
                    for u in range(UB):
                        if u + 1 < UB:
                            gate_up(i, u + 1)
                        elif not final:
                            gate_up(i + 1, 0)
                        down(i, u)
                        if u + 1 < UB:
                            spread(i, u + 1)
                        elif not final:
                            spread(i + 1, 0)
                        if u == NB2 + 1:
                            back(i, 0)
                    back(i, 1)

                gate_up(0, 0)
                spread(0, 0)
                with pe.Fori(0, TRIPS - 1) as i:
                    trip(i, False)
                trip(TRIPS - 1, True)

            @block.scalar
            def _(act):
                def silu(i, u):
                    q, n = use(i, u)
                    r = rows(u % NB2)
                    act.wait_ge(g_ps[q], n + 1)
                    act.wait_ge(h_ok[q], n)
                    nc.scalar.activation(s4[q][:r], bank[q][:r, :CH], ACT.Silu).then_inc(s_ok[q], 1)

                def trip(i, final):
                    for u in range(UB):
                        if u + 1 < UB:
                            silu(i, u + 1)
                        elif not final:
                            silu(i + 1, 0)
                        if u % NB2 == NB2 - 1:
                            p = u // NB2
                            q, n = use(i, u)
                            act.wait_ge(dn[q], n + 1)
                            act.wait_ge(zt[p], i)
                            nc.scalar.activation(y4[p][:], bank[5 + p][:, :CH], ACT.Copy).then_inc(yS[p], 1)

                silu(0, 0)
                with act.Fori(0, TRIPS - 1) as i:
                    trip(i, False)
                trip(TRIPS - 1, True)

            @block.vector
            def _(dve):
                d = Steps(dve, t_ok)

                def residual(i, p):
                    dve.wait_ge(zt[p], i + 1)
                    at = bass.ds(6 * i + 3 * p, 3)
                    nc.vector.tensor_tensor(R[:, at, :], R[:, at, :], bank[7][:, :CH].rearrange("p (t c) -> p t c", c=C),
                                            ALU.add).then_inc(R_ok, 1)

                with dve.Fori(0, TRIPS) as i:
                    d.enter(i, 2 * (NB2 - 1))
                    for u in range(UB):
                        q, n = use(i, u)
                        k = u % NB2
                        r = rows(k)
                        dve.wait_ge(s_ok[q], n + 1)
                        if k < NB2 - 1:
                            dve.wait_ge(u_ps[q], UPS * i + sum(v % 2 == q and v % NB2 < NB2 - 1 for v in range(u + 1)))
                            d.did(nc.vector.tensor_tensor(t4[q][:], bank[2 + q][:, :CH], s4[q][:], ALU.mult))
                            d.wait()
                            dve.wait_ge(cb_ps, (NB2 - 1) * 2 * i + (NB2 - 1) * (u // NB2) + k + 1)
                            dve.wait_ge(dn[q], n)
                            nc.vector.tensor_tensor(h4[q][:], bank[4][:, :CH], t4[q][:], ALU.mult).then_inc(h_ok[q], 1)
                        else:
                            dve.wait_ge(dn[q], n)
                            nc.vector.tensor_tensor(h4[q][:r], bank[q][r:2 * r, :CH], s4[q][:r],
                                                    ALU.mult).then_inc(h_ok[q], 1)
                        if u == NB2 + 1:
                            residual(i, 0)
                    residual(i, 1)
                d.leave(TRIPS)
        local.close()
        if upto == 4:
            dbg(nc, ctx, R[:].rearrange("p t c -> p (t c)"))
            return

        stage5[0] = True
        GN = GT * P
        JB = [(k * P, min(P, SS - k * P)) for k in range(NB_SS)]
        hT = [wide1[:, p * GN:(p + 1) * GN] for p in range(2)]
        lT = [wide2[:, p * GN:(p + 1) * GN] for p in range(2)]
        PT = [wide0[:, p * NB_SS * SS:(p + 1) * NB_SS * SS].rearrange("j (k i) -> j k i", k=NB_SS) for p in range(2)]
        local = ExitStack()
        ctx.callback(local.close)
        V = [lsb(f"V{p}", [P, NB_SS, C + 1]) for p in range(2)]
        sH = [lsb(f"sH{p}", [P, SS], F32R) for p in range(2)]
        sQK = [lsb(f"sQK{p}", [P, SS], F32R) for p in range(2)]
        Q = [lsb(f"Q{p}", [97, SS], F32R) for p in range(2)]
        K = [lsb(f"K{p}", [97, NB_SS * P], F32R) for p in range(2)]
        mx = [lsb(f"mx{p}", [P, NB_SS]) for p in range(2)]
        rs = [lsb(f"rs{p}", [P, NB_SS]) for p in range(2)]
        var5, rs5, xn5, tr5, xt5, xl5, e_ps, e_ok, sh5, st5, qk_in, mx_ok, mT, mH, mL, v_ok, pt_ok, pv, o_ok = (
            sems(n) for n in ("var5 rs5 xn5 tr5 xt5 xl5 e_ps e_ok sh5 st5 qk_in mx_ok mT mH mL v_ok pt_ok pv "
                              "o_ok").split())
        dve5, qk0, rr5 = sem("dve5"), sem("qk0"), sem("rr5")
        EU = 2 + 2 * NB_SS
        M_ROWS = 97

        def e_tile(g, bp, w):
            return w % 2, EU * g + EU // 2 * bp + w // 2

        def halves(ap, rows=P):
            return ap[:rows].rearrange("r (h n) -> r h n", h=2)[:, :, :HALF]

        def i_blocks(bp):
            if bp == 0:
                return [(k * P, n, k, 0) for k, (_, n) in enumerate(JB)]
            return [(0, P // 2, NB_SS - 1, P // 2)] + [(P // 2 + k * P, P, NB_SS + k, 0) for k in range(NB_SS - 1)]

        with nc.Block() as block:
            @block.gpsimd
            def _(pool):
                with pool.Fori(0, 2) as i:
                    for p in range(2):
                        pool.wait_ge(var5[p], i + 1)
                        norm_rstd(GT, p, P, rs5[p])

            @block.sync
            def _(sp):
                for done in early_sems:
                    sp.sem_clear(done)
                with sp.Fori(0, B // 2) as g:
                    for bp in range(2):
                        sp.wait_ge(st5[bp], g + 1)
                        sp.dma_start(Q[bp][0:64, :].bitcast(F32), sQK[bp][0:64, :].bitcast(F32)).then_inc(qk_in[bp], 16)
                        sp.dma_start(K[bp][0:64, :SS].bitcast(F32), sQK[bp][64:128, :].bitcast(F32)).then_inc(qk_in[bp], 16)

            @block.vector
            def _(dve):
                d = Steps(dve, dve5)
                r = Steps(dve, rr5)
                for p in range(2):
                    nc.vector.memset(V[p][:, :, C:C + 1], 1.0).then_inc(qk0, 1)
                    nc.vector.memset(K[p][:].bitcast(F32), 0.0).then_inc(qk0, 1)
                    nc.vector.memset(Q[p][64:97, :].bitcast(F32), 0.0).then_inc(qk0, 1)
                dve.wait_ge(qk0, 6)
                for p in range(2):
                    nc.vector.memset(Q[p][64:65, :].bitcast(F32), -1.0).then_inc(qk0, 1)
                    nc.vector.memset(Q[p][96:97, :].bitcast(F32), -1.0).then_inc(qk0, 1)
                with dve.Fori(0, 2) as i:
                    d.enter(i, 2 * NORM_STEPS)
                    r.enter(i, 4 * NB_SS)
                    for p in range(2):
                        norm_stats(d, R[:, group(i, p), :], GT, p, P, EPS_C, var5[p])
                    for p in range(2):
                        dve.wait_ge(rs5[p], i + 1)
                        dve.wait_ge(tr5[0], 3 * i)
                        dve.wait_ge(tr5[1], 3 * i)
                        norm_apply(R[:, group(i, p), :], GT, p, P, xn5[p])
                        for j in range(3):
                            q, n = chunk_use(i, p, j)
                            dve.wait_ge(xt5[q], n + 1)
                            at = slice(j * CH, (j + 1) * CH)
                            nc.vector.tensor_tensor(lT[p][:, at], bank[4 + q][:, :CH], hT[p][:, at].bitcast(F32),
                                                    ALU.subtract).then_inc(xl5[q], 1)
                        g = 2 * i + p
                        for bp in range(2):
                            e, n = e_tile(g, bp, 0)
                            dve.wait_ge(sh5[bp], g + 1)
                            dve.wait_ge(qk_in[bp], 32 * g)
                            nc.vector.scalar_tensor_tensor(
                                sQK[bp][:].rearrange("r (h n) -> r h n", h=2), halves(psum[e]),
                                konst[:, K_SGN + 1:K_SGN + 2],
                                sH[bp][:].bitcast(F32).rearrange("r (h n) -> r h n", h=2),
                                ALU.mult, ALU.subtract).then_inc(st5[bp], 1)
                            for k, (_, m) in enumerate(JB):
                                e, n = e_tile(g, bp, 2 + k)
                                dve.wait_ge(e_ps[e], n + 1)
                                if k == 0:
                                    dve.wait_ge(mT[bp], g)
                                nc.vector.tensor_reduce(mx[bp][:m, k:k + 1], halves(psum[e], m), AX.XY,
                                                        ALU.max).then_inc(mx_ok[bp], 1)
                            dve.wait_ge(mH[bp], g + 1)
                            nc.vector.tensor_tensor(K[bp][96:97, :SS], psum[2][0:1, :SS], K[bp][64:65, :SS].bitcast(F32),
                                                    ALU.subtract).then_inc(mL[bp], 1)
                            for k, (_, m, tile, lo) in enumerate(i_blocks(bp)):
                                dve.wait_ge(pv[bp], NB_SS * g + (3 if k < 3 else NB_SS))
                                o = bank[6 + k // 3][lo:lo + m, k % 3 * (C + 1):(k % 3 + 1) * (C + 1)]
                                r.did(nc.vector.reciprocal(rs[bp][lo:lo + m, k:k + 1], o[:, C:C + 1]))
                                r.wait()
                                at = R[lo:lo + m, bass.ds(2 * GT * i + GT * p + tile, 1), :].rearrange("p t c -> p (t c)")
                                nc.vector.scalar_tensor_tensor(at, o[:, :C], rs[bp][lo:lo + m, k:k + 1], at,
                                                               ALU.mult, ALU.add).then_inc(o_ok[bp], 1)
                r.leave(2)
                d.leave(2)

            @block.scalar
            def _(act):
                act.wait_ge(qk0, 10)
                with act.Fori(0, 2) as i:
                    for p in range(2):
                        for j in range(3):
                            q, n = chunk_use(i, p, j)
                            act.wait_ge(tr5[q], n + 1)
                            act.wait_ge(pv[1], NB_SS * 2 * i)
                            nc.scalar.activation(hT[p][:, j * CH:(j + 1) * CH], bank[4 + q][:, :CH],
                                                 ACT.Copy).then_inc(xt5[q], 1)
                        g = 2 * i + p
                        for bp in range(2):
                            e, n = e_tile(g, bp, 0)
                            act.wait_ge(e_ps[e], n + 1)
                            act.wait_ge(st5[bp], g)
                            nc.scalar.activation(sH[bp][:].rearrange("r (h n) -> r h n", h=2), halves(psum[e]),
                                                 ACT.Copy, scale=konst[:, K_SGN:K_SGN + 1]).then_inc(sh5[bp], 1)
                            e, n = e_tile(g, bp, 1)
                            act.wait_ge(e_ps[e], n + 1)
                            act.wait_ge(pv[bp], NB_SS * g)
                            for k, (_, m) in enumerate(JB):
                                at = k // 4 * 512 + k % 4 * C
                                ins = nc.scalar.activation(V[bp][:m, k, :C], psum[e][:m, at:at + C], ACT.Copy,
                                                           scale=gam[:m])
                            ins.then_inc(v_ok[bp], 1)
                            act.wait_ge(mT[bp], g + 1)
                            nc.scalar.activation(K[bp][64:65, :SS], psum[2][0:1, :SS], ACT.Copy).then_inc(mH[bp], 1)
                            for k, (_, m) in enumerate(JB):
                                e, n = e_tile(g, bp, 2 + NB_SS + k)
                                act.wait_ge(e_ps[e], n + 1)
                                nc.scalar.activation(PT[bp][:m, k, :].rearrange("j (h n) -> j h n", h=2),
                                                     halves(psum[e], m), ACT.Exp).then_inc(pt_ok[bp], 1)

            @block.tensor
            def _(pe):
                pe.wait_ge(qk0, 10)

                def e_free(g, bp, w):
                    e, n = e_tile(g, bp, w)
                    if w == 0:
                        (pe.wait_ge(pt_ok[1 - bp], NB_SS * g + (NB_SS if bp else 0)))
                    elif w == 1:
                        pass
                    elif w == 2:
                        pe.wait_ge(st5[bp], g + 1)
                    elif w == 3:
                        pe.wait_ge(v_ok[bp], g + 1)
                    elif w < 4 + NB_SS:
                        pe.wait_ge(mx_ok[bp], NB_SS * g + w - 3)
                    else:
                        pe.wait_ge(pt_ok[bp], NB_SS * g + w - 3 - NB_SS)
                    return e

                with pe.Fori(0, 2) as i:
                    for p in range(2):
                        pe.wait_ge(xn5[p], i + 1)
                        g = 2 * i + p
                        for j in range(3):
                            q, n = chunk_use(i, p, j)
                            pe.wait_ge(xl5[q], n)
                            pe.wait_ge(mL[1], g)
                            for t in range(3):
                                last = nc.tensor.transpose(bank[4 + q][:, t * P:(t + 1) * P], xn[p][:, 3 * j + t, :],
                                                           ident)
                            last.then_inc(tr5[q], 1)
                        for bp in range(2):
                            if bp == 0:
                                for j in (1, 2):
                                    q, n = chunk_use(i, p, j)
                                    pe.wait_ge(xl5[q], n + 1)
                            e = e_free(g, bp, 0)
                            for h in range(2):
                                o = psum[e][:, h * 512:h * 512 + HALF]
                                at = slice(bp * SS + h * HALF, bp * SS + (h + 1) * HALF)
                                w = slice(W_QK, W_QK + C)
                                nc.tensor.matmul(o, gu_w[0][:, w], hT[p][:, at], start=True, stop=False)
                                nc.tensor.matmul(o, gu_w[0][:, w], lT[p][:, at], start=False, stop=False)
                                last = nc.tensor.matmul(o, gu_w[1][:, w], hT[p][:, at], start=False, stop=True)
                            last.then_inc(e_ps[e], 1)
                            e = e_free(g, bp, 1)
                            for k, (j0, m) in enumerate(JB):
                                o = psum[e][:m, k // 4 * 512 + k % 4 * C:k // 4 * 512 + k % 4 * C + C]
                                at = slice(bp * SS + j0, bp * SS + j0 + m)
                                w = slice(W_V, W_V + C)
                                nc.tensor.matmul(o, hT[p][:, at], gu_w[0][:, w], start=True, stop=False)
                                nc.tensor.matmul(o, lT[p][:, at], gu_w[0][:, w], start=False, stop=False)
                                last = nc.tensor.matmul(o, hT[p][:, at], gu_w[1][:, w], start=False, stop=True)
                            last.then_inc(e_ps[e], 1)
                            pe.wait_ge(qk_in[bp], 32 * (g + 1))
                            for k, (i0, m) in enumerate(JB):
                                e = e_free(g, bp, 2 + k)
                                for h in range(2):
                                    last = nc.tensor.matmul(psum[e][:, h * 512:h * 512 + HALF], K[bp][:64, i0:i0 + P],
                                                            Q[bp][:64, h * HALF:(h + 1) * HALF], start=True, stop=True)
                                last.then_inc(e_ps[e], 1)
                            pe.wait_ge(mx_ok[bp], NB_SS * (g + 1))
                            if bp == 0:
                                pe.wait_ge(mL[1], g)
                            else:
                                pe.wait_ge(mL[0], g + 1)
                            for k, (i0, m) in enumerate(JB):
                                last = nc.tensor.transpose(psum[2][0:1, i0:i0 + m], mx[bp][:m, k:k + 1], ident[:m, :m])
                            last.then_inc(mT[bp], 1)
                            pe.wait_ge(mL[bp], g + 1)
                            for k, (j0, m) in enumerate(JB):
                                e = e_free(g, bp, 2 + NB_SS + k)
                                for h in range(2):
                                    last = nc.tensor.matmul(psum[e][:m, h * 512:h * 512 + HALF], Q[bp][:, j0:j0 + m],
                                                            K[bp][:, h * HALF:(h + 1) * HALF], start=True, stop=True)
                                last.then_inc(e_ps[e], 1)
                            pe.wait_ge(pt_ok[bp], NB_SS * (g + 1))
                            for k, (i0, m, _, lo) in enumerate(i_blocks(bp)):
                                if k == 0:
                                    if bp == 0:
                                        pe.wait_ge(o_ok[1], NB_SS * g)
                                    else:
                                        pe.wait_ge(o_ok[0], NB_SS * (g + 1))
                                for jk, (_, mj) in enumerate(JB):
                                    last = nc.tensor.matmul(
                                        bank[6 + k // 3][lo:lo + m, k % 3 * (C + 1):(k % 3 + 1) * (C + 1)],
                                        PT[bp][:mj, jk, i0:i0 + m], V[bp][:mj, jk, :],
                                        start=jk == 0, stop=jk == NB_SS - 1)
                                last.then_inc(pv[bp], 1)
        local.close()
        if upto == 5:
            dbg(nc, ctx, R[:].rearrange("p t c -> p (t c)"))
            return

        early.close()
        gidx = sb("gidx", [P, NT], I32)
        prob = sb("prob", [P, NT])
        local = ExitStack()
        ctx.callback(local.close)
        zrow = lsb("zrow", [P, 12, C])
        ZFILLS = SLOTS // (SR * 12) + NT // 12
        tri = lsb("tri", [P, P], BF16)
        ones = lsb("ones", [P, P], BF16)
        oh = [lsb(f"oh{p}", [P, GT, E1], BF16) for p in range(2)]
        lg = [lsb(f"lg{p}", [P, GT, E1]) for p in range(2)]
        lx = [lsb(f"lx{p}", [P, GT, E1]) for p in range(2)]
        w1 = [lsb(f"w1_{p}", [P, GT, E1]) for p in range(2)]
        cm = [lsb(f"cm{p}", [P, 8, GT]) for p in range(2)]
        sidx = [lsb(f"sidx{p}", [P, GT], I32) for p in range(2)]
        carry = lsb("carry", [P, 2, E1])
        var6, rs6, xn6, tr6, xt6, lm6, d6, ex6, oh6, cnt6, cr6, sx6, sc6 = (
            sems(n) for n in "var6 rs6 xn6 tr6 xt6 lm6 d6 ex6 oh6 cnt6 cr6 sx6 sc6".split())
        dve6, r6, k6, z6, zf6 = sem("dve6"), sem("r6"), sem("k6"), sem("z6"), sem("zf6")
        ROUTE_STEPS = 18

        def per_expert(c):
            return c.unsqueeze(2).to_broadcast([P, GT, E1])

        with nc.Block() as block:
            @block.sync
            def _(sp):
                sp.wait_ge(z6, 1)
                for k in range(SLOTS // (SR * 12)):
                    sp.dma_start(slots[k * SR * 12:(k + 1) * SR * 12, :].rearrange("(p t) c -> p t c", t=12),
                                 zrow[:SR]).then_inc(zf6, 16)
                for k in range(NT // 12):
                    sp.dma_start(slots[SLOTS + k * P * 12:SLOTS + (k + 1) * P * 12, :].rearrange("(p t) c -> p t c", t=12),
                                 zrow[:]).then_inc(zf6, 16)
                sp.wait_ge(zf6, 16 * ZFILLS)

            @block.gpsimd
            def _(pool):
                nc.gpsimd.memset(zrow[:], 0.0).then_inc(z6, 1)
                for i in range(2):
                    for p in range(2):
                        pool.wait_ge(var6[p], i + 1)
                        norm_rstd(GT, p, P, rs6[p])
                    for p in range(2):
                        pool.wait_ge(sx6[p], i + 1)
                        pool.wait_ge(zf6, 16 * ZFILLS)
                        for t in range(GT):
                            nc.gpsimd.indirect_dma_start(
                                slots, bass.IndirectOffsetOnAxis(sidx[p][:, t:t + 1], 0),
                                xn[p][:, t, :], None).then_inc(sc6[p], 16)
                for p in range(2):
                    pool.wait_ge(sc6[p], 16 * GT * 2)

            @block.vector
            def _(dve):
                d = Steps(dve, dve6)
                r = Steps(dve, r6)
                nc.vector.tensor_copy(tri[:], konst[:, K_TRI:K_TRI + P]).then_inc(k6, 1)
                nc.vector.tensor_copy(ones[:], konst[:, K_ONE:K_ONE + P]).then_inc(k6, 1)
                nc.vector.memset(carry[:], 0.0).then_inc(k6, 1)
                dve.wait_ge(k6, 3)
                with dve.Fori(0, 2) as i:
                    d.enter(i, 2 * NORM_STEPS)
                    r.enter(i, 2 * ROUTE_STEPS)
                    for p in range(2):
                        norm_stats(d, R[:, group(i, p), :], GT, p, P, EPS_T, var6[p])
                    for p in range(2):
                        dve.wait_ge(rs6[p], i + 1)
                        dve.wait_ge(sc6[p], 16 * GT * i)
                        norm_apply(R[:, group(i, p), :], GT, p, P, xn6[p])
                    for p in range(2):
                        c = cm[p]
                        q, n = chunk_use(i, p, 2)
                        dve.wait_ge(lm6[q], n + 1)
                        r.did(nc.vector.tensor_tensor(lg[p][:], bank[2 + p][:, :GT * E1].rearrange("p (t e) -> p t e", e=E1),
                                                      rb1[:].unsqueeze(1).to_broadcast([P, GT, E1]), ALU.add))
                        r.wait()
                        r.did(nc.vector.tensor_reduce(c[:, 0], lg[p][:], AX.X, ALU.max))
                        r.wait()
                        nc.vector.tensor_tensor(lx[p][:], lg[p][:], per_expert(c[:, 0]), ALU.subtract).then_inc(d6[p], 1)
                        r.did(nc.vector.tensor_tensor(w1[p][:], lg[p][:], per_expert(c[:, 0]), ALU.is_equal))
                        r.wait()
                        r.did(nc.vector.tensor_tensor(w1[p][:], w1[p][:],
                                                      konst[:, K_PRI + 16:K_PRI + 32].unsqueeze(1).to_broadcast([P, GT, E1]),
                                                      ALU.mult))
                        r.wait()
                        r.did(nc.vector.tensor_reduce(c[:, 1], w1[p][:], AX.X, ALU.max))
                        r.wait()
                        nc.vector.tensor_tensor(oh[p][:], w1[p][:], per_expert(c[:, 1]), ALU.is_equal).then_inc(oh6[p], 1)
                        dve.wait_ge(oh6[p], i + 1)
                        r.did(nc.vector.tensor_tensor(w1[p][:], oh[p][:],
                                                      konst[:, K_EB:K_EB + E1].unsqueeze(1).to_broadcast([P, GT, E1]),
                                                      ALU.mult))
                        r.wait()
                        r.did(nc.vector.tensor_reduce(c[:, 2], w1[p][:], AX.X, ALU.add))
                        dve.wait_ge(ex6[p], i + 1)
                        r.did(nc.vector.tensor_reduce(c[:, 3], lx[p][:], AX.X, ALU.add))
                        r.wait()
                        r.did(nc.vector.reciprocal(prob[:, group(i, p)], c[:, 3]))
                        dve.wait_ge(cnt6[p], i + 1)
                        r.did(nc.vector.tensor_tensor(lg[p][:], bank[4 + p][:, :GT * E1].rearrange("p (t e) -> p t e", e=E1),
                                                      carry[:, p].unsqueeze(1).to_broadcast([P, GT, E1]), ALU.add))
                        nc.vector.tensor_tensor(carry[:, 1 - p], bank[4 + p][:, GT * E1:(GT + 1) * E1], carry[:, p],
                                                ALU.add).then_inc(cr6[p], 1)
                        r.wait()
                        r.did(nc.vector.tensor_tensor(w1[p][:], lg[p][:], oh[p][:], ALU.mult))
                        r.wait()
                        r.did(nc.vector.tensor_reduce(c[:, 4], w1[p][:], AX.X, ALU.add))
                        r.wait()
                        r.did(nc.vector.tensor_scalar(c[:, 5], c[:, 4], float(CAP), None, ALU.is_le))
                        r.did(nc.vector.scalar_tensor_tensor(c[:, 6], c[:, 4], -1.0, c[:, 2], ALU.add, ALU.add))
                        r.wait()
                        trash = konst[:, K_N:K_N + NT][:, group(i, p)]
                        r.did(nc.vector.tensor_tensor(c[:, 6], c[:, 6], trash, ALU.subtract))
                        r.wait()
                        r.did(nc.vector.tensor_tensor(c[:, 6], c[:, 6], c[:, 5], ALU.mult))
                        r.wait()
                        r.did(nc.vector.tensor_tensor(c[:, 6], c[:, 6], trash, ALU.add))
                        r.wait()
                        r.did(nc.vector.scalar_tensor_tensor(gidx[:, group(i, p)], c[:, 5], float(SLOTS + N), c[:, 6],
                                                             ALU.mult, ALU.add))
                        nc.vector.tensor_copy(sidx[p][:], c[:, 6]).then_inc(sx6[p], 1)
                        if p == 0:
                            dve.wait_ge(cr6[0], i + 1)
                        else:
                            dve.wait_ge(cr6[1], i + 1)
                d.leave(2)
                r.leave(2)

            @block.scalar
            def _(act):
                with act.Fori(0, 2) as i:
                    for p in range(2):
                        for j in range(3):
                            q, n = chunk_use(i, p, j)
                            act.wait_ge(tr6[q], n + 1)
                            act.wait_ge(lm6[q], n)
                            nc.scalar.activation(xTf[q][:], bank[q][:, :CH], ACT.Copy).then_inc(xt6[q], 1)
                    for p in range(2):
                        act.wait_ge(d6[p], i + 1)
                        nc.scalar.activation(lx[p][:], lx[p][:], ACT.Exp).then_inc(ex6[p], 1)

            @block.tensor
            def _(pe):
                def logits(i, p, j):
                    q, n = chunk_use(i, p, j)
                    pe.wait_ge(xt6[q], n + 1)
                    for t in range(3):
                        k = 3 * j + t
                        last = nc.tensor.matmul(bank[2 + p][:, k * E1:(k + 1) * E1], xTf[q][:, t * P:(t + 1) * P],
                                                rt1[:], start=True, stop=True)
                    last.then_inc(lm6[q], 1)

                pe.wait_ge(k6, 3)
                with pe.Fori(0, 2) as i:
                    for p in range(2):
                        pe.wait_ge(xn6[p], i + 1)
                        pe.wait_ge(oh6[p], i)
                        for j in range(3):
                            q, n = chunk_use(i, p, j)
                            pe.wait_ge(xt6[q], n)
                            for t in range(3):
                                last = nc.tensor.transpose(bank[q][:, t * P:(t + 1) * P], xn[p][:, 3 * j + t, :], ident)
                            last.then_inc(tr6[q], 1)
                            if j:
                                logits(i, p, j - 1)
                        logits(i, p, 2)
                    for p in range(2):
                        pe.wait_ge(oh6[p], i + 1)
                        pe.wait_ge(cr6[p], i)
                        o = bank[4 + p]
                        nc.tensor.matmul(o[:, :GT * E1], tri[:], oh[p][:].rearrange("p t e -> p (t e)"),
                                         start=True, stop=False, skip_group_check=True)
                        for t in range(GT):
                            later = GT - t
                            last = nc.tensor.matmul(
                                o[:, (t + 1) * E1:(GT + 1) * E1].rearrange("p (k e) -> p k e", e=E1), ones[:],
                                oh[p][:, t:t + 1, :].to_broadcast([P, later, E1]),
                                start=False, stop=t == GT - 1, skip_group_check=True)
                        last.then_inc(cnt6[p], 1)
        local.close()
        if upto == 6:
            dbg(nc, ctx, gidx[:], prob[:])
            return

        local = ExitStack()
        ctx.callback(local.close)
        NBUF = 4
        xe = [lsb(f"xe{k}", [SR, 3, C]) for k in range(NBUF)]
        xeT = [lsb(f"xeT{k}", [C, CAP]) for k in range(NBUF)]
        ye = [lsb(f"ye{k}", [SR, 3, C]) for k in range(NBUF)]
        in7, tr7, xt7, ym7, ye7, st7 = (sems(n, NBUF) for n in "in7 tr7 xt7 ym7 ye7 st7".split())
        rows_in = slots[0:SLOTS, :].rearrange("(e p t) c -> e p t c", e=E1, t=3)
        rows_out = slots[SLOTS + N:, :].rearrange("(e p t) c -> e p t c", e=E1, t=3)
        with nc.Block() as block:
            @block.sync
            def _(sp):
                with sp.Fori(0, E1 // NBUF) as i:
                    for k in range(NBUF):
                        expert = sp.snap(NBUF * i + k)
                        sp.wait_ge(tr7[k], i)
                        sp.dma_start(xe[k][:], rows_in[expert]).then_inc(in7[k], 16)

            @block.tensor
            def _(pe):
                with pe.Fori(0, E1 // NBUF) as i:
                    for k in range(NBUF):
                        pe.wait_ge(in7[k], 16 * i + 16)
                        pe.wait_ge(xt7[k], i)
                        for t in range(3):
                            last = nc.tensor.transpose(bank[k][:, t * SR:(t + 1) * SR], xe[k][:, t, :], ident[:SR, :SR])
                        last.then_inc(tr7[k], 1)
                    for k in range(NBUF):
                        pe.wait_ge(xt7[k], i + 1)
                        pe.wait_ge(ye7[k], i)
                        for t in range(3):
                            last = nc.tensor.matmul(bank[4 + k][:SR, t * C:(t + 1) * C], xeT[k][:, t * SR:(t + 1) * SR],
                                                    ew[:, bass.ds(NBUF * i + k, 1), :], start=True, stop=True)
                        last.then_inc(ym7[k], 1)

            @block.scalar
            def _(act):
                with act.Fori(0, E1 // NBUF) as i:
                    for k in range(NBUF):
                        act.wait_ge(tr7[k], i + 1)
                        act.wait_ge(ym7[k], i)
                        nc.scalar.activation(xeT[k][:], bank[k][:, :CAP], ACT.Copy).then_inc(xt7[k], 1)
                    for k in range(NBUF):
                        act.wait_ge(ye7[k], i + 1)
                        act.dma_start(rows_out[NBUF * i + k], ye[k][:]).then_inc(st7[k], 16)
                for k in range(NBUF):
                    act.wait_ge(st7[k], 16 * (E1 // NBUF))

            @block.vector
            def _(dve):
                with dve.Fori(0, E1 // NBUF) as i:
                    for k in range(NBUF):
                        dve.wait_ge(ym7[k], i + 1)
                        dve.wait_ge(st7[k], 16 * i)
                        nc.vector.tensor_tensor(ye[k][:], bank[4 + k][:SR, :CH].rearrange("p (t c) -> p t c", c=C),
                                                eb[:SR, bass.ds(NBUF * i + k, 1), :].to_broadcast([SR, 3, C]),
                                                ALU.add).then_inc(ye7[k], 1)
        local.close()
        if upto == 7:
            dbg(nc, ctx, gidx[:])
            return

        gi = [sb(f"gi{p}", [P, GT], I32) for p in range(2)]
        gi8, ga8, r8, o8 = (sems(n) for n in "gi8 ga8 r8 o8".split())
        out_t = out.rearrange("b h w c -> (b h w) c").rearrange("(t p) c -> p t c", p=P)
        with nc.Block() as block:
            @block.gpsimd
            def _(pool):
                for i in range(2):
                    for p in range(2):
                        pool.wait_ge(gi8[p], i + 1)
                        if i:
                            pool.wait_ge(r8[p], GT * i)
                        for t in range(GT):
                            nc.gpsimd.indirect_dma_start(
                                xn[p][:, t, :], None, slots,
                                bass.IndirectOffsetOnAxis(gi[p][:, t:t + 1], 0)).then_inc(ga8[p], 16)

            @block.vector
            def _(dve):
                with dve.Fori(0, 2) as i:
                    for p in range(2):
                        dve.wait_ge(ga8[p], 16 * GT * i)
                        nc.vector.tensor_copy(gi[p][:], gidx[:, group(i, p)]).then_inc(gi8[p], 1)
                    for p in range(2):
                        dve.wait_ge(ga8[p], 16 * GT * (i + 1))
                        for t in range(GT):
                            tile = bass.ds(2 * GT * i + GT * p + t, 1)
                            at = R[:, tile, :].rearrange("p t c -> p (t c)")
                            nc.vector.scalar_tensor_tensor(at, xn[p][:, t, :], prob[:, tile], at, ALU.mult,
                                                           ALU.add).then_inc(r8[p], 1)

            @block.sync
            def _(sp):
                for i in range(2):
                    for p in range(2):
                        tiles = slice(2 * GT * i + GT * p, 2 * GT * i + GT * p + GT)
                        sp.wait_ge(r8[p], GT * (i + 1))
                        sp.dma_start(out_t[:, tiles, :], R[:, tiles, :]).then_inc(o8[p], 16)
                for p in range(2):
                    sp.wait_ge(o8[p], 32)


def constants():
    import numpy as np

    k = np.zeros((P, K_COLS), np.float32)
    row = np.arange(P)
    k[:, K_ID:K_ID + P] = np.eye(P)
    k[:, K_TRI:K_TRI + P] = row[:, None] <= row[None, :]
    k[:, K_ONE:K_ONE + P] = 1
    k[:G96, K_DIAG:K_DIAG + G96] = row[:G96, None] // S == row[None, :G96] // S
    for e in range(E2):
        k[e, K_SEL + e * H2:K_SEL + (e + 1) * H2] = 1
        k[32 + e, K_SEL + e * H2:K_SEL + (e + 1) * H2] = 1
    high = np.where(row < 64, row < 32, row % 32 < 16)
    k[:, K_SGN] = np.where(high, -1, 1)
    k[:, K_SGN + 1] = np.where(high, 0, 1)
    k[:, K_PRI:K_PRI + E2] = E2 - np.arange(E2)
    k[:, K_PRI + 16:K_PRI + 32] = E1 - np.arange(E1)
    k[:, K_EB:K_EB + E1] = np.arange(E1) * CAP
    k[:, K_N:K_N + NT] = SLOTS + np.arange(NT)[None, :] * P + row[:, None]
    return k


def lay_out(inputs):
    import numpy as np

    g = {n: np.asarray(a) for n, a in inputs.items()}
    pairs = [np.transpose(g[f"L0_ffn_W_{n}"], (1, 0, 2)).reshape(C, E2 // 2, 2 * H2) for n in ("gate", "up")]
    experts = np.stack(pairs, 2).reshape(C, 2 * E2 * H2)
    qk = [np.tile(g["L1_conv_Wq"], (1, 4)), np.tile(g["L1_conv_Wk"], (1, 4))]
    return {
        "x": g["x"],
        "konst": constants(),
        "wkvq": np.concatenate([g[f"L0_conv_w{n}_w"].T for n in "kvq"], 1),
        "bkvq": np.tile(np.concatenate([g[f"L0_conv_w{n}_b"] for n in "kvq"]), T96)[None],
        "woT": g["L0_conv_out_w"].T,
        "ob": g["L0_conv_out_b"],
        "tabT": g["L0_conv_w_bias_table"][:S, :S].T,
        "wstage": np.concatenate([experts, g["L0_ffn_shared_gate"], g["L0_ffn_shared_up"], *qk, g["L1_conv_Wv"]], 1),
        "wd": g["L0_ffn_W_down"].reshape(E2 * H2, C),
        "wd_s": g["L0_ffn_shared_down"],
        "rt2": g["L0_ffn_router"],
        "rt1": g["L1_ffn_switch_w"].T,
        "rb1": g["L1_ffn_switch_b"],
        "gam": g["L1_conv_gamma"],
        "ew": np.transpose(g["L1_ffn_expert_w"], (2, 0, 1)),
        "eb": g["L1_ffn_expert_b"],
    }


def kernel(**inputs):
    import numpy as np
    import concourse.bacc as bacc
    from concourse.bass_utils import run_bass_kernel_spmd

    nc = bacc.Bacc("TRN2", target_bir_lowering=False, num_devices=1)
    arrays = {f"in_{n}": np.ascontiguousarray(a) for n, a in lay_out(inputs).items()}
    A = {n[3:]: nc.dram_tensor(n, a.shape, mybir.dt.from_np(a.dtype), kind="ExternalInput").ap()
         for n, a in arrays.items()}
    out = nc.dram_tensor("out", (B, S, S, C), F32, kind="ExternalOutput").ap()
    metaformer_kernel(nc, A, out)
    r = run_bass_kernel_spmd(nc, [arrays], core_ids=[0])
    return r.results[0]["out"]
```

```python
from contextlib import ExitStack

import concourse.bass as bass
from concourse import mybir

F32 = mybir.dt.float32
F32R = mybir.dt.float32r
BF16 = mybir.dt.bfloat16
I32 = mybir.dt.int32
ALU = mybir.AluOpType
ACT = mybir.ActivationFunctionType
AX = mybir.AxisListType

B, S, C = 8, 24, 128
SS = S * S
N = B * SS
P = 128
NT = N // P
HID = 16
G96 = 4 * S
T96 = SS // G96
E2, H2 = 8, 64
NB2 = E2 // 2 + 1
E1 = 16
CAP = int(1.2 * N / E1)
SLOTS = E1 * CAP
SR = CAP // 3
GT = 9
CH = 3 * P
HALF = SS // 2
NB_SS = -(-SS // P)
EPS_C, EPS_T = 1e-6, 1e-5
BIG = 1.0e4

K_ID, K_TRI, K_ONE, K_DIAG, K_SEL, K_SGN, K_PRI, K_EB = 0, 128, 256, 384, 480, 992, 994, 1026
K_N = K_EB + 16
K_COLS = K_N + NT


class Steps:

    def __init__(self, eng, sem):
        self.eng, self.sem, self.base, self.n = eng, sem, 0, 0

    def did(self, ins):
        ins.then_inc(self.sem, 1)
        self.n += 1

    def wait(self):
        self.eng.wait_ge(self.sem, self.base + self.n)

    def enter(self, i, per):
        self.start, self.per = self.base + self.n, per
        self.base, self.n = self.start + i * per, 0

    def leave(self, trips):
        assert self.n == self.per, (self.n, self.per)
        self.base, self.n = self.start + trips * self.per, 0


def metaformer_kernel(nc, A, out, upto=8, dbg=None):
    ctx = ExitStack()
    with ctx:
        def sb(name, shape, dt=F32):
            return ctx.enter_context(nc.sbuf_tensor(name, shape, dt))

        early, early_sems = ExitStack(), []

        def sem(name):
            if early_sems is not None and not stage5[0]:
                early_sems.append(early.enter_context(nc.semaphore(name)))
                return early_sems[-1]
            return ctx.enter_context(nc.semaphore(name))

        stage5 = [False]

        def sems(name, n=2):
            return [sem(f"{name}{j}") for j in range(n)]

        R = sb("R", [P, NT, C])
        konst = sb("konst", [P, K_COLS])
        ident = konst[:, K_ID:K_ID + P]
        ones_row = konst[0:1, K_ONE:K_ONE + P]
        xn = [sb(f"xn{p}", [P, GT, C]) for p in range(2)]
        st = [sb(f"st{p}", [P, GT, 6]) for p in range(2)]
        sm = [sb(f"sm{p}", [P, 6, GT]) for p in range(2)]
        rstd = [sb(f"rstd{p}", [P, GT]) for p in range(2)]
        xTf = [sb(f"xTf{p}", [P, CH]) for p in range(2)]
        wide0 = sb("wide0", [P, 2 * 5 * SS])
        wide1 = sb("wide1", [P, N], F32R)
        wide2 = sb("wide2", [P, N], F32R)
        neg_half = sb("neg_half", [P, GT])
        psum = [ctx.enter_context(nc.psum_tensor(f"ps{j}", [P, 1024], F32)) for j in range(4)]
        bank = [psum[j // 2][:, (j % 2) * 512:(j % 2) * 512 + 512] for j in range(8)]

        slots = nc.dram_tensor("slots", [2 * SLOTS + N, C], F32, kind="Internal").ap()

        def norm_stats(d, src, n, p, rows, eps, var_ok):
            for t in range(n):
                ins = nc.vector.bn_stats(st[p][:rows, t, :], src[:, t, :])
            norm_moments(d, ins, n, p, rows, eps, var_ok)

        def norm_moments(d, ins, n, p, rows, eps, var_ok, mean=0.5):
            d.did(ins)
            d.wait()
            s, m = st[p][:rows, 0:n, :], sm[p]
            d.did(nc.vector.tensor_tensor(m[:rows, 1, :n], s[:, :, 1], s[:, :, 4], ALU.subtract))
            d.did(nc.vector.tensor_tensor(m[:rows, 0, :n], s[:, :, 1], s[:, :, 4], ALU.add))
            d.did(nc.vector.tensor_tensor(m[:rows, 2, :n], s[:, :, 2], s[:, :, 5], ALU.add))
            d.wait()
            d.did(nc.vector.tensor_tensor(m[:rows, 3, :n], m[:rows, 1, :n], m[:rows, 1, :n], ALU.mult))
            d.did(nc.vector.tensor_scalar(m[:rows, 4, :n], m[:rows, 0, :n], mean, None, ALU.mult))
            d.wait()
            d.did(nc.vector.scalar_tensor_tensor(m[:rows, 3, :n], m[:rows, 3, :n], C / 4.0, m[:rows, 2, :n],
                                                 ALU.mult, ALU.add))
            d.wait()
            nc.vector.tensor_scalar(m[:rows, 5, :n], m[:rows, 3, :n], 1.0 / C, eps,
                                    ALU.mult, ALU.add).then_inc(var_ok, 1)
        NORM_STEPS = 7

        def norm_rstd(n, p, rows, rstd_ok):
            nc.gpsimd.tensor_tensor(rstd[p][:rows, :n], sm[p][:rows, 5, :n], neg_half[:rows, :n],
                                    ALU.pow).then_inc(rstd_ok, 1)

        def norm_apply(src, n, p, rows, xn_ok):
            for t in range(n):
                ins = nc.vector.tensor_scalar(xn[p][:rows, t, :], src[:, t, :], sm[p][:rows, 4, t:t + 1],
                                              rstd[p][:rows, t:t + 1], ALU.subtract, ALU.mult)
            ins.then_inc(xn_ok, 1)

        wkvq = sb("wkvq", [C, 3 * HID])
        bkvq = sb("bkvq", [1, T96 * 3 * HID])
        woT = sb("woT", [T96 * HID, T96, C])
        ob = sb("ob", [C, 1])
        tabT = sb("tabT", [G96, S])
        Wmix = sb("Wmix", [G96, G96])
        wcol = 2 * NB2 * P - P
        wstage = sb("wstage", [C, wcol + 2 * C])
        gu_w = [sb(f"gu_w{h}", [C, wcol + 2 * C], F32R) for h in range(2)]
        wd = sb("wd", [P, NB2, C])
        sel = sb("sel", [40, E2 // 2 * P], F32R)
        rt2 = sb("rt2", [C, E2])
        rt1 = sb("rt1", [C, E1])
        rb1 = sb("rb1", [P, E1])
        gam = sb("gam", [P, 1])
        ew = sb("ew", [C, E1, C])
        eb = sb("eb", [P, E1, C])
        W_QK, W_V = wcol, wcol + C

        ld = sem("ld")
        ld2 = sem("ld2")
        n_ld = [0, 0]

        local = ExitStack()
        ctx.callback(local.close)

        def lsb(name, shape, dt=F32):
            return local.enter_context(nc.sbuf_tensor(name, shape, dt))

        kvq = lsb("kvq", [G96, B, T96, 3 * HID])
        xa = [wide0[:G96, p * T96 * C:(p + 1) * T96 * C].rearrange("p (t c) -> p t c", c=C) for p in range(2)]
        xaT = [wide0[:, 1536 + p * SS:1536 + (p + 1) * SS] for p in range(2)]
        xv = A["x"].rearrange("b (t r) w c -> b (r w) t c", r=4)
        xa_in, xn_ok, xaT_ps, xaT_ok = sems("xa_in"), sems("xn_ok"), sems("xaT_ps"), sems("xaT_ok")
        var_ok, rstd_ok, kvq_ps, kvq_ok = sems("var_ok"), sems("rstd_ok"), sems("kvq_ps"), sems("kvq_ok")
        dve1, msk = sem("dve1"), sem("msk")
        woT0 = sem("woT0")
        LOADS1 = 3
        with nc.Block() as block:
            @block.sync
            def _(sp):
                sp.dma_start(konst[:], A["konst"]).then_inc(ld, 16)
                sp.dma_start(wkvq[:], A["wkvq"]).then_inc(ld, 16)
                sp.dma_start(bkvq[:], A["bkvq"]).then_inc(ld, 16)
                with sp.Fori(0, B // 2) as i:
                    for p in range(2):
                        image = sp.snap(2 * i + p)
                        sp.wait_ge(xn_ok[p], i)
                        sp.dma_start(xa[p], xv[image]).then_inc(xa_in[p], 16)
                sp.dma_start(R[:], A["x"].rearrange("b h w c -> (b h w) c").rearrange(
                    "(t p) c -> p t c", p=P)).then_inc(ld2, 16)
                for k in range(4):
                    sp.dma_start(tabT[k * S:(k + 1) * S, :], A["tabT"]).then_inc(ld2, 16)
                sp.wait_ge(woT0, 1)
                for t in range(T96):
                    sp.dma_start(woT[t * HID:(t + 1) * HID, t, :], A["woT"]).then_inc(ld2, 16)
                sp.dma_start(ob[:], A["ob"].rearrange("(c o) -> c o", o=1)).then_inc(ld2, 16)
                sp.dma_start(wstage[:], A["wstage"]).then_inc(ld2, 16)
                sp.dma_start(wd[:, 0:NB2 - 1, :], A["wd"].rearrange("(k p) c -> p k c", p=P)).then_inc(ld2, 16)
                sp.dma_start(wd[0:H2, NB2 - 1, :], A["wd_s"]).then_inc(ld2, 16)
                sp.dma_start(rt2[:], A["rt2"]).then_inc(ld2, 16)
                sp.dma_start(rt1[:], A["rt1"]).then_inc(ld2, 16)
                sp.dma_start(rb1[:], A["rb1"].rearrange("(o e) -> o e", o=1).to_broadcast([P, E1])).then_inc(ld2, 16)
                sp.dma_start(gam[:], A["gam"].rearrange("(o e) -> o e", o=1).to_broadcast([P, 1])).then_inc(ld2, 16)
                sp.dma_start(ew[:], A["ew"]).then_inc(ld2, 16)
                sp.dma_start(eb[:], A["eb"].rearrange("(o e) c -> o e c", o=1).to_broadcast([P, E1, C])).then_inc(ld2, 16)
                n_ld[1] = 1 + 4 + T96 + 10
                sp.wait_ge(ld2, 16 * n_ld[1])

            @block.gpsimd
            def _(pool):
                nc.gpsimd.memset(woT[:], 0.0).then_inc(woT0, 1)
                nc.gpsimd.memset(neg_half[:], -0.5).then_inc(msk, 1)
                pool.wait_ge(msk, 1)
                with pool.Fori(0, B // 2) as i:
                    for p in range(2):
                        pool.wait_ge(var_ok[p], i + 1)
                        norm_rstd(T96, p, G96, rstd_ok[p])

            @block.vector
            def _(dve):
                d = Steps(dve, dve1)
                with dve.Fori(0, B // 2) as i:
                    d.enter(i, 2 * NORM_STEPS)
                    for p in range(2):
                        dve.wait_ge(xa_in[p], 16 * i + 16)
                        norm_stats(d, xa[p], T96, p, G96, EPS_C, var_ok[p])
                    for p in range(2):
                        dve.wait_ge(rstd_ok[p], i + 1)
                        dve.wait_ge(xaT_ps[p], i)
                        norm_apply(xa[p], T96, p, G96, xn_ok[p])
                d.leave(B // 2)

            @block.tensor
            def _(pe):
                pe.wait_ge(ld, 16 * LOADS1)
                with pe.Fori(0, B // 2) as i:
                    for p in range(2):
                        pe.wait_ge(xn_ok[p], i + 1)
                        pe.wait_ge(xaT_ok[p], i)
                        for t in range(T96):
                            last = nc.tensor.transpose(
                                psum[p][:, (t // 3) * 512 + (t % 3) * G96:(t // 3) * 512 + (t % 3) * G96 + G96],
                                xn[p][:G96, t, :], ident[:G96, :G96])
                        last.then_inc(xaT_ps[p], 1)
                    for p in range(2):
                        pe.wait_ge(xaT_ok[p], i + 1)
                        pe.wait_ge(kvq_ok[p], i)
                        o = bank[4 + p]
                        nc.tensor.matmul(o[:G96, :T96 * 3 * HID], ones_row[:, :G96], bkvq[:], start=True, stop=False)
                        for t in range(T96):
                            last = nc.tensor.matmul(o[:G96, t * 3 * HID:(t + 1) * 3 * HID],
                                                    xaT[p][:, t * G96:(t + 1) * G96], wkvq[:],
                                                    start=False, stop=t == T96 - 1)
                        last.then_inc(kvq_ps[p], 1)

            @block.scalar
            def _(act):
                with act.Fori(0, B // 2) as i:
                    for p in range(2):
                        act.wait_ge(xaT_ps[p], i + 1)
                        act.wait_ge(kvq_ps[p], i)
                        nc.scalar.activation(xaT[p].rearrange("c (h n) -> c h n", h=2),
                                             psum[p][:].rearrange("c (h n) -> c h n", h=2)[:, :, :HALF],
                                             ACT.Copy).then_inc(xaT_ok[p], 1)
                    for p in range(2):
                        act.wait_ge(kvq_ps[p], i + 1)
                        nc.scalar.activation(
                            kvq[:, 2 * i + p], bank[4 + p][:G96, :T96 * 3 * HID].rearrange("p (t d) -> p t d", t=T96),
                            ACT.Copy).then_inc(kvq_ok[p], 1)
        if upto == 1:
            dbg(nc, ctx, kvq[:].rearrange("p b t d -> p (b t d)"))
            return

        TD = T96 * HID
        kx = lsb("kx", [G96, T96, HID])
        ek = lsb("ek", [G96, B, TD])
        ekv = lsb("ekv", [G96, B, TD])
        eq = lsb("eq", [G96, B, TD])
        mt = lsb("mt", [TD, 4, CH])
        y = [lsb(f"y{p}", [TD, CH]) for p in range(2)]
        oT = wide0[:, :N]
        kmax, ksub, eks, ekvs, eqs, tab, wmix = (sem(n) for n in "kmax ksub eks ekvs eqs tab wmix".split())
        mix_ps, qTs, y_ok, oT_ps, oT_ok, tok_ps, tok_ok = (
            sem(n) for n in "mix_ps qTs y_ok oT_ps oT_ok tok_ps tok_ok".split())
        dve2 = sem("dve2")
        kv4 = kvq[:].rearrange("p b t (x d) -> p b t x d", x=3)
        split_h, split_l = sem("split_h"), sem("split_l")
        with nc.Block() as block:
            @block.vector
            def _(dve):
                d = Steps(dve, dve2)
                d.did(nc.vector.tensor_reduce(kx[:], kv4[:, :, :, 0, :].rearrange("p b t d -> p t d b"), AX.X, ALU.max))
                d.wait()
                for b in range(B):
                    ins = nc.vector.tensor_tensor(ek[:, b].rearrange("p (t d) -> p t d", t=T96), kv4[:, b, :, 0, :],
                                                  kx[:], ALU.subtract)
                ins.then_inc(ksub, 1)
                dve.wait_ge(tab, 1)
                nc.vector.tensor_tensor(Wmix[:].rearrange("p (k i) -> p k i", k=4),
                                        konst[:G96, K_DIAG:K_DIAG + G96].rearrange("p (k i) -> p k i", k=4),
                                        tabT[:].unsqueeze(1).to_broadcast([G96, 4, S]), ALU.mult).then_inc(wmix, 1)
                dve.wait_ge(eks, 1)
                for b in range(B):
                    ins = nc.vector.tensor_tensor(ekv[:, b].rearrange("p (t d) -> p t d", t=T96),
                                                  ek[:, b].rearrange("p (t d) -> p t d", t=T96),
                                                  kv4[:, b, :, 1, :], ALU.mult)
                ins.then_inc(ekvs, 1)
                dve.wait_ge(eqs, 1)
                d.did(nc.vector.tensor_scalar(eq[:], eq[:], 1.0, None, ALU.add))
                for h in range(2):
                    m = mt[:, 2 * h:2 * h + 2]
                    dve.wait_ge(qTs, h + 1)
                    d.did(nc.vector.tensor_tensor(m[:, 1], bank[3 * h][:TD, :CH], m[:, 0], ALU.mult))
                    d.wait()
                    d.did(nc.vector.reciprocal(m[:, 0], m[:, 1]))
                    d.wait()
                    nc.vector.tensor_tensor(y[h][:], bank[3 * h + 1][:TD, :CH], m[:, 0], ALU.mult).then_inc(y_ok, 1)
                dve.wait_ge(split_h, 1)
                nc.vector.tensor_tensor(gu_w[1][:], wstage[:], gu_w[0][:].bitcast(F32), ALU.subtract).then_inc(split_l, 1)
                with dve.Fori(0, NT // 3) as i:
                    dve.wait_ge(tok_ps, i + 1)
                    nc.vector.tensor_tensor(R[:, bass.ds(3 * i, 3), :], R[:, bass.ds(3 * i, 3), :],
                                            bank[6][:, :CH].rearrange("p (t c) -> p t c", c=C),
                                            ALU.add).then_inc(tok_ok, 1)

            @block.scalar
            def _(act):
                nc.scalar.activation(tabT[:], tabT[:], ACT.Exp).then_inc(tab, 1)
                for b in range(B):
                    ins = nc.scalar.activation(eq[:, b].rearrange("p (t d) -> p t d", t=T96), kv4[:, b, :, 2, :],
                                               ACT.Exp, scale=-1.0)
                ins.then_inc(eqs, 1)
                act.wait_ge(ksub, 1)
                nc.scalar.activation(ek[:], ek[:], ACT.Exp).then_inc(eks, 1)
                for h in range(2):
                    act.wait_ge(mix_ps, h + 1)
                    nc.scalar.activation(mt[:, 2 * h], bank[3 * h + 2][:TD, :CH], ACT.Copy).then_inc(qTs, 1)
                nc.scalar.activation(gu_w[0][:], wstage[:], ACT.Copy).then_inc(split_h, 1)
                for h in range(2):
                    for t in range(T96):
                        n = h * T96 + t
                        act.wait_ge(oT_ps, n + 1)
                        nc.scalar.activation(
                            oT.rearrange("c (b t n) -> c b t n", b=B, t=T96)[:, 4 * h:4 * h + 4, t, :],
                            bank[6 + n % 2][:, :CH].rearrange("c (b n) -> c b n", b=4),
                            ACT.Identity, bias=ob[:]).then_inc(oT_ok, 1)

            @block.tensor
            def _(pe):
                pe.wait_ge(ekvs, 1)
                pe.wait_ge(wmix, 1)
                pe.wait_ge(dve2, 2)
                for h in range(2):
                    for b in range(4):
                        at = slice(b * G96, (b + 1) * G96)
                        nc.tensor.matmul(bank[3 * h][:TD, at], ek[:, 4 * h + b], Wmix[:], start=True, stop=True)
                        nc.tensor.matmul(bank[3 * h + 1][:TD, at], ekv[:, 4 * h + b], Wmix[:], start=True, stop=True)
                        last = nc.tensor.transpose(bank[3 * h + 2][:TD, at], eq[:, 4 * h + b], ident[:G96, :G96])
                    last.then_inc(mix_ps, 1)
                for h in range(2):
                    pe.wait_ge(y_ok, h + 1)
                    for t in range(T96):
                        n = h * T96 + t
                        if n >= 2:
                            pe.wait_ge(oT_ok, n - 1)
                        nc.tensor.matmul(bank[6 + n % 2][:, :CH], woT[:, t, :], y[h][:], start=True,
                                         stop=True).then_inc(oT_ps, 1)
                pe.wait_ge(oT_ok, 2 * T96)
                for i in range(NT // 3):
                    if i >= 1:
                        pe.wait_ge(tok_ok, i)
                    for t in range(3):
                        last = nc.tensor.transpose(bank[6][:, t * P:(t + 1) * P],
                                                   oT[:, (3 * i + t) * P:(3 * i + t + 1) * P], ident)
                    last.then_inc(tok_ps, 1)
        if upto == 2:
            dbg(nc, ctx, R[:].rearrange("p t c -> p (t c)"))
            return
        local.close()

        def group(i, p):
            return bass.ds(2 * GT * i + GT * p, GT)

        def chunk_use(i, p, j):
            u = 3 * p + j
            return u % 2, 3 * i + u // 2

        lg2 = sb("lg2", [P, NT, E2])
        local = ExitStack()
        ctx.callback(local.close)
        xTH, xTL = wide1, wide2
        var3, rs3, xn3, tr3, xt3, xl3, lm3, lg3 = (
            sems(n) for n in "var3 rs3 xn3 tr3 xt3 xl3 lm3 lg3".split())
        dve3, dve3b, ex3, spl3, cps3, csb3, cdr3, cT3, cz3, sl3 = (
            sem(n) for n in "dve3 dve3b ex3 spl3 cps3 csb3 cdr3 cT3 cz3 sl3".split())
        cT = lsb("cT", [40, N], F32R)
        with nc.Block() as block:
            @block.gpsimd
            def _(pool):
                nc.gpsimd.memset(cT[:].bitcast(F32), 0.0).then_inc(cz3, 1)
                with pool.Fori(0, 2) as i:
                    for p in range(2):
                        pool.wait_ge(var3[p], i + 1)
                        norm_rstd(GT, p, P, rs3[p])

            @block.vector
            def _(dve):
                d = Steps(dve, dve3)
                with dve.Fori(0, 2) as i:
                    d.enter(i, 2 * NORM_STEPS)
                    for p in range(2):
                        norm_stats(d, R[:, group(i, p), :], GT, p, P, EPS_T, var3[p])
                    for p in range(2):
                        dve.wait_ge(rs3[p], i + 1)
                        dve.wait_ge(tr3[0], 3 * i)
                        dve.wait_ge(tr3[1], 3 * i)
                        norm_apply(R[:, group(i, p), :], GT, p, P, xn3[p])
                        for j in range(3):
                            q, n = chunk_use(i, p, j)
                            dve.wait_ge(xt3[q], n + 1)
                            at = bass.ds(CH * (6 * i + 3 * p + j), CH)
                            nc.vector.tensor_tensor(xTL[:, at], bank[q][:, :CH], xTH[:, at].bitcast(F32),
                                                    ALU.subtract).then_inc(xl3[q], 1)
                        dve.wait_ge(lm3[q], n + 1)
                        nc.vector.tensor_copy(lg2[:, group(i, p), :],
                                              bank[2 + p][:, :GT * E2].rearrange("p (t e) -> p t e", e=E2)
                                              ).then_inc(lg3[p], 1)
                d.leave(2)

            @block.scalar
            def _(act):
                with act.Fori(0, 2) as i:
                    for p in range(2):
                        for j in range(3):
                            q, n = chunk_use(i, p, j)
                            act.wait_ge(tr3[q], n + 1)
                            act.wait_ge(lm3[q], n)
                            nc.scalar.activation(xTf[q][:], bank[q][:, :CH], ACT.Copy)
                            nc.scalar.activation(xTH[:, bass.ds(CH * (6 * i + 3 * p + j), CH)], bank[q][:, :CH],
                                                 ACT.Copy).then_inc(xt3[q], 1)

            @block.tensor
            def _(pe):
                def logits(i, p, j):
                    q, n = chunk_use(i, p, j)
                    pe.wait_ge(xt3[q], n + 1)
                    for t in range(3):
                        k = 3 * j + t
                        last = nc.tensor.matmul(bank[2 + p][:, k * E2:(k + 1) * E2], xTf[q][:, t * P:(t + 1) * P],
                                                rt2[:], start=True, stop=True)
                    last.then_inc(lm3[q], 1)

                with pe.Fori(0, 2) as i:
                    for p in range(2):
                        pe.wait_ge(xn3[p], i + 1)
                        pe.wait_ge(lg3[p], i)
                        for j in range(3):
                            q, n = chunk_use(i, p, j)
                            pe.wait_ge(xl3[q], n)
                            for t in range(3):
                                last = nc.tensor.transpose(bank[q][:, t * P:(t + 1) * P], xn[p][:, 3 * j + t, :], ident)
                            last.then_inc(tr3[q], 1)
                            if j:
                                logits(i, p, j - 1)
                        logits(i, p, 2)

        d8 = lsb("d8", [P, NT, E2])
        ex8 = lsb("ex8", [P, NT, E2])
        w8 = [lsb(f"w8_{k}", [P, NT, E2]) for k in range(3)]
        col = [lsb(f"col{k}", [P, NT]) for k in range(4)]
        cH = lsb("cH", [P, 2, NT * E2])
        cHr = lsb("cHr", [P, NT * E2], F32R)
        cS = lsb("cS", [P, 2, 3, P])
        cdram = nc.dram_tensor("cdram", [2, NT * E2, P], F32, kind="Internal").ap()
        CR = [P, P, NT * E2 - 2 * P]
        with nc.Block() as block:
            @block.vector
            def _(dve):
                d = Steps(dve, dve3b)

                def wide(c):
                    return c[:].unsqueeze(2).to_broadcast([P, NT, E2])

                pri = konst[:, K_PRI:K_PRI + E2].unsqueeze(1).to_broadcast([P, NT, E2])

                def first_max(v, oh, tmp, m):
                    d.did(nc.vector.tensor_reduce(m[:], v[:], AX.X, ALU.max))
                    d.wait()
                    d.did(nc.vector.tensor_tensor(tmp[:], v[:], wide(m), ALU.is_equal))
                    d.wait()
                    d.did(nc.vector.tensor_tensor(tmp[:], tmp[:], pri, ALU.mult))
                    d.wait()
                    d.did(nc.vector.tensor_reduce(m[:], tmp[:], AX.X, ALU.max))
                    d.wait()
                    d.did(nc.vector.tensor_tensor(oh[:], tmp[:], wide(m), ALU.is_equal))
                    d.wait()

                d.did(nc.vector.tensor_reduce(col[0][:], lg2[:], AX.X, ALU.max))
                d.wait()
                nc.vector.tensor_tensor(d8[:], lg2[:], wide(col[0]), ALU.subtract).then_inc(sl3, 1)
                dve.wait_ge(sl3, 1)
                first_max(d8, w8[0], w8[2], col[1])
                d.did(nc.vector.scalar_tensor_tensor(lg2[:], w8[0][:], -1.0e30, d8[:], ALU.mult, ALU.add))
                d.wait()
                first_max(lg2, w8[1], w8[2], col[2])
                d.did(nc.vector.tensor_tensor(w8[0][:], w8[0][:], w8[1][:], ALU.add))
                dve.wait_ge(ex3, 1)
                d.did(nc.vector.tensor_reduce(col[0][:], ex8[:], AX.X, ALU.add))
                d.wait()
                d.did(nc.vector.reciprocal(col[3][:], col[0][:]))
                d.did(nc.vector.tensor_tensor(w8[1][:], w8[0][:], ex8[:], ALU.mult))
                d.wait()
                d.did(nc.vector.tensor_tensor(w8[2][:], w8[1][:], wide(col[3]), ALU.mult))
                d.wait()
                d.did(nc.vector.tensor_copy(cHr[:], w8[2][:].rearrange("p t e -> p (t e)")))
                d.wait()
                d.did(nc.vector.tensor_copy(cH[:, 0], cHr[:].bitcast(F32)))
                d.did(nc.vector.tensor_tensor(cH[:, 1], w8[2][:].rearrange("p t e -> p (t e)"), cHr[:].bitcast(F32),
                                              ALU.subtract))
                d.wait()
                nc.vector.tensor_copy(sel[:], konst[:40, K_SEL:K_SEL + E2 * H2]).then_inc(spl3, 1)

            @block.scalar
            def _(act):
                act.wait_ge(sl3, 1)
                nc.scalar.activation(ex8[:], d8[:], ACT.Exp).then_inc(ex3, 1)
                act.wait_ge(cps3, 1)
                for h in range(2):
                    for k in range(3):
                        ins = nc.scalar.activation(cS[:CR[k], h, k, :], bank[h][:CR[k], k * P:(k + 1) * P], ACT.Copy)
                ins.then_inc(csb3, 1)

            @block.tensor
            def _(pe):
                pe.wait_ge(spl3, 1)
                for h in range(2):
                    for k in range(3):
                        last = nc.tensor.transpose(bank[h][:CR[k], k * P:(k + 1) * P],
                                                   cH[:, h, k * P:k * P + CR[k]], ident)
                last.then_inc(cps3, 1)

            @block.sync
            def _(sp):
                sp.wait_ge(csb3, 1)
                for h in range(2):
                    for k in range(3):
                        sp.dma_start(cdram[h, k * P:k * P + CR[k], :], cS[:CR[k], h, k, :]).then_inc(cdr3, 16)
                sp.wait_ge(cdr3, 16 * 6)
                for h in range(2):
                    sp.dma_start(cT[32 * h:32 * h + E2, :].bitcast(F32).rearrange("e (t n) -> e t n", t=NT),
                                 cdram[h].rearrange("(t e) n -> e t n", e=E2)).then_inc(cT3, 16)
                sp.wait_ge(cT3, 32)
        if upto == 3:
            dbg(nc, ctx, cT[:].bitcast(F32), xTH[:].bitcast(F32), xTL[:].bitcast(F32))
            return

        s4 = [lsb(f"s4_{q}", [P, CH]) for q in range(2)]
        t4 = [lsb(f"t4_{q}", [P, CH]) for q in range(2)]
        h4 = [lsb(f"h4_{q}", [P, CH]) for q in range(2)]
        y4 = [lsb(f"y4_{p}", [P, CH]) for p in range(2)]
        g_ps, u_ps, s_ok, h_ok, dn, yS, zt = (sems(n) for n in "g_ps u_ps s_ok h_ok dn yS zt".split())
        cb_ps, t_ok, R_ok = sem("cb_ps"), sem("t_ok"), sem("R_ok")
        zrow = lsb("zrow", [P, 12, C])
        z4, zf4 = sem("z4"), sem("zf4")
        ZFILLS = SLOTS // (SR * 12) + NT // 12
        TRIPS = N // CH // 2
        UB = 2 * NB2
        UPS = NB2 - 1

        def use(i, u):
            return u % 2, NB2 * i + u // 2

        def rows(k):
            return P if k < NB2 - 1 else H2

        with nc.Block() as block:
            @block.gpsimd
            def _(pool):
                nc.gpsimd.memset(zrow[:], 0.0).then_inc(z4, 1)

            @block.sync
            def _(sp):
                sp.wait_ge(z4, 1)
                for k in range(SLOTS // (SR * 12)):
                    sp.dma_start(slots[k * SR * 12:(k + 1) * SR * 12, :].rearrange("(p t) c -> p t c", t=12),
                                 zrow[:SR]).then_inc(zf4, 16)
                for k in range(NT // 12):
                    sp.dma_start(slots[SLOTS + k * P * 12:SLOTS + (k + 1) * P * 12, :].rearrange("(p t) c -> p t c", t=12),
                                 zrow[:]).then_inc(zf4, 16)
                sp.wait_ge(zf4, 16 * ZFILLS)

            @block.tensor
            def _(pe):
                def tokens(i, u):
                    return bass.ds(CH * (2 * i + u // NB2), CH)

                def gate_up(i, u):
                    q, n = use(i, u)
                    k = u % NB2
                    for which, done in ((0, g_ps), (1, u_ps)):
                        if k == NB2 - 1 and which == 1:
                            break
                        if which == 0:
                            pe.wait_ge(s_ok[q], n)
                        pe.wait_ge(h_ok[q], n)
                        o = bank[2 * which + q][:, :CH]
                        w = slice((2 * k + which) * P, (2 * k + which + 1) * P)
                        at = tokens(i, u)
                        nc.tensor.matmul(o, gu_w[0][:, w], xTH[:, at], start=True, stop=False)
                        nc.tensor.matmul(o, gu_w[0][:, w], xTL[:, at], start=False, stop=False)
                        nc.tensor.matmul(o, gu_w[1][:, w], xTH[:, at], start=False, stop=True).then_inc(done[q], 1)

                def spread(i, u):
                    k = u % NB2
                    if k < NB2 - 1:
                        nc.tensor.matmul(bank[4][:, :CH], sel[:, k * P:(k + 1) * P], cT[:, tokens(i, u)],
                                         start=True, stop=True).then_inc(cb_ps, 1)

                def down(i, u):
                    q, n = use(i, u)
                    k, p = u % NB2, u // NB2
                    if k == 0:
                        pe.wait_ge(yS[p], i)
                    pe.wait_ge(h_ok[q], n + 1)
                    nc.tensor.matmul(bank[5 + p][:, :CH], wd[:rows(k), k, :], h4[q][:rows(k), :],
                                     start=k == 0, stop=k == NB2 - 1).then_inc(dn[q], 1)

                def back(i, p):
                    pe.wait_ge(yS[p], i + 1)
                    if p == 0:
                        pe.wait_ge(R_ok, 2 * i)
                    else:
                        pe.wait_ge(R_ok, 2 * i + 1)
                    for t in range(3):
                        last = nc.tensor.transpose(bank[7][:, t * P:(t + 1) * P], y4[p][:, t * P:(t + 1) * P], ident)
                    last.then_inc(zt[p], 1)

                def trip(i, final):
                    for u in range(UB):
                        if u + 1 < UB:
                            gate_up(i, u + 1)
                        elif not final:
                            gate_up(i + 1, 0)
                        down(i, u)
                        if u + 1 < UB:
                            spread(i, u + 1)
                        elif not final:
                            spread(i + 1, 0)
                        if u == NB2 + 1:
                            back(i, 0)
                    back(i, 1)

                gate_up(0, 0)
                spread(0, 0)
                with pe.Fori(0, TRIPS - 1) as i:
                    trip(i, False)
                trip(TRIPS - 1, True)

            @block.scalar
            def _(act):
                def silu(i, u):
                    q, n = use(i, u)
                    r = rows(u % NB2)
                    act.wait_ge(g_ps[q], n + 1)
                    act.wait_ge(h_ok[q], n)
                    nc.scalar.activation(s4[q][:r], bank[q][:r, :CH], ACT.Silu).then_inc(s_ok[q], 1)

                def trip(i, final):
                    for u in range(UB):
                        if u + 1 < UB:
                            silu(i, u + 1)
                        elif not final:
                            silu(i + 1, 0)
                        if u % NB2 == NB2 - 1:
                            p = u // NB2
                            q, n = use(i, u)
                            act.wait_ge(dn[q], n + 1)
                            act.wait_ge(zt[p], i)
                            nc.scalar.activation(y4[p][:], bank[5 + p][:, :CH], ACT.Copy).then_inc(yS[p], 1)

                silu(0, 0)
                with act.Fori(0, TRIPS - 1) as i:
                    trip(i, False)
                trip(TRIPS - 1, True)

            @block.vector
            def _(dve):
                d = Steps(dve, t_ok)

                def residual(i, p):
                    dve.wait_ge(zt[p], i + 1)
                    at = bass.ds(6 * i + 3 * p, 3)
                    nc.vector.tensor_tensor(R[:, at, :], R[:, at, :], bank[7][:, :CH].rearrange("p (t c) -> p t c", c=C),
                                            ALU.add).then_inc(R_ok, 1)

                with dve.Fori(0, TRIPS) as i:
                    d.enter(i, 2 * (NB2 - 1))
                    for u in range(UB):
                        q, n = use(i, u)
                        k = u % NB2
                        r = rows(k)
                        dve.wait_ge(s_ok[q], n + 1)
                        if k < NB2 - 1:
                            dve.wait_ge(u_ps[q], UPS * i + sum(v % 2 == q and v % NB2 < NB2 - 1 for v in range(u + 1)))
                            d.did(nc.vector.tensor_tensor(t4[q][:], bank[2 + q][:, :CH], s4[q][:], ALU.mult))
                            d.wait()
                            dve.wait_ge(cb_ps, (NB2 - 1) * 2 * i + (NB2 - 1) * (u // NB2) + k + 1)
                            dve.wait_ge(dn[q], n)
                            nc.vector.tensor_tensor(h4[q][:], bank[4][:, :CH], t4[q][:], ALU.mult).then_inc(h_ok[q], 1)
                        else:
                            dve.wait_ge(dn[q], n)
                            nc.vector.tensor_tensor(h4[q][:r], bank[q][r:2 * r, :CH], s4[q][:r],
                                                    ALU.mult).then_inc(h_ok[q], 1)
                        if u == NB2 + 1:
                            residual(i, 0)
                    residual(i, 1)
                d.leave(TRIPS)
        local.close()
        if upto == 4:
            dbg(nc, ctx, R[:].rearrange("p t c -> p (t c)"))
            return

        stage5[0] = True
        GN = GT * P
        NG = NT // GT
        JB = [(k * P, min(P, SS - k * P)) for k in range(NB_SS)]
        PT = [wide0[:, p * NB_SS * SS:(p + 1) * NB_SS * SS].rearrange("j (k i) -> j k i", k=NB_SS) for p in range(2)]
        hT, lT = wide1, wide2
        LAST = B + 6
        gidx = sb("gidx", [P, NT], I32)
        prob = sb("prob", [P, NT])
        local = ExitStack()
        ctx.callback(local.close)
        V = [lsb(f"V{p}", [P, NB_SS, C + 1]) for p in range(2)]
        sH = [lsb(f"sH{p}", [P, SS], F32R) for p in range(2)]
        sQK = [lsb(f"sQK{p}", [P, SS], F32R) for p in range(2)]
        Q = [lsb(f"Q{p}", [97, SS], F32R) for p in range(3)]
        K = [lsb(f"K{p}", [97, NB_SS * P], F32R) for p in range(3)]
        mx = [lsb(f"mx{p}", [P, NB_SS]) for p in range(2)]
        rs = [lsb(f"rs{p}", [P, NB_SS]) for p in range(2)]
        nmr = [lsb(f"nmr{p}", [P, GT]) for p in range(2)]
        tri = lsb("tri", [P, P], BF16)
        ones = lsb("ones", [P, P], BF16)
        oh = [lsb(f"oh{p}", [P, GT, E1], BF16) for p in range(2)]
        lg = [lsb(f"lg{p}", [P, GT, E1]) for p in range(2)]
        lx = [lsb(f"lx{p}", [P, GT, E1]) for p in range(2)]
        w1 = [lsb(f"w1_{p}", [P, GT, E1]) for p in range(2)]
        cm = [lsb(f"cm{p}", [P, 8, GT]) for p in range(2)]
        sidx = [lsb(f"sidx{p}", [P, GT], I32) for p in range(2)]
        carry = lsb("carry", [P, 2, E1])
        init5, var5, var6, rs5, rs6, xn5, xn6, t_ps, t_hi, t_lo, qk_ps, sh_ok, st_ok, qk_in = (
            sem(n) for n in "init5 var5 var6 rs5 rs6 xn5 xn6 t_ps t_hi t_lo qk_ps sh_ok st_ok qk_in".split())
        qk_in = [qk_in, sem("qk_in1")]
        v_ps, v_ok, e_ps, mx_ok, mT, mH, mL, et_ps, pt_ok, pv, o_ok, k0, k6 = (
            sem(n) for n in "v_ps v_ok e_ps mx_ok mT mH mL et_ps pt_ok pv o_ok k0 k6".split())
        l_tr, l_xt, l_ps, lg_ok, d6, ex6, oh6, cnt6, cr6, sx6, dve5, rr5, r6 = (
            sem(n) for n in "l_tr l_xt l_ps lg_ok d6 ex6 oh6 cnt6 cr6 sx6 dve5 rr5 r6".split())
        sc6 = sems("sc6")
        early.close()

        def halves(ap, rows=P):
            return ap[:rows].rearrange("r (h n) -> r h n", h=2)[:, :, :HALF]

        def i_blocks(n):
            g, odd = n // 2, n % 2
            if not odd:
                return [(k * P, m, GT * g + k, 0) for k, (_, m) in enumerate(JB)]
            return [(0, P // 2, GT * g + NB_SS - 1, P // 2)] + [
                (P // 2 + k * P, P, GT * g + NB_SS + k, 0) for k in range(NB_SS - 1)]

        def tiles(g):
            return slice(GT * g, GT * (g + 1))

        def ahead(n):
            g, chunks = ((n + 3) // 2, (0, 1)) if n % 2 else ((n + 2) // 2, (2,))
            return (g, chunks) if 0 <= g < NG else (None, ())

        def behind(n, lag):
            g = (n - lag) // 2
            return g if (n - lag) % 2 == 0 and 0 <= g < NG else None

        def per_expert(c):
            return c.unsqueeze(2).to_broadcast([P, GT, E1])

        K0 = 15
        BEFORE = 2
        with nc.Block() as block:
            @block.gpsimd
            def _(pool):
                for g in range(BEFORE):
                    pool.wait_ge(var5, g + 1)
                    norm_rstd(GT, g, P, rs5)
                z = Steps(pool, k0)
                firsts = [(K[q][:], 0.0) for q in range(3)] + [(Q[q][64:97, :], 0.0) for q in range(3)]
                firsts += [(Q[q][r:r + 1, :], -1.0) for q in range(3) for r in (64, 96)]
                firsts += [(V[p][:, :, C:C + 1], 1.0) for p in range(2)] + [(carry[:], 0.0)]
                for ap, value in firsts:
                    z.did(nc.gpsimd.memset(ap.bitcast(F32), value))
                    z.wait()
                for g in range(BEFORE, NG):
                    p = g % 2
                    pool.wait_ge(var5, g + 1)
                    pool.wait_ge(xn5, g - 1)
                    norm_rstd(GT, p, P, rs5)
                    pool.wait_ge(rs5, g + 1)
                    pool.wait_ge(t_ps, 3 * (g - 1))
                    for t in range(GT):
                        ins = nc.gpsimd.tensor_scalar(xn[p][:, t, :], R[:, GT * g + t, :], sm[p][:, 4, t:t + 1],
                                                      rstd[p][:, t:t + 1], ALU.subtract, ALU.mult)
                    ins.then_inc(xn5, 1)

                def scatter(g):
                    pool.wait_ge(sx6, g + 1)
                    for t in range(GT):
                        nc.gpsimd.indirect_dma_start(
                            slots, bass.IndirectOffsetOnAxis(sidx[g % 2][:, t:t + 1], 0),
                            xn[g % 2][:, t, :], None).then_inc(sc6[g % 2], 16)

                for g in range(NG):
                    p = g % 2
                    pool.wait_ge(var6, g + 1)
                    if g >= 2:
                        pool.wait_ge(xn6, 3 * (g - 1))
                    norm_rstd(GT, p, P, rs6)
                    pool.wait_ge(rs6, 2 * g + 1)
                    nc.gpsimd.tensor_tensor(nmr[p][:], sm[p][:, 4, :], rstd[p][:], ALU.mult).then_inc(rs6, 1)
                    if g:
                        scatter(g - 1)
                scatter(NG - 1)
                for p in range(2):
                    pool.wait_ge(sc6[p], 16 * GT * 2)

            @block.sync
            def _(sp):
                for done in early_sems:
                    sp.sem_clear(done)
                sp.wait_ge(k0, K0)
                for n in range(B):
                    q = n % 3
                    sp.wait_ge(st_ok, n + 1)
                    if n >= 3:
                        sp.wait_ge(et_ps, NB_SS * (n - 2))
                    sp.dma_start(Q[q][0:64, :].bitcast(F32), sQK[n % 2][0:64, :].bitcast(F32)).then_inc(qk_in[n % 2], 16)
                    sp.dma_start(K[q][0:64, :SS].bitcast(F32), sQK[n % 2][64:128, :].bitcast(F32)).then_inc(
                        qk_in[n % 2], 16)

            @block.vector
            def _(dve):
                d = Steps(dve, dve5)
                o_step = Steps(dve, rr5)
                r = Steps(dve, r6)

                def apply5(g):
                    p = g % 2
                    dve.wait_ge(rs5, g + 1)
                    norm_apply(R[:, tiles(g), :], GT, p, P, xn5)

                def maximum(n, k):
                    m = JB[k][1]
                    dve.wait_ge(e_ps, NB_SS * n + k + 1)
                    if k == 0 and n >= 2:
                        dve.wait_ge(mT, n - 1)
                    nc.vector.tensor_reduce(mx[n % 2][:m, k:k + 1], halves(psum[1], m), AX.XY, ALU.max).then_inc(mx_ok, 1)

                def stack(n):
                    dve.wait_ge(sh_ok, n + 1)
                    if n >= 2:
                        dve.wait_ge(qk_in[n % 2], 32 * (n // 2))
                    nc.vector.scalar_tensor_tensor(
                        sQK[n % 2][:].rearrange("r (h n) -> r h n", h=2), halves(psum[2]), konst[:, K_SGN + 1:K_SGN + 2],
                        sH[n % 2][:].bitcast(F32).rearrange("r (h n) -> r h n", h=2),
                        ALU.mult, ALU.subtract).then_inc(st_ok, 1)

                def low_row(n):
                    dve.wait_ge(mH, n + 1)
                    nc.vector.tensor_tensor(K[n % 3][96:97, :SS], psum[1][0:1, :SS], K[n % 3][64:65, :SS].bitcast(F32),
                                            ALU.subtract).then_inc(mL, 1)

                def attended(n, ks):
                    blocks = i_blocks(n)
                    dve.wait_ge(pv, NB_SS * n + ks[-1] + 1)
                    for k in ks:
                        _, m, _, lo = blocks[k]
                        at = k % 3 * (C + 1) + C
                        o_step.did(nc.vector.reciprocal(rs[n % 2][lo:lo + m, k:k + 1],
                                                        bank[6 + k // 3][lo:lo + m, at:at + 1]))
                    o_step.wait()
                    for k in ks:
                        _, m, tile, lo = blocks[k]
                        o = bank[6 + k // 3][lo:lo + m, k % 3 * (C + 1):k % 3 * (C + 1) + C]
                        at = R[lo:lo + m, tile, :]
                        nc.vector.scalar_tensor_tensor(at, o, rs[n % 2][lo:lo + m, k:k + 1], at,
                                                       ALU.mult, ALU.add).then_inc(o_ok, 1)

                def low_halves(n):
                    g, chunks = ahead(n)
                    for c in chunks:
                        dve.wait_ge(t_hi, 3 * g + c + 1)
                        at = slice(g * GN + c * CH, g * GN + (c + 1) * CH)
                        nc.vector.tensor_tensor(lT[:, at], bank[4 + c % 2][:, :CH], hT[:, at].bitcast(F32),
                                                ALU.subtract).then_inc(t_lo, 1)

                def add_bias(g, c):
                    dve.wait_ge(l_ps, 3 * g + c + 1)
                    nc.vector.tensor_tensor(lg[g % 2][:, 3 * c:3 * c + 3, :],
                                            bank[4 + c % 2][:, CH:CH + 3 * E1].rearrange("p (t e) -> p t e", e=E1),
                                            rb1[:].unsqueeze(1).to_broadcast([P, 3, E1]), ALU.add).then_inc(lg_ok, 1)

                def route_max(g):
                    p = g % 2
                    c = cm[p]
                    dve.wait_ge(lg_ok, 3 * g + 3)
                    r.did(nc.vector.tensor_reduce(c[:, 0], lg[p][:], AX.X, ALU.max))
                    r.wait()
                    nc.vector.tensor_tensor(lx[p][:], lg[p][:], per_expert(c[:, 0]), ALU.subtract).then_inc(d6, 1)
                    r.did(nc.vector.tensor_tensor(w1[p][:], lg[p][:], per_expert(c[:, 0]), ALU.is_equal))

                def route_first(g):
                    p = g % 2
                    c = cm[p]
                    r.wait()
                    r.did(nc.vector.tensor_tensor(w1[p][:], w1[p][:],
                                                  konst[:, K_PRI + 16:K_PRI + 32].unsqueeze(1).to_broadcast([P, GT, E1]),
                                                  ALU.mult))
                    r.wait()
                    r.did(nc.vector.tensor_reduce(c[:, 1], w1[p][:], AX.X, ALU.max))
                    r.wait()
                    nc.vector.tensor_tensor(oh[p][:], w1[p][:], per_expert(c[:, 1]), ALU.is_equal).then_inc(oh6, 1)

                def route_slot(g):
                    p = g % 2
                    c = cm[p]
                    dve.wait_ge(oh6, g + 1)
                    r.did(nc.vector.tensor_tensor(w1[p][:], oh[p][:],
                                                  konst[:, K_EB:K_EB + E1].unsqueeze(1).to_broadcast([P, GT, E1]),
                                                  ALU.mult))
                    r.wait()
                    r.did(nc.vector.tensor_reduce(c[:, 2], w1[p][:], AX.X, ALU.add))

                def place_counts(g):
                    p = g % 2
                    dve.wait_ge(cnt6, g + 1)
                    if g:
                        dve.wait_ge(cr6, g)
                    else:
                        dve.wait_ge(k0, K0)
                    r.did(nc.vector.tensor_tensor(lg[p][:], bank[4][:, :GT * E1].rearrange("p (t e) -> p t e", e=E1),
                                                  carry[:, p].unsqueeze(1).to_broadcast([P, GT, E1]), ALU.add))
                    nc.vector.tensor_tensor(carry[:, 1 - p], bank[4][:, GT * E1:(GT + 1) * E1], carry[:, p],
                                            ALU.add).then_inc(cr6, 1)

                def place_sums(g):
                    p = g % 2
                    c = cm[p]
                    r.wait()
                    r.did(nc.vector.tensor_tensor(w1[p][:], lg[p][:], oh[p][:], ALU.mult))
                    dve.wait_ge(ex6, g + 1)
                    r.did(nc.vector.tensor_reduce(c[:, 3], lx[p][:], AX.X, ALU.add))
                    r.wait()
                    r.did(nc.vector.tensor_reduce(c[:, 4], w1[p][:], AX.X, ALU.add))
                    r.did(nc.vector.reciprocal(prob[:, tiles(g)], c[:, 3]))

                def place_index(g):
                    p = g % 2
                    c = cm[p]
                    r.wait()
                    r.did(nc.vector.tensor_scalar(c[:, 5], c[:, 4], float(CAP), None, ALU.is_le))
                    r.did(nc.vector.scalar_tensor_tensor(c[:, 6], c[:, 4], -1.0, c[:, 2], ALU.add, ALU.add))
                    r.wait()
                    trash = konst[:, K_N:K_N + NT][:, tiles(g)]
                    r.did(nc.vector.tensor_tensor(c[:, 6], c[:, 6], trash, ALU.subtract))
                    r.wait()
                    r.did(nc.vector.tensor_tensor(c[:, 6], c[:, 6], c[:, 5], ALU.mult))
                    r.wait()
                    r.did(nc.vector.tensor_tensor(c[:, 6], c[:, 6], trash, ALU.add))
                    r.wait()
                    if g >= 2:
                        dve.wait_ge(sc6[p], 16 * GT * (g // 2))
                    nc.vector.tensor_copy(sidx[p][:], c[:, 6]).then_inc(sx6, 1)
                    r.did(nc.vector.scalar_tensor_tensor(gidx[:, tiles(g)], c[:, 5], float(SLOTS + N), c[:, 6],
                                                         ALU.mult, ALU.add))

                for g in range(BEFORE):
                    norm_stats(d, R[:, tiles(g), :], GT, g, P, EPS_C, var5)
                nc.vector.tensor_copy(tri[:], konst[:, K_TRI:K_TRI + P]).then_inc(k6, 1)
                nc.vector.tensor_copy(ones[:], konst[:, K_ONE:K_ONE + P]).then_inc(k6, 1)
                apply5(0)
                low_halves(-3)
                for n in range(-2, LAST):
                    stats = n + 2 if n in (0, 1) else behind(n, 3)
                    for k in range(NB_SS):
                        if 0 <= n + 1 < B:
                            maximum(n + 1, k)
                        if k == 0 and n + 2 < B:
                            stack(n + 2)
                        if stats is not None and k < 3:
                            if k == 0 and n in (0, 1):
                                dve.wait_ge(xn5, stats - 1)
                            elif k == 0 and stats >= 2:
                                dve.wait_ge(xn6, 3 * (stats - 1))
                            elif k == 0:
                                dve.wait_ge(xn5, stats + 3)
                            for t in range(3 * k, 3 * k + 3):
                                ins = nc.vector.bn_stats(st[stats % 2][:, t, :], R[:, GT * stats + t, :])
                        if k == 2 and behind(n, 5) is not None:
                            add_bias(behind(n, 5), 0)
                            add_bias(behind(n, 5), 1)
                        if k == 3 and 0 <= n - 1 < B:
                            attended(n - 1, (0, 1, 2))
                        if k < 3 and behind(n, 6) is not None:
                            (route_max, route_first, route_slot)[k](behind(n, 6))
                        if k == 4 and behind(n, 6) is not None:
                            place_counts(behind(n, 6))
                        if k < 2 and behind(n, 7) is not None:
                            (place_sums, place_index)[k](behind(n, 7))
                    if stats is not None:
                        norm_moments(d, ins, GT, stats % 2, P, EPS_C if n in (0, 1) else EPS_T,
                                     var5 if n in (0, 1) else var6, mean=0.5 if n in (0, 1) else -0.5)
                    if n == -2:
                        low_halves(n)
                        apply5(1)
                    if 0 <= n + 1 < B:
                        low_row(n + 1)
                    if behind(n, 5) is not None:
                        add_bias(behind(n, 5), 2)
                    if n > -2:
                        low_halves(n)
                    if 0 <= n - 1 < B:
                        attended(n - 1, (3, 4))

            @block.scalar
            def _(act):
                def high_halves(n):
                    g, chunks = ahead(n)
                    for c in chunks:
                        act.wait_ge(t_ps, 3 * g + c + 1)
                        nc.scalar.activation(hT[:, g * GN + c * CH:g * GN + (c + 1) * CH], bank[4 + c % 2][:, :CH],
                                             ACT.Copy).then_inc(t_hi, 1)

                def router_copy(g, c):
                    act.wait_ge(l_tr, 3 * g + c + 1)
                    if 3 * g + c >= 2:
                        act.wait_ge(l_ps, 3 * g + c - 1)
                    nc.scalar.activation(xTf[(3 * g + c) % 2][:], bank[4 + c % 2][:, :CH], ACT.Copy).then_inc(l_xt, 1)

                for n in range(-3, LAST):
                    g = behind(n, 4)
                    for k in range(NB_SS):
                        if 0 <= n < B:
                            m = JB[k][1]
                            act.wait_ge(et_ps, NB_SS * n + k + 1)
                            if k == 0 and n >= 2:
                                act.wait_ge(pv, NB_SS * (n - 1))
                            nc.scalar.activation(PT[n % 2][:m, k, :].rearrange("j (h n) -> j h n", h=2),
                                                 halves(psum[0], m), ACT.Exp).then_inc(pt_ok, 1)
                        if k == 0 and 0 <= n + 2 < B:
                            act.wait_ge(qk_ps, n + 3)
                            if n >= 0:
                                act.wait_ge(st_ok, n + 1)
                            nc.scalar.activation(sH[n % 2][:].rearrange("r (h n) -> r h n", h=2), halves(psum[2]),
                                                 ACT.Copy, scale=konst[:, K_SGN:K_SGN + 1]).then_inc(sh_ok, 1)
                        if k == 1 and behind(n, 5) is not None:
                            router_copy(behind(n, 5), 0)
                            router_copy(behind(n, 5), 1)
                        if k == 1 and behind(n, 6) is not None:
                            p = behind(n, 6) % 2
                            act.wait_ge(d6, behind(n, 6) + 1)
                            nc.scalar.activation(lx[p][:], lx[p][:], ACT.Exp).then_inc(ex6, 1)
                        if g is not None and k < 3:
                            if k == 0:
                                act.wait_ge(rs6, 2 * g + 2)
                                if g >= 2:
                                    act.wait_ge(sc6[g % 2], 16 * GT * (g // 2))
                                else:
                                    act.wait_ge(t_ps, 3 * (g + 3))
                            for t in range(3 * k, 3 * k + 3):
                                ins = nc.scalar.activation(xn[g % 2][:, t, :], R[:, GT * g + t, :], ACT.Identity,
                                                           bias=nmr[g % 2][:, t:t + 1], scale=rstd[g % 2][:, t:t + 1])
                            ins.then_inc(xn6, 1)
                        if k == 3 and 0 <= n < B:
                            act.wait_ge(v_ps, n + 1)
                            if n >= 2:
                                act.wait_ge(pv, NB_SS * (n - 1))
                            for kk, (_, m) in enumerate(JB):
                                at = kk // 4 * 512 + kk % 4 * C
                                ins = nc.scalar.activation(V[n % 2][:m, kk, :C], psum[2][:m, at:at + C], ACT.Copy,
                                                           scale=gam[:m])
                            ins.then_inc(v_ok, 1)
                    if 0 <= n + 1 < B:
                        act.wait_ge(k0, K0)
                        act.wait_ge(mT, n + 2)
                        nc.scalar.activation(K[(n + 1) % 3][64:65, :SS], psum[1][0:1, :SS], ACT.Copy).then_inc(mH, 1)
                    if behind(n, 5) is not None:
                        router_copy(behind(n, 5), 2)
                    high_halves(n)

            @block.tensor
            def _(pe):
                issued = dict(T=0, QK=0, V=0, L=0, C=0)

                def banks_empty():
                    for kind, read in (("T", t_lo), ("QK", st_ok), ("V", v_ok), ("L", lg_ok), ("C", cr6)):
                        if issued[kind]:
                            pe.wait_ge(read, issued[kind])

                def transposes(n):
                    g, chunks = ahead(n)
                    if chunks:
                        pe.wait_ge(xn5, g + 1)
                        banks_empty()
                    for c in chunks:
                        for t in range(3):
                            last = nc.tensor.transpose(bank[4 + c % 2][:, t * P:(t + 1) * P], xn[g % 2][:, 3 * c + t, :],
                                                       ident)
                        last.then_inc(t_ps, 1)
                        issued["T"] += 1

                def project_qk(n):
                    banks_empty()
                    w = slice(W_QK, W_QK + C)
                    for h in range(2):
                        o = psum[2][:, h * 512:h * 512 + HALF]
                        at = slice(n * SS + h * HALF, n * SS + (h + 1) * HALF)
                        nc.tensor.matmul(o, gu_w[0][:, w], hT[:, at], start=True, stop=False)
                        nc.tensor.matmul(o, gu_w[0][:, w], lT[:, at], start=False, stop=False)
                        last = nc.tensor.matmul(o, gu_w[1][:, w], hT[:, at], start=False, stop=True)
                    last.then_inc(qk_ps, 1)
                    issued["QK"] += 1

                def project_v(n):
                    banks_empty()
                    w = slice(W_V, W_V + C)
                    for k, (j0, m) in enumerate(JB):
                        o = psum[2][:m, k // 4 * 512 + k % 4 * C:k // 4 * 512 + k % 4 * C + C]
                        at = slice(n * SS + j0, n * SS + j0 + m)
                        nc.tensor.matmul(o, hT[:, at], gu_w[0][:, w], start=True, stop=False)
                        nc.tensor.matmul(o, lT[:, at], gu_w[0][:, w], start=False, stop=False)
                        last = nc.tensor.matmul(o, hT[:, at], gu_w[1][:, w], start=False, stop=True)
                    last.then_inc(v_ps, 1)
                    issued["V"] += 1

                def energies(n, k):
                    if k:
                        pe.wait_ge(mx_ok, NB_SS * n + k)
                    else:
                        pe.wait_ge(k0, K0)
                        pe.wait_ge(qk_in[n % 2], 32 * (n // 2 + 1))
                        if n:
                            pe.wait_ge(mL, n)
                    i0 = JB[k][0]
                    for h in range(2):
                        last = nc.tensor.matmul(psum[1][:, h * 512:h * 512 + HALF], K[n % 3][:64, i0:i0 + P],
                                                Q[n % 3][:64, h * HALF:(h + 1) * HALF], start=True, stop=True)
                    last.then_inc(e_ps, 1)

                def energies_T(n, k):
                    j0, m = JB[k]
                    if k == 0:
                        pe.wait_ge(mL, n + 1)
                    if n or k:
                        pe.wait_ge(pt_ok, NB_SS * n + k)
                    for h in range(2):
                        last = nc.tensor.matmul(psum[0][:m, h * 512:h * 512 + HALF], Q[n % 3][:, j0:j0 + m],
                                                K[n % 3][:, h * HALF:(h + 1) * HALF], start=True, stop=True)
                    last.then_inc(et_ps, 1)

                def maxima_row(n):
                    pe.wait_ge(mx_ok, NB_SS * (n + 1))
                    for k, (i0, m) in enumerate(JB):
                        last = nc.tensor.transpose(psum[1][0:1, i0:i0 + m], mx[n % 2][:m, k:k + 1], ident[:m, :m])
                    last.then_inc(mT, 1)

                def attend(n, k):
                    i0, m, _, lo = i_blocks(n)[k]
                    if k == 0:
                        pe.wait_ge(pt_ok, NB_SS * (n + 1))
                        pe.wait_ge(v_ok, n + 1)
                    if k in (0, 3) and n:
                        pe.wait_ge(o_ok, NB_SS * (n - 1) + (3 if k == 0 else NB_SS))
                    for jk, (_, mj) in enumerate(JB):
                        last = nc.tensor.matmul(bank[6 + k // 3][lo:lo + m, k % 3 * (C + 1):(k % 3 + 1) * (C + 1)],
                                                PT[n % 2][:mj, jk, i0:i0 + m], V[n % 2][:mj, jk, :],
                                                start=jk == 0, stop=jk == NB_SS - 1)
                    last.then_inc(pv, 1)

                def router_transposes(g, c):
                    pe.wait_ge(xn6, 3 * g + c + 1)
                    if c == 0:
                        banks_empty()
                    elif c == 2:
                        banks_empty()
                    for t in range(3):
                        last = nc.tensor.transpose(bank[4 + c % 2][:, t * P:(t + 1) * P], xn[g % 2][:, 3 * c + t, :], ident)
                    last.then_inc(l_tr, 1)
                    issued["L"] += 1

                def logits(g, c):
                    pe.wait_ge(l_xt, 3 * g + c + 1)
                    for t in range(3):
                        last = nc.tensor.matmul(bank[4 + c % 2][:, CH + t * E1:CH + (t + 1) * E1],
                                                xTf[(3 * g + c) % 2][:, t * P:(t + 1) * P], rt1[:], start=True, stop=True)
                    last.then_inc(l_ps, 1)

                def counts(g):
                    banks_empty()
                    pe.wait_ge(k6, 2)
                    pe.wait_ge(oh6, g + 1)
                    o = bank[4]
                    nc.tensor.matmul(o[:, :GT * E1], tri[:], oh[g % 2][:].rearrange("p t e -> p (t e)"),
                                     start=True, stop=False, skip_group_check=True)
                    for t in range(GT):
                        later = GT - t
                        last = nc.tensor.matmul(
                            o[:, (t + 1) * E1:(GT + 1) * E1].rearrange("p (k e) -> p k e", e=E1), ones[:],
                            oh[g % 2][:, t:t + 1, :].to_broadcast([P, later, E1]),
                            start=False, stop=t == GT - 1, skip_group_check=True)
                    last.then_inc(cnt6, 1)
                    issued["C"] += 1

                transposes(-3)
                for n in range(-2, LAST):
                    g = behind(n, 5)
                    for k in range(NB_SS):
                        if 0 <= n - 1 < B and k < NB_SS - 1:
                            attend(n - 1, k)
                        if 0 <= n + 1 < B:
                            energies(n + 1, k)
                        if 0 <= n < B:
                            energies_T(n, k)
                        if k == 0 and n + 2 < B:
                            project_qk(n + 2)
                        if k == 1 and g is not None:
                            router_transposes(g, 0)
                            router_transposes(g, 1)
                        if k == 2 and g is not None:
                            logits(g, 0)
                            logits(g, 1)
                        if k == 3 and 0 <= n < B:
                            project_v(n)
                        if k == 4 and g is not None:
                            router_transposes(g, 2)
                        if k == 4 and behind(n, 6) is not None:
                            counts(behind(n, 6))
                        if 0 <= n - 1 < B and k == NB_SS - 1:
                            attend(n - 1, k)
                    if 0 <= n + 1 < B:
                        maxima_row(n + 1)
                    if g is not None:
                        logits(g, 2)
                    transposes(n)
        local.close()
        if upto == 6:
            dbg(nc, ctx, gidx[:], prob[:])
            return

        local = ExitStack()
        ctx.callback(local.close)
        NBUF, NBANK = 8, 4
        USES = NBUF // NBANK
        xe = [lsb(f"xe{k}", [SR, 3, C]) for k in range(NBUF)]
        ye = [lsb(f"ye{k}", [SR, 3, C]) for k in range(NBUF)]
        xeT = [lsb(f"xeT{k}", [C, CAP]) for k in range(NBANK)]
        in7, st7 = sems("in7", NBUF), sems("st7", NBUF)
        tr7, xt7, ym7, ye7 = (sems(n, NBANK) for n in "tr7 xt7 ym7 ye7".split())
        NPART = NT // 3
        ga8 = sems("ga8", NPART)
        r8, o8 = sem("r8"), sem("o8")
        rows_in = slots[0:SLOTS, :].rearrange("(e p t) c -> e p t c", e=E1, t=3)
        rows_out = slots[SLOTS + N:, :].rearrange("(e p t) c -> e p t c", e=E1, t=3)
        out_t = out.rearrange("b h w c -> (b h w) c").rearrange("(t p) c -> p t c", p=P)
        fetched = [xn[0][:], xn[1][:]] + [wide0[:, p * GT * C:(p + 1) * GT * C].rearrange("p (t c) -> p t c", c=C)
                                          for p in range(2)]

        def buffers(i):
            return [(k, k % NBANK, USES * i + k // NBANK) for k in range(NBUF)]

        with nc.Block() as block:
            @block.sync
            def _(sp):
                with sp.Fori(0, E1 // NBUF) as i:
                    for k, _, _ in buffers(i):
                        expert = sp.snap(NBUF * i + k)
                        sp.wait_ge(tr7[k % NBANK], USES * i)
                        sp.dma_start(xe[k][:], rows_in[expert]).then_inc(in7[k], 16)
                for part in range(NPART):
                    at = slice(3 * part, 3 * part + 3)
                    sp.wait_ge(r8, part + 1)
                    sp.dma_start(out_t[:, at, :], R[:, at, :]).then_inc(o8, 16)
                sp.wait_ge(o8, 16 * NPART)

            @block.tensor
            def _(pe):
                def product(i, k, q, n):
                    pe.wait_ge(xt7[q], n + 1)
                    pe.wait_ge(ye7[q], n)
                    for t in range(3):
                        last = nc.tensor.matmul(bank[NBANK + q][:SR, t * C:(t + 1) * C], xeT[q][:, t * SR:(t + 1) * SR],
                                                ew[:, bass.ds(NBUF * i + k, 1), :], start=True, stop=True)
                    last.then_inc(ym7[q], 1)

                with pe.Fori(0, E1 // NBUF) as i:
                    for k, q, n in buffers(i):
                        pe.wait_ge(in7[k], 16 * i + 16)
                        pe.wait_ge(xt7[q], n)
                        for t in range(3):
                            last = nc.tensor.transpose(bank[q][:, t * SR:(t + 1) * SR], xe[k][:, t, :], ident[:SR, :SR])
                        last.then_inc(tr7[q], 1)
                        if k >= 2:
                            product(i, *buffers(i)[k - 2])
                    for late in buffers(i)[-2:]:
                        product(i, *late)

            @block.scalar
            def _(act):
                def store(i, k, q, n):
                    act.wait_ge(ye7[q], n + 1)
                    act.dma_start(rows_out[NBUF * i + k], ye[k][:]).then_inc(st7[k], 16)

                with act.Fori(0, E1 // NBUF) as i:
                    for k, q, n in buffers(i):
                        act.wait_ge(tr7[q], n + 1)
                        act.wait_ge(ym7[q], n)
                        nc.scalar.activation(xeT[q][:], bank[q][:, :CAP], ACT.Copy).then_inc(xt7[q], 1)
                        if k >= 4:
                            store(i, *buffers(i)[k - 4])
                    for late in buffers(i)[-4:]:
                        store(i, *late)

            @block.vector
            def _(dve):
                with dve.Fori(0, E1 // NBUF) as i:
                    for k, q, n in buffers(i):
                        dve.wait_ge(ym7[q], n + 1)
                        dve.wait_ge(st7[k], 16 * i)
                        nc.vector.tensor_tensor(ye[k][:], bank[NBANK + q][:SR, :CH].rearrange("p (t c) -> p t c", c=C),
                                                eb[:SR, bass.ds(NBUF * i + k, 1), :].to_broadcast([SR, 3, C]),
                                                ALU.add).then_inc(ye7[q], 1)
                for part in range(NPART):
                    dve.wait_ge(ga8[part], 16 * 3)
                    for t in range(3 * part, 3 * part + 3):
                        ins = nc.vector.scalar_tensor_tensor(R[:, t, :], fetched[t // GT][:, t % GT, :], prob[:, t:t + 1],
                                                             R[:, t, :], ALU.mult, ALU.add)
                    ins.then_inc(r8, 1)

            @block.gpsimd
            def _(pool):
                for k in range(NBUF):
                    pool.wait_ge(st7[k], 16 * (E1 // NBUF))
                for t in range(NT):
                    nc.gpsimd.indirect_dma_start(
                        fetched[t // GT][:, t % GT, :], None, slots,
                        bass.IndirectOffsetOnAxis(gidx[:, t:t + 1], 0)).then_inc(ga8[t // 3], 16)


def constants():
    import numpy as np

    k = np.zeros((P, K_COLS), np.float32)
    row = np.arange(P)
    k[:, K_ID:K_ID + P] = np.eye(P)
    k[:, K_TRI:K_TRI + P] = row[:, None] <= row[None, :]
    k[:, K_ONE:K_ONE + P] = 1
    k[:G96, K_DIAG:K_DIAG + G96] = row[:G96, None] // S == row[None, :G96] // S
    for e in range(E2):
        k[e, K_SEL + e * H2:K_SEL + (e + 1) * H2] = 1
        k[32 + e, K_SEL + e * H2:K_SEL + (e + 1) * H2] = 1
    high = np.where(row < 64, row < 32, row % 32 < 16)
    k[:, K_SGN] = np.where(high, -1, 1)
    k[:, K_SGN + 1] = np.where(high, 0, 1)
    k[:, K_PRI:K_PRI + E2] = E2 - np.arange(E2)
    k[:, K_PRI + 16:K_PRI + 32] = E1 - np.arange(E1)
    k[:, K_EB:K_EB + E1] = np.arange(E1) * CAP
    k[:, K_N:K_N + NT] = SLOTS + np.arange(NT)[None, :] * P + row[:, None]
    return k


def lay_out(inputs):
    import numpy as np

    g = {n: np.asarray(a) for n, a in inputs.items()}
    pairs = [np.transpose(g[f"L0_ffn_W_{n}"], (1, 0, 2)).reshape(C, E2 // 2, 2 * H2) for n in ("gate", "up")]
    experts = np.stack(pairs, 2).reshape(C, 2 * E2 * H2)
    qk = [np.tile(g["L1_conv_Wq"], (1, 4)), np.tile(g["L1_conv_Wk"], (1, 4))]
    return {
        "x": g["x"],
        "konst": constants(),
        "wkvq": np.concatenate([g[f"L0_conv_w{n}_w"].T for n in "kvq"], 1),
        "bkvq": np.tile(np.concatenate([g[f"L0_conv_w{n}_b"] for n in "kvq"]), T96)[None],
        "woT": g["L0_conv_out_w"].T,
        "ob": g["L0_conv_out_b"],
        "tabT": g["L0_conv_w_bias_table"][:S, :S].T,
        "wstage": np.concatenate([experts, g["L0_ffn_shared_gate"], g["L0_ffn_shared_up"], *qk, g["L1_conv_Wv"]], 1),
        "wd": g["L0_ffn_W_down"].reshape(E2 * H2, C),
        "wd_s": g["L0_ffn_shared_down"],
        "rt2": g["L0_ffn_router"],
        "rt1": g["L1_ffn_switch_w"].T,
        "rb1": g["L1_ffn_switch_b"],
        "gam": g["L1_conv_gamma"],
        "ew": np.transpose(g["L1_ffn_expert_w"], (2, 0, 1)),
        "eb": g["L1_ffn_expert_b"],
    }


def kernel(**inputs):
    import numpy as np
    import concourse.bacc as bacc
    from concourse.bass_utils import run_bass_kernel_spmd

    nc = bacc.Bacc("TRN2", target_bir_lowering=False, num_devices=1)
    arrays = {f"in_{n}": np.ascontiguousarray(a) for n, a in lay_out(inputs).items()}
    A = {n[3:]: nc.dram_tensor(n, a.shape, mybir.dt.from_np(a.dtype), kind="ExternalInput").ap()
         for n, a in arrays.items()}
    out = nc.dram_tensor("out", (B, S, S, C), F32, kind="ExternalOutput").ap()
    metaformer_kernel(nc, A, out)
    r = run_bass_kernel_spmd(nc, [arrays], core_ids=[0])
    return r.results[0]["out"]
```

```python
from contextlib import ExitStack

import concourse.bass as bass
from concourse import mybir

F32 = mybir.dt.float32
F32R = mybir.dt.float32r
BF16 = mybir.dt.bfloat16
I32 = mybir.dt.int32
ALU = mybir.AluOpType
ACT = mybir.ActivationFunctionType
AX = mybir.AxisListType

B, S, C = 8, 24, 128
SS = S * S
N = B * SS
P = 128
NT = N // P
HID = 16
G96 = 4 * S
T96 = SS // G96
E2, H2 = 8, 64
NB2 = E2 // 2 + 1
E1 = 16
CAP = int(1.2 * N / E1)
SR = P
SLOTS = E1 * 3 * SR
GT = 9
CH = 3 * P
HALF = SS // 2
NB_SS = -(-SS // P)
EPS_C, EPS_T = 1e-6, 1e-5

K_ID, K_TRI, K_ONE, K_DIAG, K_SEL, K_SGN, K_PRI, K_EB = 0, 128, 256, 384, 480, 992, 994, 1026
K_N = K_EB + 16
K_COLS = K_N + NT


class Steps:

    def __init__(self, eng, sem):
        self.eng, self.sem, self.base, self.n = eng, sem, 0, 0

    def did(self, ins):
        ins.then_inc(self.sem, 1)
        self.n += 1

    def wait(self):
        self.eng.wait_ge(self.sem, self.base + self.n)

    def enter(self, i, per):
        self.start, self.per = self.base + self.n, per
        self.base, self.n = self.start + i * per, 0

    def leave(self, trips):
        assert self.n == self.per, (self.n, self.per)
        self.base, self.n = self.start + trips * self.per, 0


def metaformer_kernel(nc, A, out):
    ctx = ExitStack()
    with ctx:
        def sb(name, shape, dt=F32):
            return ctx.enter_context(nc.sbuf_tensor(name, shape, dt))

        early, early_sems = ExitStack(), []

        def sem(name):
            early_sems.append(early.enter_context(nc.semaphore(name)))
            return early_sems[-1]

        def sems(name, n=2):
            return [sem(f"{name}{j}") for j in range(n)]

        def late_sem(name):
            return ctx.enter_context(nc.semaphore(name))

        def late_sems(name, n=2):
            return [late_sem(f"{name}{j}") for j in range(n)]

        R = sb("R", [P, NT, C])
        konst = sb("konst", [P, K_COLS])
        ident = konst[:, K_ID:K_ID + P]
        xn = [sb(f"xn{p}", [P, GT, C]) for p in range(2)]
        NG = NT // GT
        st_all = sb("st", [P, NG, GT, 6])
        sm_all = sb("sm", [P, NG, 6, GT])
        rstd_all = sb("rstd", [P, NG, GT])
        st, sm, rstd = ([a[:, g] for g in range(NG)] for a in (st_all, sm_all, rstd_all))
        xTf = [sb(f"xTf{p}", [P, CH]) for p in range(2)]
        wide0 = sb("wide0", [P, 2 * 5 * SS])
        wide1 = sb("wide1", [P, N], F32R)
        wide2 = sb("wide2", [P, N], F32R)
        neg_half = sb("neg_half", [P, GT])
        psum = [ctx.enter_context(nc.psum_tensor(f"ps{j}", [P, 1024], F32)) for j in range(4)]
        bank = [psum[j // 2][:, (j % 2) * 512:(j % 2) * 512 + 512] for j in range(8)]

        slots = nc.dram_tensor("slots", [2 * SLOTS + N, C], F32, kind="Internal").ap()

        def norm_stats(d, src, n, p, rows, eps, var_ok, mean=0.5):
            for t in range(n):
                ins = nc.vector.bn_stats(st[p][:rows, t, :], src[:, t, :])
            norm_moments(d, ins, n, p, rows, eps, var_ok, mean)

        def norm_moments(d, ins, n, p, rows, eps, var_ok, mean=0.5):
            d.did(ins)
            d.wait()
            s, m = st[p][:rows, 0:n, :], sm[p]
            d.did(nc.vector.tensor_tensor(m[:rows, 1, :n], s[:, :, 1], s[:, :, 4], ALU.subtract))
            d.did(nc.vector.tensor_tensor(m[:rows, 0, :n], s[:, :, 1], s[:, :, 4], ALU.add))
            d.did(nc.vector.tensor_tensor(m[:rows, 2, :n], s[:, :, 2], s[:, :, 5], ALU.add))
            d.wait()
            d.did(nc.vector.tensor_tensor(m[:rows, 3, :n], m[:rows, 1, :n], m[:rows, 1, :n], ALU.mult))
            d.did(nc.vector.tensor_scalar(m[:rows, 4, :n], m[:rows, 0, :n], mean, None, ALU.mult))
            d.wait()
            d.did(nc.vector.scalar_tensor_tensor(m[:rows, 3, :n], m[:rows, 3, :n], C / 4.0, m[:rows, 2, :n],
                                                 ALU.mult, ALU.add))
            d.wait()
            nc.vector.tensor_scalar(m[:rows, 5, :n], m[:rows, 3, :n], 1.0 / C, eps,
                                    ALU.mult, ALU.add).then_inc(var_ok, 1)
        NORM_STEPS = 7

        def norm_rstd(n, p, rows, rstd_ok):
            nc.gpsimd.tensor_tensor(rstd[p][:rows, :n], sm[p][:rows, 5, :n], neg_half[:rows, :n],
                                    ALU.pow).then_inc(rstd_ok, 1)

        def norm_apply(src, n, p, rows, xn_ok):
            for t in range(n):
                ins = nc.vector.tensor_scalar(xn[p][:rows, t, :], src[:, t, :], sm[p][:rows, 4, t:t + 1],
                                              rstd[p][:rows, t:t + 1], ALU.subtract, ALU.mult)
            ins.then_inc(xn_ok, 1)

        wkvq = sb("wkvq", [C, 3 * HID])
        bkvq = sb("bkvq", [G96, T96 * 3 * HID])
        wo = sb("wo", [33, C])
        tabT = sb("tabT", [G96, S])
        Wmix = sb("Wmix", [G96, G96])
        wcol = 2 * NB2 * P - P
        wstage = sb("wstage", [C, wcol + 2 * C])
        gu_w = [sb(f"gu_w{h}", [C, wcol + 2 * C], F32R) for h in range(2)]
        wd = sb("wd", [P, NB2, C])
        sel = sb("sel", [40, E2 // 2 * P], F32R)
        rt2 = sb("rt2", [C, E2])
        rt1 = sb("rt1", [C, E1])
        rb1 = sb("rb1", [P, E1])
        gam = sb("gam", [P, 1])
        ew = sb("ew", [C, E1, C])
        eb = sb("eb", [P, E1, C])
        W_QK, W_V = wcol, wcol + C

        ld = sem("ld")
        ld2 = sem("ld2")

        local = ExitStack()
        ctx.callback(local.close)

        def lsb(name, shape, dt=F32):
            return local.enter_context(nc.sbuf_tensor(name, shape, dt))

        kvq = lsb("kvq", [G96, B, T96, 3 * HID])
        stage1 = ExitStack()
        ctx.callback(stage1.close)
        xall = stage1.enter_context(nc.sbuf_tensor("xall", [G96, B * T96, C], F32))
        nmr_odd = stage1.enter_context(nc.sbuf_tensor("nmr_odd", [G96, T96], F32))
        xaT = [wide0[:, p * SS:(p + 1) * SS] for p in range(2)]

        def image(i, p):
            return bass.ds(T96 * (2 * i + p), T96)

        xa_in, xn_ok, xaT_ps, xaT_ok = sems("xa_in"), sems("xn_ok"), sems("xaT_ps"), sems("xaT_ok")
        var_ok, rstd_ok, kvq_ps, kvq_ok = sems("var_ok"), sems("rstd_ok"), sems("kvq_ps"), sems("kvq_ok")
        dve1, msk = sem("dve1"), sem("msk")
        wo0 = sem("wo0")
        LOADS1, LOADS2 = 3, 2 + 4 + 11
        with nc.Block() as block:
            @block.sync
            def _(sp):
                for b in range(B):
                    if b >= 2:
                        sp.wait_ge(xa_in[b % 2], 16 * (b // 2))
                    sp.dma_start(xall[:, T96 * b:T96 * (b + 1), :],
                                 A["x"][b].rearrange("(t r) w c -> (r w) t c", r=4)).then_inc(xa_in[b % 2], 16)
                    if b == 1:
                        sp.dma_start(ident, A["konst"][:, K_ID:K_ID + P]).then_inc(ld, 16)
                        sp.dma_start(wkvq[:], A["wkvq"]).then_inc(ld, 16)
                        sp.dma_start(bkvq[:], A["bkvq"].to_broadcast([G96, T96 * 3 * HID])).then_inc(ld, 16)
                sp.dma_start(konst[:, K_ID + P:], A["konst"][:, K_ID + P:]).then_inc(ld2, 16)
                sp.dma_start(R[:], A["x"].rearrange("b h w c -> (b h w) c").rearrange(
                    "(t p) c -> p t c", p=P)).then_inc(ld2, 16)
                for k in range(4):
                    sp.dma_start(tabT[k * S:(k + 1) * S, :], A["tabT"]).then_inc(ld2, 16)
                sp.wait_ge(wo0, 1)
                sp.dma_start(wo[0:HID, :], A["woT"]).then_inc(ld2, 16)
                sp.dma_start(wo[32:33, :], A["ob"].rearrange("(o c) -> o c", o=1)).then_inc(ld2, 16)
                sp.dma_start(wstage[:], A["wstage"]).then_inc(ld2, 16)
                sp.dma_start(wd[:, 0:NB2 - 1, :], A["wd"].rearrange("(k p) c -> p k c", p=P)).then_inc(ld2, 16)
                sp.dma_start(wd[0:H2, NB2 - 1, :], A["wd_s"]).then_inc(ld2, 16)
                sp.dma_start(rt2[:], A["rt2"]).then_inc(ld2, 16)
                sp.dma_start(rt1[:], A["rt1"]).then_inc(ld2, 16)
                sp.dma_start(rb1[:], A["rb1"].rearrange("(o e) -> o e", o=1).to_broadcast([P, E1])).then_inc(ld2, 16)
                sp.dma_start(gam[:], A["gam"].rearrange("(o e) -> o e", o=1).to_broadcast([P, 1])).then_inc(ld2, 16)
                sp.dma_start(ew[:], A["ew"]).then_inc(ld2, 16)
                sp.dma_start(eb[:], A["eb"].rearrange("(o e) c -> o e c", o=1).to_broadcast([P, E1, C])).then_inc(ld2, 16)
                sp.wait_ge(ld2, 16 * LOADS2)

            @block.gpsimd
            def _(pool):
                nc.gpsimd.memset(wo[:], 0.0).then_inc(wo0, 1)
                nc.gpsimd.memset(neg_half[:], -0.5).then_inc(msk, 1)
                pool.wait_ge(msk, 1)
                with pool.Fori(0, B // 2) as i:
                    for p in range(2):
                        pool.wait_ge(var_ok[p], i + 1)
                        norm_rstd(T96, p, G96, rstd_ok[p])
                    pool.wait_ge(rstd_ok[1], 2 * i + 1)
                    nc.gpsimd.tensor_tensor(nmr_odd[:], sm[1][:G96, 4, :T96], rstd[1][:G96, :T96],
                                            ALU.mult).then_inc(rstd_ok[1], 1)

            @block.vector
            def _(dve):
                d = Steps(dve, dve1)

                def add_bias(i):
                    dve.wait_ge(ld, 16 * LOADS1)
                    for p in range(2):
                        dve.wait_ge(kvq_ps[p], i + 1)
                        nc.vector.tensor_tensor(kvq[:, 2 * i + p],
                                                bank[4 + p][:G96, :T96 * 3 * HID].rearrange("p (t d) -> p t d", t=T96),
                                                bkvq[:].rearrange("p (t d) -> p t d", t=T96),
                                                ALU.add).then_inc(kvq_ok[p], 1)

                def trip(i, first=False):
                    for p in range(2):
                        dve.wait_ge(xa_in[p], 16 * i + 16)
                        if p and not first:
                            dve.wait_ge(xn_ok[1], i)
                        norm_stats(d, xall[:, image(i, p), :], T96, p, G96, EPS_C, var_ok[p], mean=(0.5, -0.5)[p])
                    dve.wait_ge(rstd_ok[0], i + 1)
                    if not first:
                        dve.wait_ge(xaT_ps[0], i)
                    norm_apply(xall[:, image(i, 0), :], T96, 0, G96, xn_ok[0])

                trip(0, first=True)
                with dve.Fori(1, B // 2) as i:
                    d.enter(i - 1, 2 * NORM_STEPS)
                    trip(i)
                    add_bias(i - 1)
                d.leave(B // 2 - 1)
                add_bias(B // 2 - 1)

            @block.tensor
            def _(pe):
                def trip(i, first=False):
                    for p in range(2):
                        pe.wait_ge(xn_ok[p], i + 1)
                        if not first:
                            pe.wait_ge(xaT_ok[p], i)
                        for t in range(T96):
                            last = nc.tensor.transpose(
                                psum[p][:, (t // 3) * 512 + (t % 3) * G96:(t // 3) * 512 + (t % 3) * G96 + G96],
                                xn[p][:G96, t, :], ident[:G96, :G96])
                        last.then_inc(xaT_ps[p], 1)
                    for p in range(2):
                        pe.wait_ge(xaT_ok[p], i + 1)
                        if not first:
                            pe.wait_ge(kvq_ok[p], i)
                        o = bank[4 + p]
                        for t in range(T96):
                            last = nc.tensor.matmul(o[:G96, t * 3 * HID:(t + 1) * 3 * HID],
                                                    xaT[p][:, t * G96:(t + 1) * G96], wkvq[:],
                                                    start=True, stop=True)
                        last.then_inc(kvq_ps[p], 1)

                pe.wait_ge(ld, 16 * LOADS1)
                trip(0, first=True)
                with pe.Fori(1, B // 2) as i:
                    trip(i)

            @block.scalar
            def _(act):
                def trip(i, first=False):
                    act.wait_ge(rstd_ok[1], 2 * i + 2)
                    if not first:
                        act.wait_ge(xaT_ps[1], i)
                    for t in range(T96):
                        ins = nc.scalar.activation(xn[1][:G96, t, :], xall[:, image(i, 1), :][:, t, :], ACT.Identity,
                                                   bias=nmr_odd[:, t:t + 1], scale=rstd[1][:G96, t:t + 1])
                    ins.then_inc(xn_ok[1], 1)
                    for p in range(2):
                        act.wait_ge(xaT_ps[p], i + 1)
                        if not first:
                            act.wait_ge(kvq_ps[p], i)
                        nc.scalar.activation(xaT[p].rearrange("c (h n) -> c h n", h=2),
                                             psum[p][:].rearrange("c (h n) -> c h n", h=2)[:, :, :HALF],
                                             ACT.Copy).then_inc(xaT_ok[p], 1)

                trip(0, first=True)
                with act.Fori(1, B // 2) as i:
                    trip(i)

        stage1.close()
        TD = T96 * HID
        kx = lsb("kx", [G96, T96, HID])
        ek = lsb("ek", [G96, B, TD])
        ekv = lsb("ekv", [G96, B, TD])
        eq = lsb("eq", [G96, B, TD])
        mt = lsb("mt", [TD, 4, CH])
        y = [lsb(f"y{p}", [TD, CH]) for p in range(2)]
        ytok = wide0[0:33, :N]
        ksub, eks, ekvs, eqs, tab, wmix = (sem(n) for n in "ksub eks ekvs eqs tab wmix".split())
        mix_ps, qTs, y_ok, tok_ps, tok_ok, ones2 = (sem(n) for n in "mix_ps qTs y_ok tok_ps tok_ok ones2".split())
        y_in = sems("y_in")
        TOK = (6, 7, 0, 1)
        dve2 = sem("dve2")
        kv4 = kvq[:].rearrange("p b t (x d) -> p b t x d", x=3)
        split_h = sem("split_h")

        def btd(a):
            return a[:].rearrange("p b (t d) -> p b t d", t=T96)

        var3, rs3, dve3, nm3 = (sem(n) for n in "var3 rs3 dve3 nm3".split())
        xn3 = sems("xn3")
        nmr3 = [lsb(f"nmr3_{g}", [P, GT]) for g in range(2)]
        with nc.Block() as block:
            @block.vector
            def _(dve):
                d = Steps(dve, dve2)
                f = Steps(dve, dve3)

                def stats3(n):
                    dve.wait_ge(tok_ok, n + 1)
                    for t in range(3 * n, 3 * n + 3):
                        ins = nc.vector.bn_stats(st[t // GT][:, t % GT, :], R[:, t, :])
                    if n % 3 == 2:
                        norm_moments(f, ins, GT, n // 3, P, EPS_T, var3, mean=-0.5 if n < 6 else 0.5)

                d.did(nc.vector.tensor_reduce(kx[:], kv4[:, :, :, 0, :].rearrange("p b t d -> p t d b"), AX.X, ALU.max))
                d.wait()
                nc.vector.tensor_tensor(btd(ek), kv4[:, :, :, 0, :], kx[:].unsqueeze(1).to_broadcast([G96, B, T96, HID]),
                                        ALU.subtract).then_inc(ksub, 1)
                dve.wait_ge(tab, 1)
                nc.vector.tensor_tensor(Wmix[:].rearrange("p (k i) -> p k i", k=4),
                                        konst[:G96, K_DIAG:K_DIAG + G96].rearrange("p (k i) -> p k i", k=4),
                                        tabT[:].unsqueeze(1).to_broadcast([G96, 4, S]), ALU.mult).then_inc(wmix, 1)
                dve.wait_ge(eks, 1)
                nc.vector.tensor_tensor(btd(ekv), btd(ek), kv4[:, :, :, 1, :], ALU.mult).then_inc(ekvs, 1)
                dve.wait_ge(eqs, 1)
                d.did(nc.vector.tensor_scalar(eq[:], eq[:], 1.0, None, ALU.add))
                for h in range(2):
                    m = mt[:, 2 * h:2 * h + 2]
                    dve.wait_ge(qTs, h + 1)
                    d.did(nc.vector.tensor_tensor(m[:, 1], bank[3 * h][:TD, :CH], m[:, 0], ALU.mult))
                    d.wait()
                    d.did(nc.vector.reciprocal(m[:, 0], m[:, 1]))
                    d.wait()
                    nc.vector.tensor_tensor(y[h][:], bank[3 * h + 1][:TD, :CH], m[:, 0], ALU.mult).then_inc(y_ok, 1)
                dve.wait_ge(split_h, 1)
                nc.vector.tensor_tensor(gu_w[1][:], wstage[:], gu_w[0][:].bitcast(F32), ALU.subtract)
                for i in range(2):
                    for j in range(NT // 6):
                        n = NT // 6 * i + j
                        dve.wait_ge(tok_ps, n + 1)
                        nc.vector.tensor_tensor(R[:, 3 * n:3 * n + 3, :], R[:, 3 * n:3 * n + 3, :],
                                                bank[TOK[n % len(TOK)]][:, :CH].rearrange("p (t c) -> p t c", c=C),
                                                ALU.add).then_inc(tok_ok, 1)
                        if n:
                            stats3(n - 1)
                stats3(NT // 3 - 1)

            @block.scalar
            def _(act):
                nc.scalar.activation(tabT[:], tabT[:], ACT.Exp).then_inc(tab, 1)
                nc.scalar.activation(btd(eq), kv4[:, :, :, 2, :], ACT.Exp, scale=-1.0).then_inc(eqs, 1)
                act.wait_ge(ksub, 1)
                nc.scalar.activation(ek[:], ek[:], ACT.Exp).then_inc(eks, 1)
                for h in range(2):
                    act.wait_ge(mix_ps, h + 1)
                    nc.scalar.activation(mt[:, 2 * h], bank[3 * h + 2][:TD, :CH], ACT.Copy).then_inc(qTs, 1)
                nc.scalar.activation(gu_w[0][:], wstage[:], ACT.Copy).then_inc(split_h, 1)
                for g in range(2):
                    act.wait_ge(nm3, g + 1)
                    for t in range(GT):
                        ins = nc.scalar.activation(xn[g][:, t, :], R[:, GT * g + t, :], ACT.Identity,
                                                   bias=nmr3[g][:, t:t + 1], scale=rstd[g][:, t:t + 1])
                        if t % 3 == 2:
                            ins.then_inc(xn3[g], 1)

            @block.gpsimd
            def _(pool):
                nc.gpsimd.memset(ytok[:], 1.0).then_inc(ones2, 1)
                for g in range(NG):
                    pool.wait_ge(var3, g + 1)
                    norm_rstd(GT, g, P, rs3)
                    if g < 2:
                        pool.wait_ge(rs3, g + 1)
                        nc.gpsimd.tensor_tensor(nmr3[g][:], sm[g][:, 4, :], rstd[g][:], ALU.mult).then_inc(nm3, 1)

            @block.sync
            def _(sp):
                sp.wait_ge(ones2, 1)
                for h in range(2):
                    sp.wait_ge(y_ok, h + 1)
                    for t in range(T96):
                        to = ytok[0:HID, :].rearrange("d (b t n) -> d b t n", b=B, t=T96)
                        sp.dma_start(to[:, 4 * h:4 * h + 4, t, :],
                                     y[h][t * HID:(t + 1) * HID, :].rearrange("d (b n) -> d b n", b=4)
                                     ).then_inc(y_in[h], 16)

            @block.tensor
            def _(pe):
                pe.wait_ge(ekvs, 1)
                pe.wait_ge(wmix, 1)
                pe.wait_ge(dve2, 2)
                for h in range(2):
                    for b in range(4):
                        at = slice(b * G96, (b + 1) * G96)
                        nc.tensor.matmul(bank[3 * h][:TD, at], ek[:, 4 * h + b], Wmix[:], start=True, stop=True)
                        nc.tensor.matmul(bank[3 * h + 1][:TD, at], ekv[:, 4 * h + b], Wmix[:], start=True, stop=True)
                        last = nc.tensor.transpose(bank[3 * h + 2][:TD, at], eq[:, 4 * h + b], ident[:G96, :G96])
                    last.then_inc(mix_ps, 1)
                for h in range(2):
                    pe.wait_ge(y_in[h], 16 * T96)
                    for j in range(NT // 6):
                        n = NT // 6 * h + j
                        if n >= len(TOK):
                            pe.wait_ge(tok_ok, n - len(TOK) + 1)
                        for t in range(3):
                            last = nc.tensor.matmul(bank[TOK[n % len(TOK)]][:, t * P:(t + 1) * P],
                                                    ytok[:, (3 * n + t) * P:(3 * n + t + 1) * P], wo[:],
                                                    start=True, stop=True)
                        last.then_inc(tok_ps, 1)
        local.close()

        TRIPS3 = NG // 2

        BEFORE = 2
        var5, rs5, xn5, dve5, k0 = (late_sem(n) for n in "var5 rs5 xn5 dve5 k0".split())
        V = [sb(f"V{p}", [P, NB_SS, C + 1]) for p in range(2)]
        Q = [sb(f"Q{p}", [97, SS], F32R) for p in range(3)]
        K = [sb(f"K{p}", [97, NB_SS * P], F32R) for p in range(3)]
        carry = sb("carry", [P, 2, E1])
        lg2 = sb("lg2", [P, NT, E2])
        local = ExitStack()
        ctx.callback(local.close)
        xTH, xTL = wide1, wide2
        lm3, lg3 = sems("lm3"), sems("lg3")
        tr3, xt3, xl3 = (sem(n) for n in "tr3 xt3 xl3".split())
        dve3b, ex3, spl3, cps3, cH3, cL3, cz3, sl3 = (
            sem(n) for n in "dve3b ex3 spl3 cps3 cH3 cL3 cz3 sl3".split())
        cT = lsb("cT", [40, N], F32R)
        CB = [0, 1, 4, 5, 6, 7]
        TB = 4
        TH = NT // 2
        EARLY = TH // TB
        d8, ex8 = ([a[:, h * TH:(h + 1) * TH] for h in range(2)] for a in (
            lsb("d8", [P, NT, E2]), lsb("ex8", [P, NT, E2])))
        weights = lsb("weights", [P, NT, E2])
        w8 = [lsb(f"w8_{k}", [P, TH, E2]) for k in range(3)]
        col = [lsb(f"col{k}", [P, TH]) for k in range(2)]
        TOP2_STEPS = 15

        def wide(c):
            return c[:].unsqueeze(2).to_broadcast([P, TH, E2])

        def first_max(d, v, oh, tmp, m):
            pri = konst[:, K_PRI:K_PRI + E2].unsqueeze(1).to_broadcast([P, TH, E2])
            d.did(nc.vector.tensor_tensor(tmp[:], v, wide(m), ALU.is_equal))
            d.wait()
            d.did(nc.vector.tensor_tensor(tmp[:], tmp[:], pri, ALU.mult))
            d.wait()
            d.did(nc.vector.tensor_reduce(m[:], tmp[:], AX.X, ALU.max))
            d.wait()
            d.did(nc.vector.tensor_tensor(oh[:], tmp[:], wide(m), ALU.is_equal))
            d.wait()

        def choose(d, h):
            lg = lg2[:, h * TH:(h + 1) * TH, :]
            d.did(nc.vector.tensor_reduce(col[0][:], lg, AX.X, ALU.max))
            d.wait()
            nc.vector.tensor_tensor(d8[h], lg, wide(col[0]), ALU.subtract).then_inc(sl3, 1)
            first_max(d, lg, w8[0], w8[2], col[0])
            d.eng.wait_ge(sl3, h + 1)
            d.did(nc.vector.scalar_tensor_tensor(lg, w8[0][:], -1.0e30, d8[h], ALU.mult, ALU.add))
            d.wait()
            d.did(nc.vector.tensor_reduce(col[1][:], lg, AX.X, ALU.max))
            d.wait()
            first_max(d, lg, w8[1], w8[2], col[1])
            d.did(nc.vector.tensor_tensor(w8[0][:], w8[0][:], w8[1][:], ALU.add))

        def weigh(d, h):
            d.eng.wait_ge(ex3, h + 1)
            d.did(nc.vector.tensor_reduce(col[0][:], ex8[h], AX.X, ALU.add))
            d.wait()
            d.did(nc.vector.reciprocal(col[1][:], col[0][:]))
            d.did(nc.vector.tensor_tensor(w8[1][:], w8[0][:], ex8[h], ALU.mult))
            d.wait()
            nc.vector.tensor_tensor(weights[:, h * TH:(h + 1) * TH], w8[1][:], wide(col[1]),
                                    ALU.mult).then_inc(spl3, 1)

        with nc.Block() as block:
            @block.gpsimd
            def _(pool):
                nc.gpsimd.memset(cT[:].bitcast(F32), 0.0).then_inc(cz3, 1)

            @block.vector
            def _(dve):
                def apply(g):
                    dve.wait_ge(rs3, g + 1)
                    dve.wait_ge(tr3, 3 * (g - 1))
                    for t in range(GT):
                        ins = nc.vector.tensor_scalar(xn[g % 2][:, t, :], R[:, GT * g + t, :], sm[g][:, 4, t:t + 1],
                                                      rstd[g][:, t:t + 1], ALU.subtract, ALU.mult)
                        if t % 3 == 2:
                            ins.then_inc(xn3[g % 2], 1)

                def low_halves3(g):
                    for u in range(3 * g, 3 * g + 3):
                        dve.wait_ge(xt3, u + 1)
                        at = slice(CH * u, CH * (u + 1))
                        nc.vector.tensor_tensor(xTL[:, at], bank[CB[u % 6]][:, :CH], xTH[:, at].bitcast(F32),
                                                ALU.subtract).then_inc(xl3, 1)

                def keep_logits(g):
                    u = 3 * g + 2
                    dve.wait_ge(lm3[u % 2], u // 2 + 1)
                    nc.vector.tensor_copy(lg2[:, GT * g:GT * (g + 1), :],
                                          bank[2 + g % 2][:, :GT * E2].rearrange("p (t e) -> p t e", e=E2)
                                          ).then_inc(lg3[g % 2], 1)

                low_halves3(0)
                apply(2)
                low_halves3(1)
                keep_logits(0)
                apply(3)
                keep_logits(1)
                dve.wait_ge(lg3[1], 1)
                d = Steps(dve, dve3b)
                choose(d, 0)
                for g in range(2, NG):
                    low_halves3(g)
                    keep_logits(g)
                weigh(d, 0)
                assert d.n == TOP2_STEPS, d.n

            @block.scalar
            def _(act):
                for i in range(TRIPS3):
                    for u in range(6):
                        q, n = u % 2, 3 * i + u // 2
                        act.wait_ge(tr3, 6 * i + u + 1)
                        if n:
                            act.wait_ge(lm3[q], n)
                        nc.scalar.activation(xTf[q][:], bank[CB[u]][:, :CH], ACT.Copy)
                        nc.scalar.activation(xTH[:, slice(CH * (6 * i + u), CH * (6 * i + u + 1))], bank[CB[u]][:, :CH],
                                             ACT.Copy).then_inc(xt3, 1)
                act.wait_ge(sl3, 1)
                nc.scalar.activation(ex8[0], d8[0], ACT.Exp).then_inc(ex3, 1)
                nc.scalar.activation(sel[:], konst[:40, K_SEL:K_SEL + E2 * H2], ACT.Copy)

            @block.tensor
            def _(pe):
                def logits(i, u):
                    q = u % 2
                    pe.wait_ge(xt3, 6 * i + u + 1)
                    if u % 3 == 0 and i:
                        pe.wait_ge(lg3[u // 3], i)
                    for t in range(3):
                        k = 3 * (u % 3) + t
                        last = nc.tensor.matmul(bank[2 + u // 3][:, k * E2:(k + 1) * E2], xTf[q][:, t * P:(t + 1) * P],
                                                rt2[:], start=True, stop=True)
                    last.then_inc(lm3[q], 1)

                for i in range(TRIPS3):
                    for u in range(6):
                        pe.wait_ge(xn3[u // 3], 3 * i + u % 3 + 1)
                        if i:
                            pe.wait_ge(xl3, u + 1)
                        for t in range(3):
                            last = nc.tensor.transpose(bank[CB[u]][:, t * P:(t + 1) * P],
                                                       xn[u // 3][:, 3 * (u % 3) + t, :], ident)
                        last.then_inc(tr3, 1)
                        if u:
                            logits(i, u - 1)
                    logits(i, 5)

        with nc.Block() as block:
            @block.vector
            def _(dve):
                d = Steps(dve, dve3b)
                d.n = TOP2_STEPS

                choose(d, 1)
                weigh(d, 1)
                for b in range(NT // TB):
                    dve.wait_ge(cH3, b + 1)
                    at = slice(b * TB * P, (b + 1) * TB * P)
                    nc.vector.tensor_tensor(cT[32:32 + E2, at], bank[b % 8][:E2, :], cT[0:E2, at].bitcast(F32),
                                            ALU.subtract).then_inc(cL3, 1)

            @block.scalar
            def _(act):
                def high_weights(first, end):
                    for b in range(first, end):
                        act.wait_ge(cps3, b + 1)
                        nc.scalar.activation(cT[0:E2, b * TB * P:(b + 1) * TB * P], bank[b % 8][:E2, :],
                                             ACT.Copy).then_inc(cH3, 1)

                act.wait_ge(cz3, 1)
                high_weights(0, EARLY)
                act.wait_ge(sl3, 2)
                nc.scalar.activation(ex8[1], d8[1], ACT.Exp).then_inc(ex3, 1)
                high_weights(EARLY, NT // TB)

            @block.tensor
            def _(pe):
                for b in range(NT // TB):
                    if b == EARLY:
                        pe.wait_ge(spl3, 2)
                    if b >= 8:
                        pe.wait_ge(cL3, b - 7)
                    for t in range(TB):
                        last = nc.tensor.transpose(bank[b % 8][:E2, t * P:(t + 1) * P], weights[:, b * TB + t, :], ident)
                    last.then_inc(cps3, 1)

        s4 = [lsb(f"s4_{q}", [P, CH]) for q in range(2)]
        t4 = [lsb(f"t4_{q}", [P, CH]) for q in range(2)]
        h4 = [lsb(f"h4_{q}", [P, CH]) for q in range(2)]
        y4 = [lsb(f"y4_{p}", [P, CH]) for p in range(2)]
        g_ps, u_ps, s_ok, h_ok, dn, yS, zt = (sems(n) for n in "g_ps u_ps s_ok h_ok dn yS zt".split())
        cb_ps, t_ok, R_ok = sem("cb_ps"), sem("t_ok"), sem("R_ok")
        zrow = lsb("zrow", [P, 12, C])
        z4, zf4 = sem("z4"), sem("zf4")
        ZFILLS = SLOTS // (SR * 12) + NT // 12
        TRIPS = N // CH // 2
        UB = 2 * NB2
        UPT = 2 * (NB2 - 1)
        UPS = NB2 - 1

        def use(i, u):
            return u % 2, NB2 * i + u // 2

        def rows(k):
            return P if k < NB2 - 1 else H2

        with nc.Block() as block:
            @block.gpsimd
            def _(pool):
                nc.gpsimd.memset(zrow[:], 0.0).then_inc(z4, 1)
                z = Steps(pool, k0)
                firsts = [(K[q][:], 0.0) for q in range(3)] + [(Q[q][64:97, :], 0.0) for q in range(3)]
                firsts += [(Q[q][r:r + 1, :], -1.0) for q in range(3) for r in (64, 96)]
                firsts += [(V[p][:, :, C:C + 1], 1.0) for p in range(2)] + [(carry[:], 0.0)]
                for ap, value in firsts:
                    z.did(nc.gpsimd.memset(ap.bitcast(F32), value))
                    z.wait()
                for g in range(BEFORE):
                    pool.wait_ge(var5, g + 1)
                    norm_rstd(GT, g, P, rs5)

            @block.sync
            def _(sp):
                sp.wait_ge(z4, 1)
                for k in range(SLOTS // (SR * 12)):
                    sp.dma_start(slots[k * SR * 12:(k + 1) * SR * 12, :].rearrange("(p t) c -> p t c", t=12),
                                 zrow[:SR]).then_inc(zf4, 16)
                for k in range(NT // 12):
                    first = SLOTS + k * P * 12
                    sp.dma_start(slots[first:first + P * 12, :].rearrange("(p t) c -> p t c", t=12),
                                 zrow[:]).then_inc(zf4, 16)
                sp.wait_ge(zf4, 16 * ZFILLS)

            @block.tensor
            def _(pe):
                def tokens(i, u):
                    return bass.ds(CH * (2 * i + u // NB2), CH)

                def product3(o, w, at, emptied=None):
                    nc.tensor.matmul(o, gu_w[0][:, w], xTH[:, at], start=True, stop=False)
                    nc.tensor.matmul(o, gu_w[0][:, w], xTL[:, at], start=False, stop=False)
                    if emptied is not None:
                        pe.wait_ge(t_ok, emptied)
                    return nc.tensor.matmul(o, gu_w[1][:, w], xTH[:, at], start=False, stop=True)

                def feed(i, u):
                    q, n = use(i, u)
                    k = u % NB2
                    pe.wait_ge(s_ok[q], n)
                    if any(v % NB2 == NB2 - 1 for v in (u - 2, u + UB - 2)):
                        pe.wait_ge(h_ok[q], n)
                    emptied = UPT * i + (NB2 - 1) * (u // NB2) + k if k < NB2 - 1 else None
                    product3(bank[q][:, :CH], slice(2 * k * P, (2 * k + 1) * P), tokens(i, u), emptied
                             ).then_inc(g_ps[q], 1)
                    if k < NB2 - 1:
                        nc.tensor.matmul(bank[4][:, :CH], sel[:, k * P:(k + 1) * P], cT[:, tokens(i, u)],
                                         start=True, stop=True).then_inc(cb_ps, 1)
                        pe.wait_ge(h_ok[q], n)
                        product3(bank[2 + q][:, :CH], slice((2 * k + 1) * P, (2 * k + 2) * P),
                                 tokens(i, u)).then_inc(u_ps[q], 1)

                def down(i, u):
                    q, n = use(i, u)
                    k, p = u % NB2, u // NB2
                    if k == 0:
                        pe.wait_ge(yS[p], i)
                    pe.wait_ge(h_ok[q], n + 1)
                    nc.tensor.matmul(bank[5 + p][:, :CH], wd[:rows(k), k, :], h4[q][:rows(k), :],
                                     start=k == 0, stop=k == NB2 - 1).then_inc(dn[q], 1)

                def back(i, p):
                    pe.wait_ge(yS[p], i + 1)
                    if p == 0:
                        pe.wait_ge(R_ok, 2 * i)
                    else:
                        pe.wait_ge(R_ok, 2 * i + 1)
                    for t in range(3):
                        last = nc.tensor.transpose(bank[7][:, t * P:(t + 1) * P], y4[p][:, t * P:(t + 1) * P], ident)
                    last.then_inc(zt[p], 1)

                def trip(i, first, final):
                    for u in range(UB):
                        if u + 1 < UB:
                            feed(i, u + 1)
                        elif not final:
                            feed(i + 1, 0)
                        down(i, u)
                        if u == 1 and not first:
                            back(i - 1, 1)
                        if u == NB2 + 1:
                            back(i, 0)

                feed(0, 0)
                trip(0, True, False)
                with pe.Fori(1, TRIPS - 1) as i:
                    trip(i, False, False)
                trip(TRIPS - 1, False, True)
                back(TRIPS - 1, 1)

            @block.scalar
            def _(act):
                def silu(i, u):
                    q, n = use(i, u)
                    r = rows(u % NB2)
                    act.wait_ge(g_ps[q], n + 1)
                    act.wait_ge(h_ok[q], n)
                    nc.scalar.activation(s4[q][:r], bank[q][:r, :CH], ACT.Silu).then_inc(s_ok[q], 1)

                def trip(i, final):
                    for u in range(UB):
                        if u + 1 < UB:
                            silu(i, u + 1)
                        elif not final:
                            silu(i + 1, 0)
                        if u % NB2 == NB2 - 1:
                            p = u // NB2
                            q, n = use(i, u)
                            act.wait_ge(dn[q], n + 1)
                            act.wait_ge(zt[p], i)
                            nc.scalar.activation(y4[p][:], bank[5 + p][:, :CH], ACT.Copy).then_inc(yS[p], 1)

                silu(0, 0)
                trip(0, False)
                with act.Fori(1, TRIPS - 1) as i:
                    trip(i, False)
                trip(TRIPS - 1, True)

            @block.vector
            def _(dve):
                d = Steps(dve, t_ok)

                def residual(i, p):
                    dve.wait_ge(zt[p], i + 1)
                    at = bass.ds(6 * i + 3 * p, 3)
                    nc.vector.tensor_tensor(R[:, at, :], R[:, at, :], bank[7][:, :CH].rearrange("p (t c) -> p t c", c=C),
                                            ALU.add).then_inc(R_ok, 1)

                def trip(i, first, final):
                    for u in range(UB):
                        q, n = use(i, u)
                        k = u % NB2
                        r = rows(k)
                        dve.wait_ge(s_ok[q], n + 1)
                        if k < NB2 - 1:
                            dve.wait_ge(cb_ps, UPT * i + (NB2 - 1) * (u // NB2) + k + 1)
                            d.did(nc.vector.tensor_tensor(t4[q][:], bank[4][:, :CH], s4[q][:], ALU.mult))
                            d.wait()
                            dve.wait_ge(u_ps[q], UPS * i + sum(v % 2 == q and v % NB2 < NB2 - 1 for v in range(u + 1)))
                            dve.wait_ge(dn[q], n)
                            nc.vector.tensor_tensor(h4[q][:], bank[2 + q][:, :CH], t4[q][:],
                                                    ALU.mult).then_inc(h_ok[q], 1)
                        else:
                            dve.wait_ge(dn[q], n)
                            nc.vector.tensor_tensor(h4[q][:r], bank[q][r:2 * r, :CH], s4[q][:r],
                                                    ALU.mult).then_inc(h_ok[q], 1)
                        if u == 2 and not first:
                            residual(i - 1, 1)
                        if u == NB2 + 2:
                            residual(i, 0)
                        if final:
                            ahead(u)

                def ahead(u):
                    if u < 6:
                        g = u // 3
                        for t in range(3 * (u % 3), 3 * (u % 3) + 3):
                            ins = nc.vector.bn_stats(st[g][:, t, :], R[:, GT * g + t, :])
                        if u % 3 == 2:
                            norm_moments(f, ins, GT, g, P, EPS_C, var5)
                    elif u < 9:
                        if u == 6:
                            dve.wait_ge(rs5, 1)
                        for t in range(3 * (u - 6), 3 * (u - 6) + 3):
                            ins = nc.vector.tensor_scalar(xn[0][:, t, :], R[:, t, :], sm[0][:, 4, t:t + 1],
                                                          rstd[0][:, t:t + 1], ALU.subtract, ALU.mult)
                        if u == 8:
                            ins.then_inc(xn5, 1)

                f = Steps(dve, dve5)
                trip(0, True, False)
                with dve.Fori(1, TRIPS - 1) as i:
                    d.enter(i - 1, UPT)
                    trip(i, False, False)
                d.leave(TRIPS - 2)
                trip(TRIPS - 1, False, True)
                residual(TRIPS - 1, 1)
        local.close()

        GN = GT * P
        JB = [(k * P, min(P, SS - k * P)) for k in range(NB_SS)]
        PT = [wide0[:, p * NB_SS * SS:(p + 1) * NB_SS * SS].rearrange("j (k i) -> j k i", k=NB_SS) for p in range(2)]
        hT, lT = wide1, wide2
        SPLIT = 3
        LAST = B + 5
        gidx = sb("gidx", [P, NT], I32)
        prob = sb("prob", [P, NT])
        local = ExitStack()
        ctx.callback(local.close)
        sH = [lsb(f"sH{p}", [P, SS], F32R) for p in range(2)]
        sQK = [lsb(f"sQK{p}", [P, SS], F32R) for p in range(2)]
        mx = [lsb(f"mx{p}", [P, NB_SS]) for p in range(2)]
        rs = [lsb(f"rs{p}", [P, NB_SS]) for p in range(2)]
        nmr = [lsb(f"nmr{p}", [P, GT]) for p in range(2)]
        tri = lsb("tri", [P, P], BF16)
        ones = lsb("ones", [P, P], BF16)
        oh = [lsb(f"oh{p}", [P, GT, E1], BF16) for p in range(2)]
        lg = [lsb(f"lg{p}", [P, GT, E1]) for p in range(2)]
        lx = [lsb(f"lx{p}", [P, GT, E1]) for p in range(2)]
        w1 = [lsb(f"w1_{p}", [P, GT, E1]) for p in range(2)]
        cm = [lsb(f"cm{p}", [P, 8, GT]) for p in range(2)]
        sidx = [lsb(f"sidx{p}", [P, GT], I32) for p in range(2)]
        var6, rs6, xn6, t_ps, t_hi, t_lo, qk_ps, sh_ok, st_ok, qk_in = (
            late_sem(n) for n in "var6 rs6 xn6 t_ps t_hi t_lo qk_ps sh_ok st_ok qk_in".split())
        qk_in = [qk_in, late_sem("qk_in1")]
        v_ps, v_ok, e_ps, mx_ok, mT, mH, mL, et_ps, pt_ok, pv, o_ok, k6 = (
            late_sem(n) for n in "v_ps v_ok e_ps mx_ok mT mH mL et_ps pt_ok pv o_ok k6".split())
        l_tr, l_xt, l_ps, lg_ok, d6, ex6, oh6, cnt6, cr6, sx6, rr5, r6 = (
            late_sem(n) for n in "l_tr l_xt l_ps lg_ok d6 ex6 oh6 cnt6 cr6 sx6 rr5 r6".split())
        sc6 = late_sems("sc6")
        early.close()

        def halves(ap, rows=P):
            return ap[:rows].rearrange("r (h n) -> r h n", h=2)[:, :, :HALF]

        def i_blocks(n):
            g, odd = n // 2, n % 2
            if not odd:
                return [(k * P, m, GT * g + k, 0) for k, (_, m) in enumerate(JB)]
            return [(0, P // 2, GT * g + NB_SS - 1, P // 2)] + [
                (P // 2 + k * P, P, GT * g + NB_SS + k, 0) for k in range(NB_SS - 1)]

        def tiles(g):
            return slice(GT * g, GT * (g + 1))

        def ahead(n):
            g, chunks = ((n + 3) // 2, (0, 1)) if n % 2 else ((n + 2) // 2, (2,))
            return (g, chunks) if 0 <= g < NG else (None, ())

        def behind(n, lag):
            g = (n - lag) // 2
            return g if (n - lag) % 2 == 0 and 0 <= g < NG else None

        def xn_buffer(g):
            return xn[g % 2] if g < NG - 1 else wide0[:, :GT * C].rearrange("p (t c) -> p t c", c=C)

        def l_bank(g, c):
            return bank[0] if c == 2 and 2 * g + 5 > B else bank[4 + c % 2]

        def e_pair(n, k):
            return 1 if n else 1 - k % 2

        def per_expert(c):
            return c.unsqueeze(2).to_broadcast([P, GT, E1])

        with nc.Block() as block:
            @block.gpsimd
            def _(pool):
                for g in range(BEFORE, NG):
                    p = g % 2
                    pool.wait_ge(var5, g + 1)
                    pool.wait_ge(xn5, g - 1)
                    norm_rstd(GT, p, P, rs5)
                    pool.wait_ge(rs5, g + 1)
                    pool.wait_ge(t_ps, 3 * (g - 1))
                    for t in range(GT):
                        ins = nc.gpsimd.tensor_scalar(xn[p][:, t, :], R[:, GT * g + t, :], sm[p][:, 4, t:t + 1],
                                                      rstd[p][:, t:t + 1], ALU.subtract, ALU.mult)
                    ins.then_inc(xn5, 1)

                def scatter(g, ts):
                    if ts[0] == 0:
                        pool.wait_ge(sx6, g + 1)
                    for t in ts:
                        nc.gpsimd.indirect_dma_start(
                            slots, bass.IndirectOffsetOnAxis(sidx[g % 2][:, t:t + 1], 0),
                            xn_buffer(g)[:, t, :], None).then_inc(sc6[g % 2], 16)

                def rstd6(g):
                    p = g % 2
                    pool.wait_ge(var6, g + 1)
                    if g >= 2:
                        pool.wait_ge(xn6, 3 * (g - 1))
                    norm_rstd(GT, p, P, rs6)
                    pool.wait_ge(rs6, 2 * g + 1)
                    nc.gpsimd.tensor_tensor(nmr[p][:], sm[p][:, 4, :], rstd[p][:], ALU.mult).then_inc(rs6, 1)

                rstd6(0)
                rstd6(1)
                scatter(0, range(GT))
                rstd6(2)
                scatter(1, range(0, SPLIT))
                rstd6(3)
                scatter(1, range(SPLIT, GT))
                scatter(2, range(GT))
                scatter(3, range(GT))
                for p in range(2):
                    pool.wait_ge(sc6[p], 16 * GT * 2)

            @block.sync
            def _(sp):
                for done in early_sems:
                    sp.sem_clear(done)
                for n in range(B):
                    q = n % 3
                    sp.wait_ge(st_ok, n + 1)
                    if n >= 3:
                        sp.wait_ge(et_ps, NB_SS * (n - 2))
                    sp.dma_start(Q[q][0:64, :].bitcast(F32), sQK[n % 2][0:64, :].bitcast(F32)).then_inc(qk_in[n % 2], 16)
                    sp.dma_start(K[q][0:64, :SS].bitcast(F32), sQK[n % 2][64:128, :].bitcast(F32)).then_inc(
                        qk_in[n % 2], 16)

            @block.vector
            def _(dve):
                d = Steps(dve, dve5)
                o_step = Steps(dve, rr5)
                r = Steps(dve, r6)

                def apply5(g):
                    p = g % 2
                    dve.wait_ge(rs5, g + 1)
                    norm_apply(R[:, tiles(g), :], GT, p, P, xn5)

                def maximum(n, k):
                    m = JB[k][1]
                    dve.wait_ge(e_ps, NB_SS * n + k + 1)
                    if k == 0 and n >= 2:
                        dve.wait_ge(mT, n - 1)
                    nc.vector.tensor_reduce(mx[n % 2][:m, k:k + 1], halves(psum[e_pair(n, k)], m), AX.XY,
                                            ALU.max).then_inc(mx_ok, 1)

                def stack(n):
                    dve.wait_ge(sh_ok, n + 1)
                    if n >= 2:
                        dve.wait_ge(qk_in[n % 2], 32 * (n // 2))
                    nc.vector.scalar_tensor_tensor(
                        sQK[n % 2][:].rearrange("r (h n) -> r h n", h=2), halves(psum[2]), konst[:, K_SGN + 1:K_SGN + 2],
                        sH[n % 2][:].bitcast(F32).rearrange("r (h n) -> r h n", h=2),
                        ALU.mult, ALU.subtract).then_inc(st_ok, 1)

                def low_row(n):
                    dve.wait_ge(mH, n + 1)
                    nc.vector.tensor_tensor(K[n % 3][96:97, :SS], psum[1][0:1, :SS], K[n % 3][64:65, :SS].bitcast(F32),
                                            ALU.subtract).then_inc(mL, 1)

                def attended(n, ks):
                    blocks = i_blocks(n)
                    dve.wait_ge(pv, NB_SS * n + ks[-1] + 1)
                    for k in ks:
                        _, m, _, lo = blocks[k]
                        at = k % 3 * (C + 1) + C
                        o_step.did(nc.vector.reciprocal(rs[n % 2][lo:lo + m, k:k + 1],
                                                        bank[6 + k // 3][lo:lo + m, at:at + 1]))
                    o_step.wait()
                    for k in ks:
                        _, m, tile, lo = blocks[k]
                        o = bank[6 + k // 3][lo:lo + m, k % 3 * (C + 1):k % 3 * (C + 1) + C]
                        at = R[lo:lo + m, tile, :]
                        nc.vector.scalar_tensor_tensor(at, o, rs[n % 2][lo:lo + m, k:k + 1], at,
                                                       ALU.mult, ALU.add).then_inc(o_ok, 1)

                def low_halves(n):
                    g, chunks = ahead(n)
                    for c in chunks:
                        dve.wait_ge(t_hi, 3 * g + c + 1)
                        at = slice(g * GN + c * CH, g * GN + (c + 1) * CH)
                        nc.vector.tensor_tensor(lT[:, at], bank[4 + c % 2][:, :CH], hT[:, at].bitcast(F32),
                                                ALU.subtract).then_inc(t_lo, 1)

                def add_bias(g, c):
                    dve.wait_ge(l_ps, 3 * g + c + 1)
                    nc.vector.tensor_tensor(lg[g % 2][:, 3 * c:3 * c + 3, :],
                                            l_bank(g, c)[:, CH:CH + 3 * E1].rearrange("p (t e) -> p t e", e=E1),
                                            rb1[:].unsqueeze(1).to_broadcast([P, 3, E1]), ALU.add).then_inc(lg_ok, 1)

                def route_max(g):
                    p = g % 2
                    c = cm[p]
                    dve.wait_ge(lg_ok, 3 * g + 3)
                    r.did(nc.vector.tensor_reduce(c[:, 0], lg[p][:], AX.X, ALU.max))
                    r.wait()
                    nc.vector.tensor_tensor(lx[p][:], lg[p][:], per_expert(c[:, 0]), ALU.subtract).then_inc(d6, 1)
                    r.did(nc.vector.tensor_tensor(w1[p][:], lg[p][:], per_expert(c[:, 0]), ALU.is_equal))

                def route_first(g):
                    p = g % 2
                    c = cm[p]
                    r.wait()
                    r.did(nc.vector.tensor_tensor(w1[p][:], w1[p][:],
                                                  konst[:, K_PRI + 16:K_PRI + 32].unsqueeze(1).to_broadcast([P, GT, E1]),
                                                  ALU.mult))
                    r.wait()
                    r.did(nc.vector.tensor_reduce(c[:, 1], w1[p][:], AX.X, ALU.max))
                    r.wait()
                    nc.vector.tensor_tensor(oh[p][:], w1[p][:], per_expert(c[:, 1]), ALU.is_equal).then_inc(oh6, 1)

                def route_slot(g):
                    p = g % 2
                    c = cm[p]
                    dve.wait_ge(oh6, g + 1)
                    r.did(nc.vector.tensor_tensor(w1[p][:], oh[p][:],
                                                  konst[:, K_EB:K_EB + E1].unsqueeze(1).to_broadcast([P, GT, E1]),
                                                  ALU.mult))
                    r.wait()
                    r.did(nc.vector.tensor_reduce(c[:, 2], w1[p][:], AX.X, ALU.add))

                def place_counts(g):
                    p = g % 2
                    dve.wait_ge(cnt6, g + 1)
                    if g:
                        dve.wait_ge(cr6, g)
                    r.did(nc.vector.tensor_tensor(lg[p][:], bank[4][:, :GT * E1].rearrange("p (t e) -> p t e", e=E1),
                                                  carry[:, p].unsqueeze(1).to_broadcast([P, GT, E1]), ALU.add))
                    nc.vector.tensor_tensor(carry[:, 1 - p], bank[4][:, GT * E1:(GT + 1) * E1], carry[:, p],
                                            ALU.add).then_inc(cr6, 1)

                def place_sums(g):
                    p = g % 2
                    c = cm[p]
                    r.wait()
                    r.did(nc.vector.tensor_tensor(w1[p][:], lg[p][:], oh[p][:], ALU.mult))
                    dve.wait_ge(ex6, g + 1)
                    r.did(nc.vector.tensor_reduce(c[:, 3], lx[p][:], AX.X, ALU.add))
                    r.wait()
                    r.did(nc.vector.tensor_reduce(c[:, 4], w1[p][:], AX.X, ALU.add))
                    r.did(nc.vector.reciprocal(prob[:, tiles(g)], c[:, 3]))

                def place_index(g):
                    p = g % 2
                    c = cm[p]
                    r.wait()
                    r.did(nc.vector.tensor_scalar(c[:, 5], c[:, 4], float(CAP), None, ALU.is_le))
                    r.did(nc.vector.scalar_tensor_tensor(c[:, 6], c[:, 4], -1.0, c[:, 2], ALU.add, ALU.add))
                    r.wait()
                    trash = konst[:, K_N:K_N + NT][:, tiles(g)]
                    r.did(nc.vector.tensor_tensor(c[:, 6], c[:, 6], trash, ALU.subtract))
                    r.wait()
                    r.did(nc.vector.tensor_tensor(c[:, 6], c[:, 6], c[:, 5], ALU.mult))
                    r.wait()
                    r.did(nc.vector.tensor_tensor(c[:, 6], c[:, 6], trash, ALU.add))
                    r.wait()
                    if g >= 2:
                        dve.wait_ge(sc6[p], 16 * GT * (g // 2))
                    nc.vector.tensor_copy(sidx[p][:], c[:, 6]).then_inc(sx6, 1)
                    r.did(nc.vector.scalar_tensor_tensor(gidx[:, tiles(g)], c[:, 5], float(SLOTS + N), c[:, 6],
                                                         ALU.mult, ALU.add))

                d.base = BEFORE * NORM_STEPS
                nc.vector.tensor_copy(tri[:], konst[:, K_TRI:K_TRI + P]).then_inc(k6, 1)
                nc.vector.tensor_copy(ones[:], konst[:, K_ONE:K_ONE + P]).then_inc(k6, 1)
                low_halves(-3)
                for n in range(-2, LAST):
                    stats = n + 2 if n in (0, 1) else behind(n, 3)
                    for k in range(NB_SS):
                        if 0 <= n + 1 < B:
                            maximum(n + 1, k)
                        if k == 0 and n + 2 < B:
                            stack(n + 2)
                        if stats is not None and k < 3:
                            if k == 0 and n not in (0, 1):
                                dve.wait_ge(o_ok, NB_SS * 2 * (stats + 1))
                            if k == 0 and n in (0, 1):
                                dve.wait_ge(xn5, stats - 1)
                            elif k == 0 and stats >= 2:
                                dve.wait_ge(xn6, 3 * (stats - 1))
                            elif k == 0:
                                dve.wait_ge(xn5, stats + 3)
                            for t in range(3 * k, 3 * k + 3):
                                ins = nc.vector.bn_stats(st[stats % 2][:, t, :], R[:, GT * stats + t, :])
                        if k == 2 and behind(n, 5) is not None:
                            add_bias(behind(n, 5), 0)
                            add_bias(behind(n, 5), 1)
                        if k == 3 and 0 <= n - 1 < B:
                            attended(n - 1, (0, 1, 2))
                        if k < 3 and behind(n, 6) is not None:
                            (route_max, route_first, route_slot)[k](behind(n, 6))
                        if k == 4 and behind(n, 6) is not None:
                            place_counts(behind(n, 6))
                    if stats is not None:
                        norm_moments(d, ins, GT, stats % 2, P, EPS_C if n in (0, 1) else EPS_T,
                                     var5 if n in (0, 1) else var6, mean=0.5 if n in (0, 1) else -0.5)
                    if n == -2:
                        low_halves(n)
                        apply5(1)
                    if 0 <= n + 1 < B:
                        low_row(n + 1)
                    if behind(n, 6) is not None:
                        place_sums(behind(n, 6))
                        place_index(behind(n, 6))
                    if behind(n, 5) is not None:
                        add_bias(behind(n, 5), 2)
                    if n > -2:
                        low_halves(n)
                    if 0 <= n - 1 < B:
                        attended(n - 1, (3, 4))

            @block.scalar
            def _(act):
                def high_halves(n):
                    g, chunks = ahead(n)
                    for c in chunks:
                        act.wait_ge(t_ps, 3 * g + c + 1)
                        nc.scalar.activation(hT[:, g * GN + c * CH:g * GN + (c + 1) * CH], bank[4 + c % 2][:, :CH],
                                             ACT.Copy).then_inc(t_hi, 1)

                def router_copy(g, c):
                    act.wait_ge(l_tr, 3 * g + c + 1)
                    if 3 * g + c >= 2:
                        act.wait_ge(l_ps, 3 * g + c - 1)
                    nc.scalar.activation(xTf[(3 * g + c) % 2][:], l_bank(g, c)[:, :CH], ACT.Copy).then_inc(l_xt, 1)

                for n in range(-3, LAST):
                    g = behind(n, 4)
                    for k in range(NB_SS):
                        if 0 <= n < B:
                            m = JB[k][1]
                            act.wait_ge(et_ps, NB_SS * n + k + 1)
                            if k == 0 and n >= 2:
                                act.wait_ge(pv, NB_SS * (n - 1))
                            nc.scalar.activation(PT[n % 2][:m, k, :].rearrange("j (h n) -> j h n", h=2),
                                                 halves(psum[0], m), ACT.Exp).then_inc(pt_ok, 1)
                        if k == 0 and 0 <= n + 2 < B:
                            act.wait_ge(qk_ps, n + 3)
                            if n >= 0:
                                act.wait_ge(st_ok, n + 1)
                            nc.scalar.activation(sH[n % 2][:].rearrange("r (h n) -> r h n", h=2), halves(psum[2]),
                                                 ACT.Copy, scale=konst[:, K_SGN:K_SGN + 1]).then_inc(sh_ok, 1)
                        if k == 1 and behind(n, 5) is not None:
                            router_copy(behind(n, 5), 0)
                            router_copy(behind(n, 5), 1)
                        if k == 1 and behind(n, 6) is not None:
                            p = behind(n, 6) % 2
                            act.wait_ge(d6, behind(n, 6) + 1)
                            nc.scalar.activation(lx[p][:], lx[p][:], ACT.Exp).then_inc(ex6, 1)
                        if g is not None and k < 3:
                            if k == 0:
                                act.wait_ge(rs6, 2 * g + 2)
                                if g == NG - 1:
                                    act.wait_ge(pv, NB_SS * (B - 1))
                                elif g >= 2:
                                    act.wait_ge(sc6[g % 2], 16 * GT * (g // 2))
                                else:
                                    act.wait_ge(t_ps, 3 * (g + 3))
                            for t in range(3 * k, 3 * k + 3):
                                ins = nc.scalar.activation(xn_buffer(g)[:, t, :], R[:, GT * g + t, :], ACT.Identity,
                                                           bias=nmr[g % 2][:, t:t + 1], scale=rstd[g % 2][:, t:t + 1])
                            ins.then_inc(xn6, 1)
                        if k == 3 and 0 <= n < B:
                            act.wait_ge(v_ps, n + 1)
                            if n >= 2:
                                act.wait_ge(pv, NB_SS * (n - 1))
                            for kk, (_, m) in enumerate(JB):
                                at = kk // 4 * 512 + kk % 4 * C
                                ins = nc.scalar.activation(V[n % 2][:m, kk, :C], psum[2][:m, at:at + C], ACT.Copy,
                                                           scale=gam[:m])
                            ins.then_inc(v_ok, 1)
                    if 0 <= n + 1 < B:
                        act.wait_ge(mT, n + 2)
                        nc.scalar.activation(K[(n + 1) % 3][64:65, :SS], psum[1][0:1, :SS], ACT.Copy).then_inc(mH, 1)
                    if behind(n, 5) is not None:
                        router_copy(behind(n, 5), 2)
                    high_halves(n)

            @block.tensor
            def _(pe):
                issued = dict(T=0, QK=0, V=0, L=0, C=0)

                def banks_empty():
                    for kind, read in (("T", t_lo), ("QK", st_ok), ("V", v_ok), ("L", lg_ok), ("C", cr6)):
                        if issued[kind]:
                            pe.wait_ge(read, issued[kind])

                def transposes(n):
                    g, chunks = ahead(n)
                    if chunks:
                        pe.wait_ge(xn5, g + 1)
                        banks_empty()
                    for c in chunks:
                        for t in range(3):
                            last = nc.tensor.transpose(bank[4 + c % 2][:, t * P:(t + 1) * P], xn[g % 2][:, 3 * c + t, :],
                                                       ident)
                        last.then_inc(t_ps, 1)
                        issued["T"] += 1

                def project_qk(n):
                    banks_empty()
                    w = slice(W_QK, W_QK + C)
                    for h in range(2):
                        o = psum[2][:, h * 512:h * 512 + HALF]
                        at = slice(n * SS + h * HALF, n * SS + (h + 1) * HALF)
                        nc.tensor.matmul(o, gu_w[0][:, w], hT[:, at], start=True, stop=False)
                        nc.tensor.matmul(o, gu_w[0][:, w], lT[:, at], start=False, stop=False)
                        last = nc.tensor.matmul(o, gu_w[1][:, w], hT[:, at], start=False, stop=True)
                    last.then_inc(qk_ps, 1)
                    issued["QK"] += 1

                def project_v(n):
                    banks_empty()
                    w = slice(W_V, W_V + C)
                    for k, (j0, m) in enumerate(JB):
                        o = psum[2][:m, k // 4 * 512 + k % 4 * C:k // 4 * 512 + k % 4 * C + C]
                        at = slice(n * SS + j0, n * SS + j0 + m)
                        nc.tensor.matmul(o, hT[:, at], gu_w[0][:, w], start=True, stop=False)
                        nc.tensor.matmul(o, lT[:, at], gu_w[0][:, w], start=False, stop=False)
                        last = nc.tensor.matmul(o, hT[:, at], gu_w[1][:, w], start=False, stop=True)
                    last.then_inc(v_ps, 1)
                    issued["V"] += 1

                def energies(n, k):
                    if k and n:
                        pe.wait_ge(mx_ok, NB_SS * n + k)
                    elif k >= 2:
                        pe.wait_ge(mx_ok, k - 1)
                    elif k == 0:
                        pe.wait_ge(qk_in[n % 2], 32 * (n // 2 + 1))
                        if n:
                            pe.wait_ge(mL, n)
                    i0 = JB[k][0]
                    for h in range(2):
                        last = nc.tensor.matmul(psum[e_pair(n, k)][:, h * 512:h * 512 + HALF], K[n % 3][:64, i0:i0 + P],
                                                Q[n % 3][:64, h * HALF:(h + 1) * HALF], start=True, stop=True)
                    last.then_inc(e_ps, 1)

                def energies_T(n, k):
                    j0, m = JB[k]
                    if k == 0:
                        pe.wait_ge(mL, n + 1)
                    if n or k:
                        pe.wait_ge(pt_ok, NB_SS * n + k)
                    for h in range(2):
                        last = nc.tensor.matmul(psum[0][:m, h * 512:h * 512 + HALF], Q[n % 3][:, j0:j0 + m],
                                                K[n % 3][:, h * HALF:(h + 1) * HALF], start=True, stop=True)
                    last.then_inc(et_ps, 1)

                def maxima_row(n):
                    pe.wait_ge(mx_ok, NB_SS * (n + 1))
                    for k, (i0, m) in enumerate(JB):
                        last = nc.tensor.transpose(psum[1][0:1, i0:i0 + m], mx[n % 2][:m, k:k + 1], ident[:m, :m])
                    last.then_inc(mT, 1)

                def attend(n, k):
                    i0, m, _, lo = i_blocks(n)[k]
                    if k == 0:
                        pe.wait_ge(pt_ok, NB_SS * (n + 1))
                        pe.wait_ge(v_ok, n + 1)
                    if k in (0, 3) and n:
                        pe.wait_ge(o_ok, NB_SS * (n - 1) + (3 if k == 0 else NB_SS))
                    for jk, (_, mj) in enumerate(JB):
                        last = nc.tensor.matmul(bank[6 + k // 3][lo:lo + m, k % 3 * (C + 1):(k % 3 + 1) * (C + 1)],
                                                PT[n % 2][:mj, jk, i0:i0 + m], V[n % 2][:mj, jk, :],
                                                start=jk == 0, stop=jk == NB_SS - 1)
                    last.then_inc(pv, 1)

                def router_transposes(g, c):
                    pe.wait_ge(xn6, 3 * g + c + 1)
                    if c == 0:
                        banks_empty()
                    elif c == 2 and l_bank(g, c) is not bank[0]:
                        banks_empty()
                    elif c == 2 and 2 * g + 5 > B + 2:
                        pe.wait_ge(lg_ok, 3 * g)
                    for t in range(3):
                        last = nc.tensor.transpose(l_bank(g, c)[:, t * P:(t + 1) * P],
                                                   xn_buffer(g)[:, 3 * c + t, :], ident)
                    last.then_inc(l_tr, 1)
                    issued["L"] += 1

                def logits(g, c):
                    pe.wait_ge(l_xt, 3 * g + c + 1)
                    for t in range(3):
                        last = nc.tensor.matmul(l_bank(g, c)[:, CH + t * E1:CH + (t + 1) * E1],
                                                xTf[(3 * g + c) % 2][:, t * P:(t + 1) * P], rt1[:], start=True, stop=True)
                    last.then_inc(l_ps, 1)

                def counts(g):
                    banks_empty()
                    pe.wait_ge(k6, 2)
                    pe.wait_ge(oh6, g + 1)
                    o = bank[4]
                    nc.tensor.matmul(o[:, :GT * E1], tri[:], oh[g % 2][:].rearrange("p t e -> p (t e)"),
                                     start=True, stop=False, skip_group_check=True)
                    for t in range(GT):
                        later = GT - t
                        last = nc.tensor.matmul(
                            o[:, (t + 1) * E1:(GT + 1) * E1].rearrange("p (k e) -> p k e", e=E1), ones[:],
                            oh[g % 2][:, t:t + 1, :].to_broadcast([P, later, E1]),
                            start=False, stop=t == GT - 1, skip_group_check=True)
                    last.then_inc(cnt6, 1)
                    issued["C"] += 1

                transposes(-3)
                for n in range(-2, LAST):
                    g = behind(n, 5)
                    for k in range(NB_SS):
                        if 0 <= n - 1 < B and k < NB_SS - 1:
                            attend(n - 1, k)
                        if 0 <= n + 1 < B:
                            energies(n + 1, k)
                        if 0 <= n < B:
                            energies_T(n, k)
                        if k == 0 and n + 2 < B:
                            project_qk(n + 2)
                        if k == 1 and g is not None:
                            router_transposes(g, 0)
                            router_transposes(g, 1)
                        if k == 2 and g is not None:
                            logits(g, 0)
                            logits(g, 1)
                        if k == 3 and 0 <= n < B:
                            project_v(n)
                        if k == (4 if n < B else 1) and g is not None:
                            router_transposes(g, 2)
                        if k == 4 and behind(n, 6) is not None:
                            counts(behind(n, 6))
                        if 0 <= n - 1 < B and k == NB_SS - 1:
                            attend(n - 1, k)
                    if 0 <= n + 1 < B:
                        maxima_row(n + 1)
                    if g is not None:
                        logits(g, 2)
                    transposes(n)
        local.close()

        local = ExitStack()
        ctx.callback(local.close)
        NBANK = 4
        xe = [lsb(f"xe{e}", [SR, 3, C]) for e in range(E1)]
        ye = [lsb(f"ye{e}", [SR, 3, C]) for e in range(E1)]
        xeT = [wide0[:, 2 * GT * C + q * CH:2 * GT * C + (q + 1) * CH] for q in range(NBANK)]
        in7, st7 = late_sems("in7", E1), late_sem("st7")
        tr7, xt7, ym7, ye7 = (late_sem(n) for n in "tr7 xt7 ym7 ye7".split())
        NPART = NT // 3
        ga8 = late_sems("ga8", NPART)
        r8, o8 = late_sem("r8"), late_sem("o8")
        rows_in = slots[0:SLOTS, :].rearrange("(e p t) c -> e p t c", e=E1, t=3)
        rows_out = slots[SLOTS + N:, :].rearrange("(e p t) c -> e p t c", e=E1, t=3)
        out_t = out.rearrange("b h w c -> (b h w) c").rearrange("(t p) c -> p t c", p=P)
        fetched = [xn[0][:], xn[1][:]] + [wide0[:, p * GT * C:(p + 1) * GT * C].rearrange("p (t c) -> p t c", c=C)
                                          for p in range(2)]

        with nc.Block() as block:
            @block.sync
            def _(sp):
                for e in range(E1):
                    sp.dma_start(xe[e][:], rows_in[e]).then_inc(in7[e], 16)
                for part in range(NPART):
                    at = slice(3 * part, 3 * part + 3)
                    sp.wait_ge(r8, part + 1)
                    sp.dma_start(out_t[:, at, :], R[:, at, :]).then_inc(o8, 16)
                sp.wait_ge(o8, 16 * NPART)

            @block.tensor
            def _(pe):
                def product(e):
                    q = e % NBANK
                    pe.wait_ge(xt7, e + 1)
                    if e >= NBANK:
                        pe.wait_ge(ye7, e - NBANK + 1)
                    for t in range(3):
                        last = nc.tensor.matmul(bank[NBANK + q][:SR, t * C:(t + 1) * C],
                                                xeT[q][:, t * SR:(t + 1) * SR], ew[:, e, :], start=True, stop=True)
                    last.then_inc(ym7, 1)

                for e in range(E1):
                    q = e % NBANK
                    pe.wait_ge(in7[e], 16)
                    if e >= NBANK:
                        pe.wait_ge(xt7, e - NBANK + 1)
                    for t in range(3):
                        last = nc.tensor.transpose(bank[q][:, t * SR:(t + 1) * SR], xe[e][:, t, :], ident[:SR, :SR])
                    last.then_inc(tr7, 1)
                    if e >= 2:
                        product(e - 2)
                for e in range(E1 - 2, E1):
                    product(e)

            @block.scalar
            def _(act):
                def store(e):
                    act.wait_ge(ye7, e + 1)
                    act.dma_start(rows_out[e], ye[e][:]).then_inc(st7, 16)

                for e in range(E1):
                    q = e % NBANK
                    act.wait_ge(tr7, e + 1)
                    if e >= NBANK:
                        act.wait_ge(ym7, e - NBANK + 1)
                    nc.scalar.activation(xeT[q], bank[q][:, :3 * SR], ACT.Copy).then_inc(xt7, 1)
                    if e >= 4:
                        store(e - 4)
                for e in range(E1 - 4, E1):
                    store(e)

            @block.vector
            def _(dve):
                for e in range(E1):
                    dve.wait_ge(ym7, e + 1)
                    nc.vector.tensor_tensor(ye[e][:], bank[NBANK + e % NBANK][:SR, :CH].rearrange("p (t c) -> p t c", c=C),
                                            eb[:SR, e:e + 1, :].to_broadcast([SR, 3, C]), ALU.add).then_inc(ye7, 1)
                for part in range(NPART):
                    dve.wait_ge(ga8[part], 16 * 3)
                    for t in range(3 * part, 3 * part + 3):
                        ins = nc.vector.scalar_tensor_tensor(R[:, t, :], fetched[t // GT][:, t % GT, :], prob[:, t:t + 1],
                                                             R[:, t, :], ALU.mult, ALU.add)
                    ins.then_inc(r8, 1)

            @block.gpsimd
            def _(pool):
                pool.wait_ge(st7, 16 * E1)
                for t in range(NT):
                    nc.gpsimd.indirect_dma_start(
                        fetched[t // GT][:, t % GT, :], None, slots,
                        bass.IndirectOffsetOnAxis(gidx[:, t:t + 1], 0)).then_inc(ga8[t // 3], 16)


def constants():
    import numpy as np

    k = np.zeros((P, K_COLS), np.float32)
    row = np.arange(P)
    k[:, K_ID:K_ID + P] = np.eye(P)
    k[:, K_TRI:K_TRI + P] = row[:, None] <= row[None, :]
    k[:, K_ONE:K_ONE + P] = 1
    k[:G96, K_DIAG:K_DIAG + G96] = row[:G96, None] // S == row[None, :G96] // S
    for e in range(E2):
        k[e, K_SEL + e * H2:K_SEL + (e + 1) * H2] = 1
        k[32 + e, K_SEL + e * H2:K_SEL + (e + 1) * H2] = 1
    high = np.where(row < 64, row < 32, row % 32 < 16)
    k[:, K_SGN] = np.where(high, -1, 1)
    k[:, K_SGN + 1] = np.where(high, 0, 1)
    k[:, K_PRI:K_PRI + E2] = E2 - np.arange(E2)
    k[:, K_PRI + 16:K_PRI + 32] = E1 - np.arange(E1)
    k[:, K_EB:K_EB + E1] = np.arange(E1) * 3 * SR
    k[:, K_N:K_N + NT] = SLOTS + np.arange(NT)[None, :] * P + row[:, None]
    return k


def lay_out(inputs):
    import numpy as np

    g = {n: np.asarray(a) for n, a in inputs.items()}
    pairs = [np.transpose(g[f"L0_ffn_W_{n}"], (1, 0, 2)).reshape(C, E2 // 2, 2 * H2) for n in ("gate", "up")]
    experts = np.stack(pairs, 2).reshape(C, 2 * E2 * H2)
    qk = [np.tile(g["L1_conv_Wq"], (1, 4)), np.tile(g["L1_conv_Wk"], (1, 4))]
    return {
        "x": g["x"],
        "konst": constants(),
        "wkvq": np.concatenate([g[f"L0_conv_w{n}_w"].T for n in "kvq"], 1),
        "bkvq": np.tile(np.concatenate([g[f"L0_conv_w{n}_b"] for n in "kvq"]), T96)[None],
        "woT": g["L0_conv_out_w"].T,
        "ob": g["L0_conv_out_b"],
        "tabT": g["L0_conv_w_bias_table"][:S, :S].T,
        "wstage": np.concatenate([experts, g["L0_ffn_shared_gate"], g["L0_ffn_shared_up"], *qk, g["L1_conv_Wv"]], 1),
        "wd": g["L0_ffn_W_down"].reshape(E2 * H2, C),
        "wd_s": g["L0_ffn_shared_down"],
        "rt2": g["L0_ffn_router"],
        "rt1": g["L1_ffn_switch_w"].T,
        "rb1": g["L1_ffn_switch_b"],
        "gam": g["L1_conv_gamma"],
        "ew": np.transpose(g["L1_ffn_expert_w"], (2, 0, 1)),
        "eb": g["L1_ffn_expert_b"],
    }


def kernel(**inputs):
    import numpy as np
    import concourse.bacc as bacc
    from concourse.bass_utils import run_bass_kernel_spmd

    nc = bacc.Bacc("TRN2", target_bir_lowering=False, num_devices=1)
    arrays = {f"in_{n}": np.ascontiguousarray(a) for n, a in lay_out(inputs).items()}
    A = {n[3:]: nc.dram_tensor(n, a.shape, mybir.dt.from_np(a.dtype), kind="ExternalInput").ap()
         for n, a in arrays.items()}
    out = nc.dram_tensor("out", (B, S, S, C), F32, kind="ExternalOutput").ap()
    metaformer_kernel(nc, A, out)
    r = run_bass_kernel_spmd(nc, [arrays], core_ids=[0])
    return r.results[0]["out"]
```
